# Optimizing a Trainium2 kernel written in Bass

```python
import numpy as np
import jax
import jax.numpy as jnp

def _softmax(x, axis=-1):
    return jax.nn.softmax(x, axis=axis)

def _gelu(x):
    return jax.nn.gelu(x, approximate=True)

def _silu(x):
    return jax.nn.silu(x)

def _sigmoid(x):
    return jax.nn.sigmoid(x)

def _layernorm(x, axis=-1, eps=1e-05):
    m = jnp.mean(x, axis=axis, keepdims=True)
    v = jnp.var(x, axis=axis, keepdims=True)
    return (x - m) / jnp.sqrt(v + eps)

def _scatter_add(tgt, idx, src, axis=0):
    return tgt.at[idx].add(src)

def _segment_sum(src, seg, n):
    return jax.ops.segment_sum(src, seg, n)
kernel_name = 'mk_xattn_seq_d2_seqx_r8_552bdf'

def setup_inputs(seed: int=0):
    np.random.seed(seed)
    _w = jnp.asarray

    def _rec_inputs():
        import jax
        import jax.numpy as jnp
        _rk = jax.random.key(seed)
        x = 7.22e-05 + 1 * jax.random.normal(jax.random.fold_in(_rk, 1), (32, 56, 256), jnp.float32)
        _lenS = 56 - jax.random.randint(jax.random.fold_in(_rk, 7), (32,), 0, max(1, 56 // 4) + 1, jnp.int32)
        _lenS2 = 1500 - jax.random.randint(jax.random.fold_in(_rk, 8), (32,), 0, max(1, 1500 // 4) + 1, jnp.int32)
        _ctx_2048P = jax.random.normal(jax.random.fold_in(_rk, 11), (32, 16, 256), jnp.float32)
        _ctx_2048c = jax.random.dirichlet(jax.random.fold_in(_rk, 511), 0.3 * jnp.ones((16,), jnp.float32), (32, 1500))
        _ctx_2048t = jnp.einsum('bsk,bkd->bsd', _ctx_2048c, _ctx_2048P)
        _ctx_2048t = _ctx_2048t * jax.lax.rsqrt(jnp.mean(jnp.square(_ctx_2048t)) + 1e-12) * 0.953939
        ctx_2048 = 2.81802e-05 + 1.00001 * (_ctx_2048t + 0.3 * jax.random.normal(jax.random.fold_in(_rk, 611), (32, 1500, 256), jnp.float32))
        _validS = jnp.arange(56)[None, :] < _lenS[:, None]
        _validS2 = jnp.arange(1500)[None, :] < _lenS2[:, None]
        _causal = jnp.tril(jnp.ones((56, 56), dtype=bool))
        mask_BxS2_bf1 = jnp.ones((32, 1500), dtype=bool)
        mask_Bx1xSxS2_ff0 = jnp.where(jnp.ones((32, 1, 56, 1500), dtype=bool), 0.0, -1000000000.0).astype(jnp.float32)
        return (x, ctx_2048, mask_BxS2_bf1, mask_Bx1xSxS2_ff0)
    x, ctx_2048, mask_BxS2_bf1, mask_Bx1xSxS2_ff0 = _rec_inputs()

    def _L0_xattn_setup():
        import jax, jax.numpy as jnp
        import numpy as np
        D = 256
        H = 16
        HD = D // H
        INNER = 4 * D
        EPS = 1e-05

        def layer_norm(x, w, b):
            mu = jnp.mean(x, axis=-1, keepdims=True)
            var = jnp.mean(jnp.square(x - mu), axis=-1, keepdims=True)
            return (x - mu) * jax.lax.rsqrt(var + EPS) * w + b
        key = jax.random.key(seed)
        ks = jax.random.split(key, 12)
        B, LQ, LK = (4, 128, 256)
        std = 0.02
        inp = {'hidden_states': jax.random.normal(ks[0], (B, LQ, D), jnp.float32), 'encoder_hidden_states': jax.random.normal(ks[1], (B, LK, D), jnp.float32), 'encoder_attention_mask': jnp.ones((B, LK), dtype=bool), 'ln1_w': jnp.ones((D,), jnp.float32), 'ln1_b': jnp.zeros((D,), jnp.float32), 'q_w': jax.random.normal(ks[2], (D, D), jnp.float32) * std, 'q_b': jnp.zeros((D,), jnp.float32), 'k_w': jax.random.normal(ks[3], (D, D), jnp.float32) * std, 'k_b': jnp.zeros((D,), jnp.float32), 'v_w': jax.random.normal(ks[4], (D, D), jnp.float32) * std, 'v_b': jnp.zeros((D,), jnp.float32), 'cproj_w': jax.random.normal(ks[5], (D, D), jnp.float32) * std, 'cproj_b': jnp.zeros((D,), jnp.float32), 'ln2_w': jnp.ones((D,), jnp.float32), 'ln2_b': jnp.zeros((D,), jnp.float32), 'fc_w': jax.random.normal(ks[6], (D, INNER), jnp.float32) * std, 'fc_b': jnp.zeros((INNER,), jnp.float32), 'proj_w': jax.random.normal(ks[7], (INNER, D), jnp.float32) * std, 'proj_b': jnp.zeros((D,), jnp.float32)}
        return inp
    _L0_xattn_all = _L0_xattn_setup()
    _L0_xattn_in = {k: v for k, v in _L0_xattn_all.items() if k in ('ln1_w', 'ln1_b', 'q_w', 'q_b', 'k_w', 'k_b', 'v_w', 'v_b', 'cproj_w', 'cproj_b', 'ln2_w', 'ln2_b', 'fc_w', 'fc_b', 'proj_w', 'proj_b')}
    del _L0_xattn_all

    def _L1_xattn_setup():
        import jax, jax.numpy as jnp
        import numpy as np
        H = 256
        NH = 32
        KVH = 8
        HD = H // NH
        GROUPS = NH // KVH
        EPS = 1e-06
        B, L, S = (4, 128, 128)

        def _gqa_forward(hidden_state, encoder_hidden_state, encoder_attention_mask, Wq, bq, Wk, bk, Wv, bv, Wo, bo, gamma, beta):
            b, l, _ = hidden_state.shape
            s = encoder_hidden_state.shape[1]
            q = hidden_state @ Wq + bq
            k = encoder_hidden_state @ Wk + bk
            v = encoder_hidden_state @ Wv + bv
            q = q.reshape(b, l, KVH, GROUPS, HD).transpose(0, 2, 3, 1, 4)
            k = k.reshape(b, s, KVH, HD).transpose(0, 2, 1, 3)
            v = v.reshape(b, s, KVH, HD).transpose(0, 2, 1, 3)
            scale = 1.0 / jnp.sqrt(jnp.asarray(HD, q.dtype))
            scores = jnp.einsum('bkgld,bksd->bkgls', q, k) * scale
            scores = scores + encoder_attention_mask[:, :, None, :, :]
            attn = jax.nn.softmax(scores, axis=-1)
            out = jnp.einsum('bkgls,bksd->bkgld', attn, v)
            out = out.transpose(0, 3, 1, 2, 4).reshape(b, l, H)
            out = out @ Wo + bo
            x = out + hidden_state
            mu = jnp.mean(x, axis=-1, keepdims=True)
            var = jnp.var(x, axis=-1, keepdims=True)
            return (x - mu) * jax.lax.rsqrt(var + EPS) * gamma + beta
        key = jax.random.key(seed)
        ks = jax.random.split(key, 12)
        sd = 0.02
        return {'hidden_state': jax.random.normal(ks[0], (B, L, H), jnp.float32), 'encoder_hidden_state': jax.random.normal(ks[1], (B, S, H), jnp.float32), 'encoder_attention_mask': jnp.zeros((B, 1, L, S), jnp.float32), 'Wq': jax.random.normal(ks[2], (H, H), jnp.float32) * sd, 'bq': jnp.zeros((H,), jnp.float32), 'Wk': jax.random.normal(ks[3], (H, KVH * HD), jnp.float32) * sd, 'bk': jnp.zeros((KVH * HD,), jnp.float32), 'Wv': jax.random.normal(ks[4], (H, KVH * HD), jnp.float32) * sd, 'bv': jnp.zeros((KVH * HD,), jnp.float32), 'Wo': jax.random.normal(ks[5], (H, H), jnp.float32) * sd, 'bo': jnp.zeros((H,), jnp.float32), 'gamma': jnp.ones((H,), jnp.float32), 'beta': jnp.zeros((H,), jnp.float32)}
    _L1_xattn_all = _L1_xattn_setup()
    _L1_xattn_in = {k: v for k, v in _L1_xattn_all.items() if k in ('Wq', 'bq', 'Wk', 'bk', 'Wv', 'bv', 'Wo', 'bo', 'gamma', 'beta')}
    del _L1_xattn_all
    return {'x': x, 'ctx_2048': ctx_2048, 'mask_BxS2_bf1': mask_BxS2_bf1, 'mask_Bx1xSxS2_ff0': mask_Bx1xSxS2_ff0, 'L0_xattn_ln1_w': _L0_xattn_in['ln1_w'], 'L0_xattn_ln1_b': _L0_xattn_in['ln1_b'], 'L0_xattn_q_w': _L0_xattn_in['q_w'], 'L0_xattn_q_b': _L0_xattn_in['q_b'], 'L0_xattn_k_w': _L0_xattn_in['k_w'], 'L0_xattn_k_b': _L0_xattn_in['k_b'], 'L0_xattn_v_w': _L0_xattn_in['v_w'], 'L0_xattn_v_b': _L0_xattn_in['v_b'], 'L0_xattn_cproj_w': _L0_xattn_in['cproj_w'], 'L0_xattn_cproj_b': _L0_xattn_in['cproj_b'], 'L0_xattn_ln2_w': _L0_xattn_in['ln2_w'], 'L0_xattn_ln2_b': _L0_xattn_in['ln2_b'], 'L0_xattn_fc_w': _L0_xattn_in['fc_w'], 'L0_xattn_fc_b': _L0_xattn_in['fc_b'], 'L0_xattn_proj_w': _L0_xattn_in['proj_w'], 'L0_xattn_proj_b': _L0_xattn_in['proj_b'], 'L1_xattn_Wq': _L1_xattn_in['Wq'], 'L1_xattn_bq': _L1_xattn_in['bq'], 'L1_xattn_Wk': _L1_xattn_in['Wk'], 'L1_xattn_bk': _L1_xattn_in['bk'], 'L1_xattn_Wv': _L1_xattn_in['Wv'], 'L1_xattn_bv': _L1_xattn_in['bv'], 'L1_xattn_Wo': _L1_xattn_in['Wo'], 'L1_xattn_bo': _L1_xattn_in['bo'], 'L1_xattn_gamma': _L1_xattn_in['gamma'], 'L1_xattn_beta': _L1_xattn_in['beta']}

def reference(x, ctx_2048, mask_BxS2_bf1, mask_Bx1xSxS2_ff0, L0_xattn_ln1_w, L0_xattn_ln1_b, L0_xattn_q_w, L0_xattn_q_b, L0_xattn_k_w, L0_xattn_k_b, L0_xattn_v_w, L0_xattn_v_b, L0_xattn_cproj_w, L0_xattn_cproj_b, L0_xattn_ln2_w, L0_xattn_ln2_b, L0_xattn_fc_w, L0_xattn_fc_b, L0_xattn_proj_w, L0_xattn_proj_b, L1_xattn_Wq, L1_xattn_bq, L1_xattn_Wk, L1_xattn_bk, L1_xattn_Wv, L1_xattn_bv, L1_xattn_Wo, L1_xattn_bo, L1_xattn_gamma, L1_xattn_beta):
    import jax
    import jax.numpy as jnp

    def _L0_xattn_ref(hidden_states, encoder_hidden_states, encoder_attention_mask, ln1_w, ln1_b, q_w, q_b, k_w, k_b, v_w, v_b, cproj_w, cproj_b, ln2_w, ln2_b, fc_w, fc_b, proj_w, proj_b):
        import jax, jax.numpy as jnp
        import numpy as np
        D = 256
        H = 16
        HD = D // H
        INNER = 4 * D
        EPS = 1e-05

        def layer_norm(x, w, b):
            mu = jnp.mean(x, axis=-1, keepdims=True)
            var = jnp.mean(jnp.square(x - mu), axis=-1, keepdims=True)
            return (x - mu) * jax.lax.rsqrt(var + EPS) * w + b
        B, LQ, _ = hidden_states.shape
        LK = encoder_hidden_states.shape[1]
        residual = hidden_states
        x = layer_norm(hidden_states, ln1_w, ln1_b)
        q = (x @ q_w + q_b).reshape(B, LQ, H, HD).transpose(0, 2, 1, 3)
        k = (encoder_hidden_states @ k_w + k_b).reshape(B, LK, H, HD).transpose(0, 2, 1, 3)
        v = (encoder_hidden_states @ v_w + v_b).reshape(B, LK, H, HD).transpose(0, 2, 1, 3)
        scale = 1.0 / np.sqrt(HD).astype(np.float32)
        scores = jnp.einsum('bhqd,bhkd->bhqk', q, k) * scale
        mask = encoder_attention_mask[:, None, None, :]
        mask_value = jnp.finfo(scores.dtype).min
        scores = jnp.where(mask, scores, mask_value)
        attn = jax.nn.softmax(scores, axis=-1)
        out = jnp.einsum('bhqk,bhkd->bhqd', attn, v)
        out = out.transpose(0, 2, 1, 3).reshape(B, LQ, D)
        out = out @ cproj_w + cproj_b
        hidden = out + residual
        residual = hidden
        y = layer_norm(hidden, ln2_w, ln2_b)
        y = jax.nn.gelu(y @ fc_w + fc_b, approximate=True)
        y = y @ proj_w + proj_b
        return residual + y

    def _L1_xattn_ref(hidden_state, encoder_hidden_state, encoder_attention_mask, Wq, bq, Wk, bk, Wv, bv, Wo, bo, gamma, beta):
        import jax, jax.numpy as jnp
        import numpy as np
        H = 256
        NH = 32
        KVH = 8
        HD = H // NH
        GROUPS = NH // KVH
        EPS = 1e-06
        B, L, S = (4, 128, 128)

        def _gqa_forward(hidden_state, encoder_hidden_state, encoder_attention_mask, Wq, bq, Wk, bk, Wv, bv, Wo, bo, gamma, beta):
            b, l, _ = hidden_state.shape
            s = encoder_hidden_state.shape[1]
            q = hidden_state @ Wq + bq
            k = encoder_hidden_state @ Wk + bk
            v = encoder_hidden_state @ Wv + bv
            q = q.reshape(b, l, KVH, GROUPS, HD).transpose(0, 2, 3, 1, 4)
            k = k.reshape(b, s, KVH, HD).transpose(0, 2, 1, 3)
            v = v.reshape(b, s, KVH, HD).transpose(0, 2, 1, 3)
            scale = 1.0 / jnp.sqrt(jnp.asarray(HD, q.dtype))
            scores = jnp.einsum('bkgld,bksd->bkgls', q, k) * scale
            scores = scores + encoder_attention_mask[:, :, None, :, :]
            attn = jax.nn.softmax(scores, axis=-1)
            out = jnp.einsum('bkgls,bksd->bkgld', attn, v)
            out = out.transpose(0, 3, 1, 2, 4).reshape(b, l, H)
            out = out @ Wo + bo
            x = out + hidden_state
            mu = jnp.mean(x, axis=-1, keepdims=True)
            var = jnp.var(x, axis=-1, keepdims=True)
            return (x - mu) * jax.lax.rsqrt(var + EPS) * gamma + beta
        return _gqa_forward(hidden_state, encoder_hidden_state, encoder_attention_mask, Wq, bq, Wk, bk, Wv, bv, Wo, bo, gamma, beta)
    x = _L0_xattn_ref(x, ctx_2048, mask_BxS2_bf1, L0_xattn_ln1_w, L0_xattn_ln1_b, L0_xattn_q_w, L0_xattn_q_b, L0_xattn_k_w, L0_xattn_k_b, L0_xattn_v_w, L0_xattn_v_b, L0_xattn_cproj_w, L0_xattn_cproj_b, L0_xattn_ln2_w, L0_xattn_ln2_b, L0_xattn_fc_w, L0_xattn_fc_b, L0_xattn_proj_w, L0_xattn_proj_b)
    x = _L1_xattn_ref(x, ctx_2048, mask_Bx1xSxS2_ff0, L1_xattn_Wq, L1_xattn_bq, L1_xattn_Wk, L1_xattn_bk, L1_xattn_Wv, L1_xattn_bv, L1_xattn_Wo, L1_xattn_bo, L1_xattn_gamma, L1_xattn_beta)
    return x

_drawn_inputs = setup_inputs


def setup_inputs(seed=0):
    import zlib

    import numpy as np

    out = dict(_drawn_inputs(seed))
    spreads = {'L0_xattn_ln1_w': (1.0, 0.6),
     'L0_xattn_ln1_b': (0.0, 0.8),
     'L0_xattn_q_b': (0.0, 0.8),
     'L0_xattn_k_b': (0.0, 0.8),
     'L0_xattn_v_b': (0.0, 0.1),
     'L0_xattn_cproj_b': (0.0, 0.1),
     'L0_xattn_ln2_w': (1.0, 0.6),
     'L0_xattn_ln2_b': (0.0, 0.745),
     'L0_xattn_fc_b': (0.0, 0.1),
     'L0_xattn_proj_b': (0.0, 0.1),
     'L1_xattn_bq': (0.0, 0.8),
     'L1_xattn_bk': (0.0, 0.8),
     'L1_xattn_bv': (0.0, 0.1),
     'L1_xattn_bo': (0.0, 0.1),
     'L1_xattn_gamma': (1.0, 0.2),
     'L1_xattn_beta': (0.0, 0.1)}
    factors = {'L0_xattn_q_w': 8.0, 'L0_xattn_k_w': 8.0, 'L1_xattn_Wq': 8.0, 'L1_xattn_Wk': 8.0}
    for name, (base, spread) in spreads.items():
        noise = np.random.default_rng([zlib.crc32(name.encode()), seed]).standard_normal(out[name].shape)
        drawn = base * np.exp(spread * noise) if base else spread * noise
        out[name] = jnp.asarray(drawn.astype(out[name].dtype))
    for name, factor in factors.items():
        out[name] = (out[name] * factor).astype(out[name].dtype)
    return out
```

```python
from contextlib import ExitStack

import numpy as np
import concourse.bass as bass
from concourse import mybir

F32 = mybir.dt.float32
BF16 = mybir.dt.bfloat16
U8 = mybir.dt.uint8
ALU = mybir.AluOpType
ACT = mybir.ActivationFunctionType
AX = mybir.AxisListType

B, LQ, D, LK = 32, 56, 256, 1500
TOK = B * LQ
KT = D // 128
NKT, KP = 12, 125
NCH, CH = 3, 500
HU = 8
COLS = HU * LQ
SLOTS = NKT
INNER = 4 * D
BIG = float(2.0 ** 126)
K_PART = (0, 0, 1, 1, 0, 2)
Q_PART = (0, 1, 0, 1, 2, 0)
NPR = 3
NMX = 3
STACK_DMAS = 14
SUB = 2 * LQ
CHUNK = 4 * SUB
NCHUNK = TOK // CHUNK


class Layer:
    def __init__(self, n, heads, kv_heads, eps):
        self.n, self.heads, self.kv, self.eps = n, heads, kv_heads, eps
        self.hd = D // heads
        self.ub = heads // HU
        self.upi = 2 * self.ub
        self.nu = B * self.ub
        self.hk = HU * kv_heads // heads
        self.m_row = 97 if n == 0 else 104
        self.kvd = kv_heads * self.hd
        self.krows = min(128, self.kvd)
        self.scale = float(self.hd) ** -0.5
        if n == 0:
            self.events = {0: "V", 1: "m", 2: "K", 3: "V", 4: "V", 5: "K", 6: "V", 7: "V", 8: "K", 10: "V"}
        else:
            self.events = {1: "m", 4: "T", 8: "K"}
        self.vt = NKT // self.ub
        self.v_copies = NKT if n == 0 else NCH


L0 = Layer(0, 16, 16, 1e-5)
L1 = Layer(1, 32, 8, 1e-6)


def wait(eng, sem, n, apart=False):
    if not isinstance(n, int):
        eng.wait_ge(sem, n)
        if apart:
            eng.nop(nofuse=True)
    elif n > 0:
        eng.wait_ge(sem, n)


def attention(nc, ly, q_parts, ctx_t, kmask, amask, wk, bk, wv, k_const, q_const, i2_d, ident_d, key_dram, o_t):
    P = f"a{ly.n}_"
    UB, UPI, NU, HD, HK = ly.ub, ly.upi, ly.nu, ly.hd, ly.hk
    NI = B // 2
    M = ly.m_row
    CR = 6 * HD
    VW = HD + 1
    VROW = ly.kv * VW
    first = ly.n == 0

    with ExitStack() as ctx:
        def sb(name, shape, dt):
            return ctx.enter_context(nc.sbuf_tensor(P + name, shape, dt))

        def pb(name, shape, dt=F32):
            return ctx.enter_context(nc.psum_tensor(P + name, shape, dt))

        def sem(name):
            return ctx.enter_context(nc.semaphore(P + name))

        stack_k = [sb(f"stack_k{i}", [128, HK, LK], BF16) for i in range(4)]
        stack_q = [sb(f"stack_q{i}", [128, HU, LQ], BF16) for i in range(4)]
        ctxt = [sb(f"ctxt{i}", [128, KT, LK], F32) for i in range(2)]
        k32 = [sb(f"k32_{i}", [128, CH if first else LK], F32) for i in range(2)]
        k_rest = sb("k_rest", [128, CH if first else LK], F32)
        k_parts = [sb(f"k_parts{i}", [128, 3, LK], BF16) for i in range(2)]
        v_sb = [sb(f"v_sb{i}", [128, NKT, ly.kv, VW], F32) for i in range(2)]
        probs = [sb(f"probs{i}", [128, COLS], F32) for i in range(NPR)]
        ot_sb = [sb(f"ot_sb{i}", [128, 2, LQ], F32) for i in range(2)]
        w_sb = sb("w_sb", [128, KT, 2, ly.kvd], F32)
        bk_sb = sb("bk_sb", [128, 2], F32)
        ident = sb("ident", [128, 128], F32)
        identb = sb("identb", [128, 128], BF16)
        pair_max = [sb(f"pair_max{i}", [128, 4, NCH], F32) for i in range(2)]
        row_max = sb("row_max", [128, 4], F32)
        max_rest = sb("max_rest", [128, 4], F32)
        neg_parts = [sb(f"neg_parts{i}", [128, 4, 3], BF16) for i in range(2)]
        neg_rows = [sb(f"neg_rows{i}", [3, HU, LQ], BF16) for i in range(2)]
        if not first:
            v_t = [sb(f"v_t{i}", [128, LK], F32) for i in range(2)]
        if first:
            kmask_sb = [sb(f"kmask{i}", [128, LK], U8) for i in range(2)]
            bias_row = [sb(f"bias_row{i}", [1, LK], BF16) for i in range(2)]
        else:
            mask_f = sb("mask_f", [128, LK], F32)
            mask_rest = sb("mask_rest", [128, LK], F32)
            mask_p = [sb(f"mask_p{i}", [128, LK], BF16) for i in range(2)]
            mask_p2 = [sb(f"mask_p2_{i}", [128, LK], BF16) for i in range(2)]
            mask_01 = [sb(f"mask_01_{i}", [128, LK], F32) for i in range(2)]
            stack_m = [sb(f"stack_m{i}", [128, LK], BF16) for i in range(2)]
            i2 = sb("i2", [128, COLS], BF16)

        mx = [pb(f"mx{i}", [128, 512]) for i in range(NMX)]
        ex = [pb(f"ex{i}", [128, 512]) for i in range(2)]
        pv = [pb(f"pv{i}", [128, 512]) for i in range(2)]
        pj = pb("pj", [128, 512])

        s_const = sem("const_loaded")
        s_init = sem("init_done")
        s_identb = sem("identb_done")
        s_ctx = [sem(f"ctx_loaded{i}") for i in range(2)]
        s_kstore = [sem(f"key_parts_stored{i}") for i in range(2)]
        s_stack = [sem(f"stack_loaded{i}") for i in range(4)]
        s_neg = [sem(f"neg_rows_loaded{i}") for i in range(2)]
        s_ot = [sem(f"o_t_stored{i}") for i in range(2)]
        s_scored = sem("exp_tile_scored")
        s_exp = sem("exp_done")
        s_pv = sem("probs_used")
        s_otc = sem("o_t_copied")
        s_mxs = sem("max_tile_scored")
        s_mxd = sem("max_tile_reduced")
        s_rm = sem("row_max_steps")
        s_np = sem("neg_parts_done")
        s_pjf = sem("proj_bank_filled")
        s_vd = sem("value_tile_done")
        s_kd = sem("key_chunk_done")
        s_kp = sem("key_part_steps")
        s_vt = sem("value_chunk_copied")
        s_ng = sem("neg_rows_done")
        if first:
            s_bias = sem("bias_row_done")
        else:
            s_mf = sem("mask_loaded")
            s_ms = sem("mask_steps")
            s_m01 = sem("mask_01_done")
            s_m2 = sem("mask_p2_done")
            s_stm = sem("stack_m_loaded")

        def is_in(i, v, total=NU, per=UPI):
            return not isinstance(i, int) or 0 <= per * i + v < total

        def q(i, v, k):
            return (UPI // k) * i + v // k

        def pj_events(i, v, slot):
            found = []
            for e in ly.events.get(slot, ""):
                batch = v // UB
                if e == "m" and is_in(i, v + 1):
                    found.append(("m", 0))
                if e == "V" and is_in(i, batch + 1, B, 2):
                    n = [s for s in sorted(ly.events) if "V" in ly.events[s]].index(slot)
                    found.append(("V", (v % UB) * ly.vt + n))
                if e == "T" and v % UB < NCH and is_in(i, batch + 1, B, 2):
                    found.append(("T", v % UB))
                if e == "K" and is_in(i, batch + 2, B, 2):
                    if first:
                        found.append(("K", [s for s in sorted(ly.events) if "K" in ly.events[s]].index(slot)))
                    elif v % UB < NCH:
                        found.append(("K", v % UB))
            return found

        def all_events(i):
            return [(v, *e) for v in range(UPI) for s in range(SLOTS) for e in pj_events(i, v, s)]

        PJ_BEFORE, PJ_PER = len(all_events(-1)), len(all_events(0))

        def pj_base(i):
            return 0 if isinstance(i, int) and i < 0 else PJ_PER * i + PJ_BEFORE

        def iterations(eng, body):
            body(-1)
            body(0)
            with eng.Fori(1, NI - 1) as i:
                body(i)
            body(NI - 1)

        def stack_count(i, v):
            return 16 * STACK_DMAS * (q(i, v, 4) + 1)

        loads = [(w_sb[:, :, 0, :], wk.rearrange("(k p) n -> p k n", p=128)),
                 (w_sb[:, :, 1, :], wv.rearrange("(k p) n -> p k n", p=128)),
                 (bk_sb[0:ly.krows, 0:ly.kvd // ly.krows], bk[:]),
                 (ident[:], ident_d[:])]
        for s in range(4):
            loads.append((stack_k[s][128 - k_const.shape[0]:, :, :],
                          k_const.unsqueeze(1).to_broadcast([k_const.shape[0], HK, LK])))
            loads.append((stack_q[s][CR:, :, :], q_const.rearrange("p (h q) -> p h q", h=HU)))
        if not first:
            loads.append((i2[:], i2_d[:]))
        MEMSETS = 7 if first else 12

        KSTEPS = 4 * NCH

        def ready(eng):
            eng.wait_ge(s_const, 16 * len(loads))
            eng.wait_ge(s_init, MEMSETS)

        block = ctx.enter_context(nc.Block())

        @block.sync
        def _(sp):
            for dst, src in loads:
                sp.dma_start(dst, src).then_inc(s_const, 16)
            ready(sp)

            def body(i):
                for v in range(UPI):
                    b = v // UB
                    if v % UB == 0 and is_in(i, b + 2, B, 2):
                        n = 2 * i + b + 2
                        if first:
                            wait(sp, s_vd, NKT * (n - 1), apart=True)
                        else:
                            wait(sp, s_kd, NCH * (n - 1), apart=True)
                            wait(sp, s_vt, NCH * (n - 1), apart=True)
                        sp.dma_start(ctxt[b % 2][:], ctx_t[n].rearrange("(k p) s -> p k s", p=128)).then_inc(s_ctx[b % 2], 16)
                        if first:
                            sp.dma_start(kmask_sb[b % 2][:],
                                         kmask[n].rearrange("(o s) -> o s", o=1).to_broadcast([128, LK])
                                         ).then_inc(s_ctx[b % 2], 16)
                        else:
                            wait(sp, s_m01, n, apart=True)
                            for h in range(2):
                                sp.dma_start(mask_f[64 * h:64 * h + LQ, :], amask[n]).then_inc(s_mf, 16)
                    if not first and v % UB == 0 and is_in(i, b + 1, B, 2):
                        n = 2 * i + b + 1
                        wait(sp, s_m2, n + 1, apart=True)
                        wait(sp, s_scored, SLOTS * UB * (n - 1), apart=True)
                        for h in range(2):
                            sp.dma_start(stack_m[(b + 1) % 2][64 * h:64 * h + LQ, :],
                                         mask_p[h][64 * h:64 * h + LQ, :]).then_inc(s_stm, 16)
                    if is_in(i, v + 3):
                        w = v + 3
                        s = w % 4
                        wb = w // UB
                        wait(sp, s_scored, SLOTS * (UPI * i + w - 3), apart=True)
                        if first:
                            wait(sp, s_kstore[w % 2], 16 * (q(i, w, 2) + 1), apart=True)
                            wait(sp, s_bias, 2 * i + wb + 1, apart=True)
                            sp.dma_start(stack_k[s][96:97, :, :],
                                         bias_row[wb % 2][:].unsqueeze(1).to_broadcast([1, HK, LK])
                                         ).then_inc(s_stack[s], 16)
                            src_k = key_dram[w % 4]
                        else:
                            wait(sp, s_kstore[wb % 2], 16 * (i + wb // 2 + 1), apart=True)
                            wait(sp, s_m2, 2 * i + wb + 1, apart=True)
                            sp.dma_start(stack_k[s][CR:CR + LQ, :, :],
                                         mask_p2[wb % 2][0:LQ, :].unsqueeze(1).to_broadcast([LQ, HK, LK])
                                         ).then_inc(s_stack[s], 16)
                            src_k = key_dram[wb % 2, (w % UB) * HK * HD:(w % UB + 1) * HK * HD]
                        src_k = src_k.rearrange("(h d) p n -> d p h n", d=HD)
                        col = (2 * i + wb) * LQ
                        hr = (w % UB) * HU * HD
                        for r in range(6):
                            sp.dma_start(stack_k[s][r * HD:(r + 1) * HD, :, :],
                                         src_k[:, K_PART[r]]).then_inc(s_stack[s], 16)
                            sp.dma_start(stack_q[s][r * HD:(r + 1) * HD, :, :],
                                         q_parts[Q_PART[r], hr:hr + HU * HD, bass.ds(col, LQ)].rearrange("(h d) t -> d h t", d=HD)
                                         ).then_inc(s_stack[s], 16)
                        sp.dma_start(stack_q[s][M:M + 3, :, :],
                                     q_const[q_const.shape[0] - 3:, :].rearrange("p (h q) -> p h q", h=HU)).then_inc(s_stack[s], 16)
                    if is_in(i, v + 1):
                        w = v + 1
                        wait(sp, s_ng, UPI * i + w + 1, apart=True)
                        sp.dma_start(stack_q[w % 4][M:M + 3, :, :], neg_rows[w % 2][:]).then_inc(s_neg[w % 2], 16)
                    if first and is_in(i, v + 4):
                        w = v + 4
                        wait(sp, s_kp, KSTEPS * (UPI * i + w + 1), apart=True)
                        wait(sp, s_stack[w % 4], stack_count(i, w - 4), apart=True)
                        sp.dma_start(key_dram[w % 4], k_parts[w % 2][:]).then_inc(s_kstore[w % 2], 16)

            iterations(sp, body)
            for p in range(2):
                sp.wait_ge(s_ot[p], 16 * (NU // 2))

        @block.gpsimd
        def _(pool):
            for x in range(2):
                nc.gpsimd.memset(v_sb[x][:], 1.0).then_inc(s_init, 1)
            if not first:
                for t in (mask_f, mask_01[0], mask_01[1]):
                    nc.gpsimd.memset(t[:], 0.0).then_inc(s_init, 1)
                for x in range(2):
                    nc.gpsimd.memset(stack_m[x][:], 0.0).then_inc(s_init, 1)
            ready(pool)

            def split_keys(i, w, x, n, slot, free):
                rows = ly.krows
                wait(pool, s_kd, NCH * (n + 1), apart=True)
                wait(pool, s_kstore[x], free, apart=True)
                src, rest, parts = k32[x][0:rows, :], k_rest[0:rows, :], k_parts[x][0:rows]
                nc.gpsimd.tensor_copy(parts[:, 0, :], src).then_inc(s_kp, 1)
                wait(pool, s_kp, 4 * n + 1, apart=True)
                nc.gpsimd.tensor_tensor(rest, src, parts[:, 0, :], ALU.subtract).then_inc(s_kp, 1)
                wait(pool, s_kp, 4 * n + 2, apart=True)
                nc.gpsimd.tensor_copy(parts[:, 1, :], rest).then_inc(s_kp, 1)
                wait(pool, s_kp, 4 * n + 3, apart=True)
                nc.gpsimd.tensor_tensor(parts[:, 2, :], rest, parts[:, 1, :], ALU.subtract).then_inc(s_kp, 1)
                wait(pool, s_kp, 4 * n + 4, apart=True)
                wait(pool, *slot, apart=True)
                return parts

            def body(i):
                for v in range(UPI):
                    b = v // UB
                    if not is_in(i, b + 2, B, 2):
                        continue
                    n = 2 * i + b + 2
                    if first:
                        if v % UB == 0:
                            wait(pool, s_ctx[b % 2], 32 * (i + b // 2 + 2), apart=True)
                            wait(pool, s_stack[(v + 1) % 4], stack_count(i, v + 1), apart=True)
                            nc.gpsimd.tensor_scalar(bias_row[b % 2][:], kmask_sb[b % 2][0:1, :], -1.0, BIG,
                                                    ALU.add, ALU.mult).then_inc(s_bias, 1)
                    elif v % UB == 0:
                        wait(pool, s_mf, 32 * (n + 1), apart=True)
                        wait(pool, s_stm, 32 * n, apart=True)
                        wait(pool, s_ms, 4 * n, apart=True)
                        nc.gpsimd.tensor_scalar(mask_f[:], mask_f[:], -BIG, None, ALU.max).then_inc(s_ms, 1)
                        wait(pool, s_ms, 4 * n + 1, apart=True)
                        nc.gpsimd.tensor_copy(mask_p[0][:], mask_f[:]).then_inc(s_ms, 1)
                        wait(pool, s_ms, 4 * n + 2, apart=True)
                        nc.gpsimd.tensor_tensor(mask_rest[:], mask_f[:], mask_p[0][:], ALU.subtract).then_inc(s_ms, 1)
                        wait(pool, s_ms, 4 * n + 3, apart=True)
                        nc.gpsimd.tensor_copy(mask_p[1][:], mask_rest[:]).then_inc(s_ms, 1)
                    elif v % UB == 1:
                        wait(pool, s_ms, 4 * n + 4, apart=True)
                        wait(pool, s_stack[(v + 2) % 4], stack_count(i, v + 2), apart=True)
                        nc.gpsimd.tensor_tensor(mask_p2[b % 2][:], mask_rest[:], mask_p[1][:],
                                                ALU.subtract).then_inc(s_m2, 1)
                    elif v % UB == 2:
                        parts = split_keys(i, v, b % 2, n, (s_stack[(v + 1) % 4], stack_count(i, v + 1)),
                                           16 * (i + b // 2 + 1))
                        pool.dma_start(key_dram[b % 2], parts).then_inc(s_kstore[b % 2], 16)
                    else:
                        wait(pool, s_m2, n + 1, apart=True)
                        wait(pool, s_mxd, SLOTS * UB * (n - 1), apart=True)
                        nc.gpsimd.tensor_tensor(mask_01[b % 2][:], mask_f[:], mask_p2[b % 2][:],
                                                ALU.subtract).then_inc(s_m01, 1)

            iterations(pool, body)

        @block.scalar
        def _(act):
            def drain_o(i, v):
                p = v % 2
                b = v // UB
                wait(act, s_pv, SLOTS * (UPI * i + v + 1))
                wait(act, s_ot[p], 16 * q(i, v, 2))
                nc.scalar.copy(ot_sb[p][:], pv[p][:, 0:2 * LQ].rearrange("p (g q) -> p g q", g=2)).then_inc(s_otc, 1)
                wait(act, s_otc, UPI * i + v + 1)
                g = 2 * (v % UB)
                act.dma_start(o_t[:, g:g + 2, bass.ds((2 * i + b) * LQ, LQ)], ot_sb[p][:]).then_inc(s_ot[p], 16)

            def bank_event(i, v, kind, n, k):
                b = v // UB
                wait(act, s_pjf, pj_base(i) + k + 1)
                if kind == "V":
                    nc.scalar.copy(v_sb[(b + 1) % 2][0:KP, n, :, 0:HD],
                                   pj[0:KP, 0:ly.kvd].rearrange("p (h d) -> p h d", d=HD)).then_inc(s_vd, 1)
                elif kind == "T":
                    nc.scalar.copy(v_sb[(b + 1) % 2][0:KP, 4 * n:4 * n + 4, :, 0:HD],
                                   pj[0:KP, 0:4 * ly.kvd].rearrange("p (t h d) -> p t h d", h=ly.kv, d=HD)).then_inc(s_vd, 1)
                else:
                    nc.scalar.copy(v_t[b % 2][64:128, n * CH:(n + 1) * CH], pj[64:128, 0:CH]).then_inc(s_vt, 1)

            def body(i):
                k = 0
                for v in range(UPI):
                    for slot in range(SLOTS):
                        if is_in(i, v):
                            t = SLOTS * (UPI * i + v) + slot
                            act.wait_ge(s_scored, t + 1)
                            wait(act, s_pv, t + 1 - NPR)
                            n = SLOTS * v + slot
                            nc.scalar.activation(probs[n % NPR][0:KP, :], ex[n % 2][0:KP, 0:COLS],
                                                 ACT.Exp).then_inc(s_exp, 1)
                        if slot == 2 and is_in(i, v) and is_in(i, v - 1):
                            drain_o(i, v - 1)
                        for kind, n in pj_events(i, v, slot):
                            if kind in "VT" or kind == "K" and not first:
                                bank_event(i, v, kind, n, k)
                            k += 1

            iterations(act, body)
            drain_o(NI - 1, UPI - 1)

        @block.vector
        def _(dve):
            for x in range(2):
                nc.vector.memset(pv[x][:], 0.0).then_inc(s_init, 1)
            for x in range(NMX):
                nc.vector.memset(mx[x][:], 0.0).then_inc(s_init, 1)
            ready(dve)
            nc.vector.tensor_copy(identb[:], ident[:]).then_inc(s_identb, 1)

            def bank_event(i, v, kind, n, k):
                b = v // UB
                wait(dve, s_pjf, pj_base(i) + k + 1)
                if kind == "K":
                    if first:
                        w, part = v + 4, k_parts[v % 2][:, :, n * CH:(n + 1) * CH]
                        key, rest = k32[0][:], k_rest[:]
                        done = KSTEPS * (UPI * i + w) + 4 * n
                        if n == 0:
                            wait(dve, s_kstore[w % 2], 16 * q(i, w, 2))
                        nc.vector.scalar_tensor_tensor(
                            out=key, in0=pj[:, 0:CH], scalar=bk_sb[:, w % UB:w % UB + 1],
                            in1=kmask_sb[b % 2][:, n * CH:(n + 1) * CH], op0=ALU.add, op1=ALU.mult).then_inc(s_kd, 1)
                        wait(dve, s_kd, NCH * (UPI * i + w) + n + 1)
                        nc.vector.tensor_copy(part[:, 0], key).then_inc(s_kp, 1)
                        wait(dve, s_kp, done + 1)
                        nc.vector.tensor_tensor(rest, key, part[:, 0], ALU.subtract).then_inc(s_kp, 1)
                        wait(dve, s_kp, done + 2)
                        nc.vector.tensor_copy(part[:, 1], rest).then_inc(s_kp, 1)
                        wait(dve, s_kp, done + 3)
                        nc.vector.tensor_tensor(part[:, 2], rest, part[:, 1], ALU.subtract).then_inc(s_kp, 1)
                    else:
                        if n == 0:
                            wait(dve, s_kp, 4 * (2 * i + b + 1))
                        r = ly.krows
                        nc.vector.tensor_scalar(k32[b % 2][0:r, n * CH:(n + 1) * CH], pj[0:r, 0:CH], bk_sb[0:r, 0:1],
                                                None, ALU.add).then_inc(s_kd, 1)
                else:
                    wait(dve, s_neg[(v + 1) % 2], 16 * q(i, v + 1, 2))
                    nc.vector.tensor_copy(
                        neg_rows[(v + 1) % 2][:].rearrange("p (a h) q -> p a h q", h=2),
                        pj[0:3, :].rearrange("p (a h q) -> p a h q", a=4, h=2)[:, :, :, 0:LQ]).then_inc(s_ng, 1)

            def body(i):
                k = 0
                for v in range(UPI):
                    for slot in range(SLOTS):
                        if is_in(i, v + 2):
                            w = v + 2
                            t = SLOTS * (UPI * i + w) + slot
                            pair, c = slot // NCH, slot % NCH
                            bank = mx[(SLOTS * w + slot) % NMX]
                            dst = pair_max[w % 2][:, pair, c:c + 1]
                            wait(dve, s_mxs, t + 1, apart=not first)
                            if first:
                                nc.vector.tensor_reduce(dst, bank[:, 0:CH], AX.X, ALU.max).then_inc(s_mxd, 1)
                            else:
                                wb = w // UB
                                if slot == 0 and w % UB == 0:
                                    wait(dve, s_m01, 2 * i + wb + 1, apart=True)
                                nc.vector.tensor_tensor_reduce(
                                    out=bank[:, 0:CH], in0=bank[:, 0:CH], in1=mask_01[wb % 2][:, c * CH:(c + 1) * CH],
                                    scale=1.0, scalar=-3.4028235e38, op0=ALU.add, op1=ALU.max,
                                    accum_out=dst).then_inc(s_mxd, 1)
                        for kind, n in pj_events(i, v, slot):
                            if kind in "mK":
                                bank_event(i, v, kind, n, k)
                            k += 1
                    if is_in(i, v + 2):
                        w = v + 2
                        g = 4 * (UPI * i + w)
                        parts = neg_parts[w % 2]
                        wait(dve, s_mxd, SLOTS * (UPI * i + w + 1))
                        nc.vector.tensor_reduce(row_max[:], pair_max[w % 2][:], AX.X, ALU.max).then_inc(s_rm, 1)
                        wait(dve, s_rm, g + 1)
                        wait(dve, s_ng, UPI * i + w - 1)
                        nc.vector.tensor_scalar(parts[:, :, 0], row_max[:], -1.0, None, ALU.mult).then_inc(s_rm, 1)
                        wait(dve, s_rm, g + 2)
                        nc.vector.scalar_tensor_tensor(out=max_rest[:], in0=row_max[:], scalar=-1.0, in1=parts[:, :, 0],
                                                       op0=ALU.mult, op1=ALU.subtract).then_inc(s_rm, 1)
                        wait(dve, s_rm, g + 3)
                        nc.vector.tensor_copy(parts[:, :, 1], max_rest[:]).then_inc(s_rm, 1)
                        wait(dve, s_rm, g + 4)
                        nc.vector.tensor_tensor(parts[:, :, 2], max_rest[:], parts[:, :, 1],
                                                ALU.subtract).then_inc(s_np, 1)

            iterations(dve, body)

        @block.tensor
        def _(pe):
            ready(pe)
            pe.wait_ge(s_identb, 1)

            def exp_scores(i, v, slot):
                s, b = v % 4, v // UB
                k = SLOTS * v + slot
                bank = ex[k % 2]
                keys = slice(slot * KP, (slot + 1) * KP)
                if slot == 0:
                    wait(pe, s_neg[v % 2], 16 * (q(i, v, 2) + 1))
                    if not first and v % UB == 0:
                        wait(pe, s_stm, 32 * (2 * i + b + 1))
                wait(pe, s_exp, SLOTS * (UPI * i + v) + slot - 1)
                if first:
                    for h in range(HU):
                        mm = nc.tensor.matmul(bank[0:KP, h * LQ:(h + 1) * LQ], stack_k[s][:, h, keys],
                                              stack_q[s][:, h, :], start=True, stop=True, skip_group_check=True)
                else:
                    nc.tensor.matmul(bank[0:KP, 0:COLS], stack_m[b % 2][:, keys], i2[:], start=True, stop=False,
                                     skip_group_check=True)
                    for g in range(HK):
                        n = HU // HK
                        mm = nc.tensor.matmul(bank[0:KP, g * n * LQ:(g + 1) * n * LQ], stack_k[s][:, g, keys],
                                              stack_q[s][:, g * n:(g + 1) * n, :], start=False, stop=True,
                                              skip_group_check=True)
                mm.then_inc(s_scored, 1)

            def max_scores(i, w, slot):
                s = w % 4
                pair, c = slot // NCH, slot % NCH
                if slot == 0:
                    wait(pe, s_stack[s], stack_count(i, w))
                wait(pe, s_mxd, SLOTS * (UPI * i + w) + slot + 1 - NMX)
                bank = mx[(SLOTS * w + slot) % NMX]
                for h in range(2):
                    head = 2 * pair + h
                    mm = nc.tensor.matmul(bank[64 * h:64 * h + LQ, 0:CH], stack_q[s][:, head, :],
                                          stack_k[s][:, head * HK // HU, c * CH:(c + 1) * CH], start=True, stop=True,
                                          skip_group_check=True)
                mm.then_inc(s_mxs, 1)

            def use_probs(i, v, slot):
                b = v // UB
                k = SLOTS * v + slot
                p = probs[k % NPR]
                bank = pv[v % 2]
                pe.wait_ge(s_exp, SLOTS * (UPI * i + v) + slot + 1)
                if slot == 0:
                    wait(pe, s_otc, UPI * i + v - 1)
                    if v % UB == 0:
                        wait(pe, s_vd, ly.v_copies * (2 * i + b + 1))
                n = 1 if first else 2
                for g in range(HU // 4 // n):
                    for j in range(4):
                        head = (v % UB) * HU + 4 * g + j if first else 2 * (v % UB) + j // 2
                        at = (4 * g + j) * n * LQ
                        mm = nc.tensor.matmul(bank[32 * j:32 * j + VW, g * n * LQ:(g + 1) * n * LQ],
                                              v_sb[b % 2][0:KP, slot, head, :], p[0:KP, at:at + n * LQ],
                                              start=(slot == 0 and g == 0), stop=(slot == SLOTS - 1),
                                              skip_group_check=True)
                mm.then_inc(s_pv, 1)

            def proj_free(i, k):
                if k > 0:
                    v, kind, n = all_events(i)[k - 1]
                elif isinstance(i, int) and i < 0:
                    return
                else:
                    v, kind, n = all_events(i - 1 if isinstance(i, int) else i)[-1]
                    v -= UPI
                b = v // UB
                if kind in "VT":
                    wait(pe, s_vd, ly.v_copies * (2 * i + b + 1) + n + 1)
                elif kind == "K":
                    if not first:
                        wait(pe, s_vt, NCH * (2 * i + b + 2) + n + 1)
                    wait(pe, s_kd, NCH * (UPI * i + v + 4 if first else 2 * i + b + 2) + n + 1)
                else:
                    wait(pe, s_ng, UPI * i + v + 2)

            def bank_event(i, v, kind, n, k):
                b = v // UB
                proj_free(i, k)
                if kind == "V":
                    for kt in range(KT):
                        mm = nc.tensor.matmul(pj[0:KP, 0:ly.kvd], ctxt[(b + 1) % 2][:, kt, n * KP:(n + 1) * KP],
                                              w_sb[:, kt, 1, :], start=(kt == 0), stop=(kt == KT - 1))
                    mm.then_inc(s_pjf, 1)
                elif kind == "K":
                    if n == 0 and (not first or v % UB == 0):
                        pe.wait_ge(s_ctx[b % 2], (32 if first else 16) * (i + b // 2 + 2))
                    m = (v % UB) * 128 if first else 0
                    for kt in range(KT):
                        mm = nc.tensor.matmul(pj[:, 0:CH], w_sb[:, kt].rearrange("p a n -> p (a n)")[:, m:m + 128],
                                              ctxt[b % 2][:, kt, n * CH:(n + 1) * CH],
                                              start=(kt == 0), stop=(kt == KT - 1))
                    mm.then_inc(s_pjf, 1)
                elif kind == "T":
                    wait(pe, s_vt, NCH * (2 * i + b + 1) + n + 1, apart=True)
                    for t in range(4):
                        at = n * CH + t * KP
                        mm = nc.tensor.transpose(pj[0:KP, t * ly.kvd:(t + 1) * ly.kvd],
                                                 v_t[(b + 1) % 2][64:128, at:at + KP], ident[64:128, 64:128])
                    mm.then_inc(s_pjf, 1)
                else:
                    wait(pe, s_np, UPI * i + v + 2)
                    for pair in range(4):
                        mm = nc.tensor.matmul(pj[0:3, pair * 128:(pair + 1) * 128], neg_parts[(v + 1) % 2][:, pair, :],
                                              identb[:], start=True, stop=True, skip_group_check=True)
                    mm.then_inc(s_pjf, 1)

            def body(i):
                k = 0
                for v in range(UPI):
                    for slot in range(SLOTS):
                        if is_in(i, v):
                            exp_scores(i, v, slot)
                        if is_in(i, v + 2):
                            max_scores(i, v + 2, slot)
                        if slot > 0 and is_in(i, v):
                            use_probs(i, v, slot - 1)
                        if slot == 0 and is_in(i, v - 1):
                            use_probs(i, v - 1, SLOTS - 1)
                        for kind, n in pj_events(i, v, slot):
                            bank_event(i, v, kind, n, k)
                            k += 1
            iterations(pe, body)
            use_probs(NI - 1, UPI - 1, SLOTS - 1)


class Chain:

    def __init__(self, eng, sem, per):
        self.eng, self.sem, self.per, self.n, self.i = eng, sem, per, 0, 0

    def begin(self, i):
        self.i, self.n = i, 0

    def link(self, ins, apart=False):
        ins.then_inc(self.sem, 1)
        self.n += 1
        wait(self.eng, self.sem, self.i * self.per + self.n, apart)

    def end(self):
        assert self.n == self.per, self.n


def row(v, n):
    return v.rearrange("(o n) -> o n", o=1).to_broadcast([128, n])


def row_stats(nc, link, x, eps, stats, aggr, inv_var):
    for s in range(4):
        link(nc.vector.bn_stats(stats[0:SUB, s, :], x[0:SUB, s, :]), apart=True)
        link(nc.vector.bn_aggr(aggr[0:SUB, s, :], stats[0:SUB, s, :]))
    link(nc.vector.tensor_scalar(inv_var[0:SUB, :], aggr[0:SUB, :, 1], eps, None, ALU.add))
    link(nc.vector.reciprocal(inv_var[0:SUB, :], inv_var[0:SUB, :]))


def normalize(nc, link, out, x, aggr, rstd):
    for s in range(4):
        link(nc.vector.tensor_scalar(out[0:SUB, s, :], x[0:SUB, s, :], aggr[0:SUB, s, 0:1], rstd[0:SUB, s:s + 1],
                                     ALU.subtract, ALU.mult))


def transpose_rows(nc, banks, x, ident):
    for kt in range(KT):
        for s in range(4):
            mm = nc.tensor.transpose(banks[kt][:, s * SUB:(s + 1) * SUB], x[0:SUB, s, kt * 128:(kt + 1) * 128],
                                     ident[0:SUB, 0:SUB])
    return mm


def project_queries(nc, banks, w, x_t):
    for m in range(2):
        for kt in range(KT):
            mm = nc.tensor.matmul(banks[m][:, 0:CHUNK], w[:, kt, m * 128:(m + 1) * 128], x_t[:, kt, :],
                                  start=(kt == 0), stop=(kt == KT - 1))
    return mm


def split_queries(nc, link, parts, q32, rest, banks, bias, scale):
    for m in range(2):
        link(nc.vector.tensor_scalar(q32[:, m, :], banks[m][:, 0:CHUNK], bias[:, m:m + 1], scale, ALU.add, ALU.mult))
    link(nc.vector.tensor_copy(parts[:, 0], q32[:]))
    link(nc.vector.tensor_tensor(rest[:], q32[:], parts[:, 0], ALU.subtract))
    link(nc.vector.tensor_copy(parts[:, 1], rest[:]))
    link(nc.vector.tensor_tensor(parts[:, 2], rest[:], parts[:, 1], ALU.subtract))


def first_queries(nc, x, ln_w, ln_b, wq, bq, ident_d, q_parts):
    with ExitStack() as ctx:
        def sb(name, shape, dt=F32):
            return ctx.enter_context(nc.sbuf_tensor("q_" + name, shape, dt))

        def sem(name):
            return ctx.enter_context(nc.semaphore("q_" + name))

        x_sb, xn = sb("x", [128, 4, D]), sb("xn", [128, 4, D])
        x_t = sb("x_t", [128, KT, CHUNK])
        stats, aggr = sb("stats", [128, 4, 6]), sb("aggr", [128, 4, 2])
        inv_var, rstd = sb("inv_var", [128, 4]), sb("rstd", [128, 4])
        s_var, s_rstd = sem("variances_done"), sem("rstd_done")
        w, lw, lb, b, ident = (sb("w", [128, KT, D]), sb("lw", [128, 2]), sb("lb", [128, 2]), sb("b", [128, 2]),
                               sb("ident", [128, 128]))
        q32, rest = sb("q32", [128, 2, CHUNK]), sb("rest", [128, 2, CHUNK])
        parts = sb("parts", [128, 3, 2, CHUNK], BF16)
        t_banks = [ctx.enter_context(nc.psum_tensor(f"q_t{i}", [128, 512], F32)) for i in range(2)]
        q_banks = [ctx.enter_context(nc.psum_tensor(f"q_q{i}", [128, 512], F32)) for i in range(2)]
        s_w, s_x, s_out = sem("weights_loaded"), sem("x_loaded"), sem("queries_stored")
        s_xn, s_tp, s_xt, s_qp, s_q, s_dve = (sem("x_normed"), sem("x_transposed"), sem("x_t_done"),
                                              sem("queries_projected"), sem("queries_split"), sem("dve_steps"))
        loads = [(w[:], wq.rearrange("(k p) n -> p k n", p=128)), (lw[:], ln_w[:]), (lb[:], ln_b[:]),
                 (b[:], bq[:]), (ident[:], ident_d[:])]
        block = ctx.enter_context(nc.Block())

        @block.sync
        def _(sp):
            for dst, src in loads:
                sp.dma_start(dst, src).then_inc(s_w, 16)
            with sp.Fori(0, NCHUNK) as i:
                sp.dma_start(x_sb[0:SUB], x[bass.ds(i * CHUNK, CHUNK), :].rearrange("(s p) d -> p s d", p=SUB)).then_inc(s_x, 16)
                wait(sp, s_q, i + 1, apart=True)
                for p in range(3):
                    sp.dma_start(q_parts[p, :, bass.ds(i * CHUNK, CHUNK)].rearrange("(m p) t -> p m t", p=128),
                                 parts[:, p]).then_inc(s_out, 16)
            sp.wait_ge(s_out, 48 * NCHUNK)

        @block.scalar
        def _(act):
            with act.Fori(0, NCHUNK) as i:
                act.wait_ge(s_var, i + 1)
                nc.scalar.activation(rstd[0:SUB, :], inv_var[0:SUB, :], ACT.Sqrt).then_inc(s_rstd, 1)

        @block.vector
        def _(dve):
            chain = Chain(dve, s_dve, 22)
            dve.wait_ge(s_w, 16 * len(loads))
            with dve.Fori(0, NCHUNK) as i:
                chain.begin(i)
                dve.wait_ge(s_x, 16 * i + 16)
                row_stats(nc, chain.link, x_sb, L0.eps, stats, aggr, inv_var)
                dve.sem_inc(s_var, 1)
                dve.wait_ge(s_rstd, i + 1)
                normalize(nc, chain.link, xn, x_sb, aggr, rstd)
                dve.sem_inc(s_xn, 1)
                dve.wait_ge(s_tp, i + 1)
                for kt in range(KT):
                    chain.link(nc.vector.tensor_scalar(x_t[:, kt, :], t_banks[kt][:, 0:CHUNK], lw[:, kt:kt + 1],
                                                       lb[:, kt:kt + 1], ALU.mult, ALU.add))
                dve.sem_inc(s_xt, 1)
                dve.wait_ge(s_qp, i + 1)
                split_queries(nc, chain.link, parts, q32, rest, q_banks, b, L0.scale)
                dve.sem_inc(s_q, 1)
                dve.wait_ge(s_out, 48 * i + 48)
                chain.end()

        @block.tensor
        def _(pe):
            pe.wait_ge(s_w, 16 * len(loads))
            with pe.Fori(0, NCHUNK) as i:
                pe.wait_ge(s_xn, i + 1)
                transpose_rows(nc, t_banks, xn, ident).then_inc(s_tp, 1)
                pe.wait_ge(s_xt, i + 1)
                project_queries(nc, q_banks, w, x_t).then_inc(s_qp, 1)


def middle(nc, x, o_t, bv, wc, bc, ln_w, ln_b, wf, bf, wp, bp, wq1, bq1, ident_d, hidden_d, q_parts):
    H, HD = L0.heads, L0.hd
    G = H // 4
    MF = INNER // 128
    with ExitStack() as ctx:
        def sb(name, shape, dt=F32):
            return ctx.enter_context(nc.sbuf_tensor("m_" + name, shape, dt))

        def sem(name):
            return ctx.enter_context(nc.semaphore("m_" + name))

        x_sb = sb("x", [128, 4, D])
        ot_sb = sb("ot", [128, G, CHUNK])
        inv = sb("inv", [128, 4, H])
        bv_sb = sb("bv", [128, KT])
        o_sb = sb("o", [128, 4, D])
        t_sb = sb("t", [128, KT, CHUNK])
        hid, yn, out = sb("hid", [128, 4, D]), sb("yn", [128, 4, D]), sb("out", [128, 4, D])
        act_t = sb("act_t", [128, MF, CHUNK])
        stats, aggr = sb("stats", [128, 4, 6]), sb("aggr", [128, 4, 2])
        inv_var, rstd = sb("inv_var", [128, 4]), sb("rstd", [128, 4])
        s_var, s_rstd = sem("variances_done"), sem("rstd_done")
        wc_sb, wf_sb, wp_sb, wq_sb = (sb("wc", [128, KT, D]), sb("wf", [128, KT, INNER]), sb("wp", [128, MF, D]),
                                      sb("wq", [128, KT, D]))
        bc_sb, bp_sb = sb("bc", [128, D]), sb("bp", [128, D])
        lw, lb, bf_sb, bq_sb, ident = (sb("lw", [128, 2]), sb("lb", [128, 2]), sb("bf", [128, MF]), sb("bq", [128, 2]),
                                       sb("ident", [128, 128]))
        q32, rest = sb("q32", [128, 2, CHUNK]), sb("rest", [128, 2, CHUNK])
        parts = sb("parts", [128, 3, 2, CHUNK], BF16)
        bank = [ctx.enter_context(nc.psum_tensor(f"m_b{i}", [128, 512], F32)) for i in range(8)]
        s_w, s_in, s_out = sem("weights_loaded"), sem("inputs_loaded"), sem("outputs_stored")
        s_pe = sem("pe_stages")
        s_on, s_ot, s_yn, s_yt, s_x1, s_x1t, s_q, s_dve = (
            sem("o_normed"), sem("o_t_done"), sem("hidden_normed"), sem("hidden_t_done"), sem("output_done"),
            sem("output_t_done"), sem("queries_split"), sem("dve_steps"))
        s_fc, s_gelu, s_qp = sem("fc_tile_projected"), sem("gelu_done"), sem("queries_projected")
        loads = [(wc_sb[:], wc.rearrange("(k p) n -> p k n", p=128)), (wf_sb[:], wf.rearrange("(k p) n -> p k n", p=128)),
                 (wp_sb[:], wp.rearrange("(k p) n -> p k n", p=128)), (wq_sb[:], wq1.rearrange("(k p) n -> p k n", p=128)),
                 (bc_sb[:], row(bc, D)), (bp_sb[:], row(bp, D)), (lw[:], ln_w[:]), (lb[:], ln_b[:]),
                 (bf_sb[:], bf[:]), (bv_sb[:], bv[:]), (bq_sb[:], bq1[:]), (ident[:], ident_d[:])]
        block = ctx.enter_context(nc.Block())

        @block.sync
        def _(sp):
            for dst, src in loads:
                sp.dma_start(dst, src).then_inc(s_w, 16)
            with sp.Fori(0, NCHUNK) as i:
                sp.dma_start(ot_sb[:], o_t[:, :, bass.ds(i * CHUNK, CHUNK)]).then_inc(s_in, 16)
                sp.dma_start(x_sb[0:SUB], x[bass.ds(i * CHUNK, CHUNK), :].rearrange("(s p) d -> p s d", p=SUB)).then_inc(s_in, 16)
                wait(sp, s_x1, i + 1, apart=True)
                sp.dma_start(hidden_d[bass.ds(i * CHUNK, CHUNK), :].rearrange("(s p) d -> p s d", p=SUB),
                             out[0:SUB]).then_inc(s_out, 16)
                wait(sp, s_q, i + 1, apart=True)
                for p in range(3):
                    sp.dma_start(q_parts[p, :, bass.ds(i * CHUNK, CHUNK)].rearrange("(m p) t -> p m t", p=128),
                                 parts[:, p]).then_inc(s_out, 16)
            sp.wait_ge(s_out, 64 * NCHUNK)

        @block.scalar
        def _(act):
            act.wait_ge(s_w, 16 * len(loads))
            with act.Fori(0, NCHUNK) as i:
                act.wait_ge(s_var, i + 1)
                nc.scalar.activation(rstd[0:SUB, :], inv_var[0:SUB, :], ACT.Sqrt).then_inc(s_rstd, 1)
                for m in range(MF):
                    act.wait_ge(s_fc, i * MF + m + 1)
                    nc.scalar.activation(act_t[:, m, :], bank[m % 4][:, 0:CHUNK], ACT.Gelu_apprx_tanh,
                                         bias=bf_sb[:, m:m + 1]).then_inc(s_gelu, 1)

        @block.vector
        def _(dve):
            chain = Chain(dve, s_dve, 50)
            dve.wait_ge(s_w, 16 * len(loads))
            with dve.Fori(0, NCHUNK) as i:
                chain.begin(i)
                dve.wait_ge(s_in, 32 * i + 32)
                dve.wait_ge(s_pe, 6 * i + 1)
                for s in range(4):
                    o = bank[s][0:SUB, :].rearrange("p (h r) -> p h r", r=32)
                    chain.link(nc.vector.reciprocal(inv[0:SUB, s, :], o[:, :, HD]))
                    chain.link(nc.vector.tensor_tensor(
                        o_sb[0:SUB, s, :].rearrange("p (h d) -> p h d", d=HD), o[:, :, 0:HD],
                        inv[0:SUB, s, :].unsqueeze(2).to_broadcast([SUB, H, HD]), ALU.mult))
                dve.sem_inc(s_on, 1)
                for s in range(4):
                    chain.link(nc.vector.tensor_tensor(x_sb[0:SUB, s, :], x_sb[0:SUB, s, :], bc_sb[0:SUB, :], ALU.add))
                dve.wait_ge(s_pe, 6 * i + 2)
                for kt in range(KT):
                    chain.link(nc.vector.tensor_scalar(t_sb[:, kt, :], bank[4 + kt][:, 0:CHUNK], bv_sb[:, kt:kt + 1],
                                                       None, ALU.add))
                dve.sem_inc(s_ot, 1)
                dve.wait_ge(s_pe, 6 * i + 3)
                for s in range(4):
                    src = bank[6 + s // 2][0:SUB, (s % 2) * D:(s % 2 + 1) * D]
                    chain.link(nc.vector.tensor_tensor(hid[0:SUB, s, :], src, x_sb[0:SUB, s, :], ALU.add))
                row_stats(nc, chain.link, hid, L0.eps, stats, aggr, inv_var)
                dve.sem_inc(s_var, 1)
                dve.wait_ge(s_rstd, i + 1)
                normalize(nc, chain.link, yn, hid, aggr, rstd)
                dve.sem_inc(s_yn, 1)
                dve.wait_ge(s_pe, 6 * i + 4)
                for kt in range(KT):
                    chain.link(nc.vector.tensor_scalar(t_sb[:, kt, :], bank[4 + kt][:, 0:CHUNK], lw[:, kt:kt + 1],
                                                       lb[:, kt:kt + 1], ALU.mult, ALU.add))
                dve.sem_inc(s_yt, 1)
                for s in range(4):
                    chain.link(nc.vector.tensor_tensor(hid[0:SUB, s, :], hid[0:SUB, s, :], bp_sb[0:SUB, :], ALU.add))
                dve.wait_ge(s_pe, 6 * i + 5)
                for s in range(4):
                    src = bank[6 + s // 2][0:SUB, (s % 2) * D:(s % 2 + 1) * D]
                    chain.link(nc.vector.tensor_tensor(out[0:SUB, s, :], src, hid[0:SUB, s, :], ALU.add))
                dve.sem_inc(s_x1, 1)
                dve.wait_ge(s_pe, 6 * i + 6)
                for kt in range(KT):
                    chain.link(nc.vector.tensor_copy(t_sb[:, kt, :], bank[4 + kt][:, 0:CHUNK]))
                dve.sem_inc(s_x1t, 1)
                dve.wait_ge(s_qp, i + 1)
                split_queries(nc, chain.link, parts, q32, rest, bank[0:2], bq_sb, L1.scale)
                dve.sem_inc(s_q, 1)
                dve.wait_ge(s_out, 64 * i + 64)
                chain.end()

        @block.tensor
        def _(pe):
            pe.wait_ge(s_w, 16 * len(loads))
            with pe.Fori(0, NCHUNK) as i:
                pe.wait_ge(s_in, 32 * i + 32)
                for s in range(4):
                    for g in range(G):
                        mm = nc.tensor.transpose(bank[s][0:SUB, g * 128:(g + 1) * 128],
                                                 ot_sb[:, g, s * SUB:(s + 1) * SUB], ident[:])
                mm.then_inc(s_pe, 1)
                pe.wait_ge(s_on, i + 1)
                transpose_rows(nc, bank[4:6], o_sb, ident).then_inc(s_pe, 1)
                pe.wait_ge(s_ot, i + 1)
                for s in range(4):
                    for kt in range(KT):
                        mm = nc.tensor.matmul(bank[6 + s // 2][0:SUB, (s % 2) * D:(s % 2 + 1) * D],
                                              t_sb[:, kt, s * SUB:(s + 1) * SUB], wc_sb[:, kt, :],
                                              start=(kt == 0), stop=(kt == KT - 1))
                mm.then_inc(s_pe, 1)
                pe.wait_ge(s_yn, i + 1)
                transpose_rows(nc, bank[4:6], yn, ident).then_inc(s_pe, 1)
                pe.wait_ge(s_yt, i + 1)
                for m in range(MF):
                    if m >= 4:
                        pe.wait_ge(s_gelu, i * MF + m - 3)
                    for kt in range(KT):
                        mm = nc.tensor.matmul(bank[m % 4][:, 0:CHUNK], wf_sb[:, kt, m * 128:(m + 1) * 128],
                                              t_sb[:, kt, :], start=(kt == 0), stop=(kt == KT - 1))
                    mm.then_inc(s_fc, 1)
                pe.wait_ge(s_gelu, i * MF + MF)
                for s in range(4):
                    for m in range(MF):
                        mm = nc.tensor.matmul(bank[6 + s // 2][0:SUB, (s % 2) * D:(s % 2 + 1) * D],
                                              act_t[:, m, s * SUB:(s + 1) * SUB], wp_sb[:, m, :],
                                              start=(m == 0), stop=(m == MF - 1))
                mm.then_inc(s_pe, 1)
                pe.wait_ge(s_x1, i + 1)
                transpose_rows(nc, bank[4:6], out, ident).then_inc(s_pe, 1)
                pe.wait_ge(s_x1t, i + 1)
                project_queries(nc, bank[0:2], wq_sb, t_sb).then_inc(s_qp, 1)


def last(nc, hidden_d, o_t, bv, wo, bo, gamma, beta, ident_d, out_d):
    H, HD = L1.heads, L1.hd
    G = H // 4
    with ExitStack() as ctx:
        def sb(name, shape, dt=F32):
            return ctx.enter_context(nc.sbuf_tensor("l_" + name, shape, dt))

        def sem(name):
            return ctx.enter_context(nc.semaphore("l_" + name))

        x_sb = sb("x", [128, 4, D])
        ot_sb = sb("ot", [128, G, CHUNK])
        inv = sb("inv", [128, 4, H])
        bv_sb = sb("bv", [128, KT])
        o_sb = sb("o", [128, 4, D])
        t_sb = sb("t", [128, KT, CHUNK])
        hid, yn = sb("hid", [128, 4, D]), sb("yn", [128, 4, D])
        stats, aggr = sb("stats", [128, 4, 6]), sb("aggr", [128, 4, 2])
        inv_var, rstd = sb("inv_var", [128, 4]), sb("rstd", [128, 4])
        s_var, s_rstd = sem("variances_done"), sem("rstd_done")
        wo_sb, bo_sb, ga_sb, be_sb, ident = (sb("wo", [128, KT, D]), sb("bo", [128, D]), sb("ga", [128, D]),
                                             sb("be", [128, D]), sb("ident", [128, 128]))
        bank = [ctx.enter_context(nc.psum_tensor(f"l_b{i}", [128, 512], F32)) for i in range(8)]
        s_w, s_in, s_out = sem("weights_loaded"), sem("inputs_loaded"), sem("outputs_stored")
        s_tp, s_pe, s_on, s_ot, s_y, s_dve = (
            sem("sums_transposed"), sem("pe_stages"), sem("o_normed"), sem("o_t_done"),
            sem("output_done"), sem("dve_steps"))
        loads = [(bv_sb[:], bv[:]), (wo_sb[:], wo.rearrange("(k p) n -> p k n", p=128)), (bo_sb[:], row(bo, D)), (ga_sb[:], row(gamma, D)),
                 (be_sb[:], row(beta, D)), (ident[:], ident_d[:])]
        block = ctx.enter_context(nc.Block())

        @block.sync
        def _(sp):
            for dst, src in loads:
                sp.dma_start(dst, src).then_inc(s_w, 16)
            with sp.Fori(0, NCHUNK) as i:
                sp.dma_start(ot_sb[:], o_t[:, :, bass.ds(i * CHUNK, CHUNK)]).then_inc(s_in, 16)
                sp.dma_start(x_sb[0:SUB], hidden_d[bass.ds(i * CHUNK, CHUNK), :].rearrange("(s p) d -> p s d", p=SUB)).then_inc(s_in, 16)
                wait(sp, s_y, i + 1, apart=True)
                sp.dma_start(out_d[bass.ds(i * CHUNK, CHUNK), :].rearrange("(s p) d -> p s d", p=SUB),
                             yn[0:SUB]).then_inc(s_out, 16)
            sp.wait_ge(s_out, 16 * NCHUNK)

        @block.scalar
        def _(act):
            with act.Fori(0, NCHUNK) as i:
                act.wait_ge(s_var, i + 1)
                nc.scalar.activation(rstd[0:SUB, :], inv_var[0:SUB, :], ACT.Sqrt).then_inc(s_rstd, 1)

        @block.vector
        def _(dve):
            chain = Chain(dve, s_dve, 56)
            dve.wait_ge(s_w, 16 * len(loads))
            with dve.Fori(0, NCHUNK) as i:
                chain.begin(i)
                dve.wait_ge(s_in, 32 * i + 32)
                for s in range(4):
                    dve.wait_ge(s_tp, 4 * i + s + 1)
                    for half in range(2):
                        o = bank[(2 * s) % 4 + half][0:SUB, :].rearrange("p (u r j c) -> p u r j c", u=2, r=2, j=4)
                        iv = inv[0:SUB, s, 16 * half:16 * half + 16].rearrange("p (u j r) -> p u r j", u=2, r=2)
                        chain.link(nc.vector.reciprocal(iv, o[:, :, :, :, HD]))
                        ov = o_sb[0:SUB, s, 128 * half:128 * half + 128].rearrange("p (u j r d) -> p u r j d", u=2, r=2, j=4)
                        for u in range(2):
                            chain.link(nc.vector.tensor_tensor(ov[:, u], o[:, u, :, :, 0:HD],
                                                               iv[:, u].unsqueeze(3).to_broadcast([SUB, 2, 4, HD]), ALU.mult))
                    dve.sem_inc(s_on, 1)
                dve.wait_ge(s_pe, 2 * i + 1)
                for kt in range(KT):
                    chain.link(nc.vector.tensor_scalar(t_sb[:, kt, :], bank[4 + kt][:, 0:CHUNK], bv_sb[:, kt:kt + 1],
                                                       None, ALU.add))
                dve.sem_inc(s_ot, 1)
                for s in range(4):
                    chain.link(nc.vector.tensor_tensor(x_sb[0:SUB, s, :], x_sb[0:SUB, s, :], bo_sb[0:SUB, :], ALU.add))
                dve.wait_ge(s_pe, 2 * i + 2)
                for s in range(4):
                    src = bank[6 + s // 2][0:SUB, (s % 2) * D:(s % 2 + 1) * D]
                    chain.link(nc.vector.tensor_tensor(hid[0:SUB, s, :], src, x_sb[0:SUB, s, :], ALU.add))
                row_stats(nc, chain.link, hid, L1.eps, stats, aggr, inv_var)
                dve.sem_inc(s_var, 1)
                dve.wait_ge(s_rstd, i + 1)
                normalize(nc, chain.link, yn, hid, aggr, rstd)
                for s in range(4):
                    chain.link(nc.vector.tensor_tensor(yn[0:SUB, s, :], yn[0:SUB, s, :], ga_sb[0:SUB, :], ALU.mult))
                for s in range(4):
                    chain.link(nc.vector.tensor_tensor(yn[0:SUB, s, :], yn[0:SUB, s, :], be_sb[0:SUB, :], ALU.add))
                dve.sem_inc(s_y, 1)
                dve.wait_ge(s_out, 16 * i + 16)
                chain.end()

        @block.tensor
        def _(pe):
            pe.wait_ge(s_w, 16 * len(loads))
            with pe.Fori(0, NCHUNK) as i:
                pe.wait_ge(s_in, 32 * i + 32)
                for s in range(4):
                    if s >= 2:
                        pe.wait_ge(s_on, 4 * i + s - 1)
                    for g in range(G):
                        mm = nc.tensor.transpose(bank[(2 * s) % 4 + g // 4][0:SUB, (g % 4) * 128:(g % 4 + 1) * 128],
                                                 ot_sb[:, g, s * SUB:(s + 1) * SUB], ident[:])
                    mm.then_inc(s_tp, 1)
                pe.wait_ge(s_on, 4 * i + 4)
                transpose_rows(nc, bank[4:6], o_sb, ident).then_inc(s_pe, 1)
                pe.wait_ge(s_ot, i + 1)
                for s in range(4):
                    for kt in range(KT):
                        mm = nc.tensor.matmul(bank[6 + s // 2][0:SUB, (s % 2) * D:(s % 2 + 1) * D],
                                              t_sb[:, kt, s * SUB:(s + 1) * SUB], wo_sb[:, kt, :],
                                              start=(kt == 0), stop=(kt == KT - 1))
                mm.then_inc(s_pe, 1)


def build(nc, a, out):
    def scratch(name, shape, dt=F32):
        return nc.dram_tensor(name, shape, dt, kind="Internal").ap()

    q0, q1 = scratch("q_parts0", [3, D, TOK], BF16), scratch("q_parts1", [3, D, TOK], BF16)
    keys0 = scratch("key_parts0", [4, 128, 3, LK], BF16)
    keys1 = scratch("key_parts1", [2, L1.kvd, 3, LK], BF16)
    o_t0, o_t1 = scratch("o_t0", [128, L0.heads // 4, TOK]), scratch("o_t1", [128, L1.heads // 4, TOK])
    hidden = scratch("hidden", [TOK, D])
    w0, w1 = "L0_xattn_", "L1_xattn_"
    first_queries(nc, a["x"], a[w0 + "ln1_w"], a[w0 + "ln1_b"], a[w0 + "q_w"], a[w0 + "q_b"], a["ident"], q0)
    attention(nc, L0, q0, a["ctx_t"], a["kmask"], None, a[w0 + "k_w"], a[w0 + "k_b"], a[w0 + "v_w"],
              a["k_const0"], a["q_const0"], a["i2"], a["ident"], keys0, o_t0)
    middle(nc, a["x"], o_t0, a[w0 + "v_b"], a[w0 + "cproj_w"], a[w0 + "cproj_b"], a[w0 + "ln2_w"], a[w0 + "ln2_b"], a[w0 + "fc_w"],
           a[w0 + "fc_b"], a[w0 + "proj_w"], a[w0 + "proj_b"], a[w1 + "Wq"], a[w1 + "bq"], a["ident"], hidden, q1)
    attention(nc, L1, q1, a["ctx_t"], None, a["amask"], a[w1 + "Wk"], a[w1 + "bk"], a[w1 + "Wv"],
              a["k_const1"], a["q_const1"], a["i2"], a["ident"], keys1, o_t1)
    last(nc, hidden, o_t1, a["bv_heads1"], a[w1 + "Wo"], a[w1 + "bo"], a[w1 + "gamma"], a[w1 + "beta"], a["ident"], out)


COLUMNS = ["L0_xattn_" + n for n in ("ln1_w", "ln1_b", "q_b", "k_b", "v_b", "ln2_w", "ln2_b", "fc_b")] + [
    "L1_xattn_bq", "L1_xattn_bk"]


def layouts(inputs, bf16):
    a = {n: np.ascontiguousarray(v) for n, v in inputs.items() if n.startswith("L")}
    for n in COLUMNS:
        v = a[n].reshape(-1)
        a[n] = np.ascontiguousarray(v.reshape(-1, min(128, v.size)).T)
    bv = np.ascontiguousarray(inputs["L1_xattn_bv"]).reshape(L1.kv, 1, L1.hd)
    a["bv_heads1"] = np.ascontiguousarray(
        np.broadcast_to(bv, (L1.kv, L1.heads // L1.kv, L1.hd)).reshape(KT, 128).T)
    a["x"] = np.ascontiguousarray(inputs["x"]).reshape(TOK, D)
    a["ctx_t"] = np.ascontiguousarray(np.asarray(inputs["ctx_2048"]).transpose(0, 2, 1))
    a["kmask"] = np.ascontiguousarray(inputs["mask_BxS2_bf1"]).view(np.uint8)
    a["amask"] = np.ascontiguousarray(inputs["mask_Bx1xSxS2_ff0"]).reshape(B, LQ, LK)
    a["ident"] = np.eye(128, dtype=np.float32)
    eye = np.tile(np.eye(LQ), (1, HU))
    k0 = np.zeros((32, LK))
    k0[1:4] = 1
    k1 = np.zeros((24, LK))
    k1[0:3] = 1
    q0 = np.zeros((32, COLS))
    q0[0] = 1
    q1 = np.zeros((80, COLS))
    q1[0:LQ] = eye
    i2 = np.zeros((128, COLS))
    i2[0:LQ] = eye
    i2[64:64 + LQ] = eye
    for name, v in (("k_const0", k0), ("k_const1", k1), ("q_const0", q0), ("q_const1", q1), ("i2", i2)):
        a[name] = v.astype(bf16)
    return a


def kernel(**inputs):
    import concourse.bacc as _bacc
    from concourse.bass_utils import run_bass_kernel_spmd as _run

    nc = _bacc.Bacc("TRN2", target_bir_lowering=False, num_devices=1)
    arrays = layouts(inputs, mybir.dt.np(BF16))
    args = {n: nc.dram_tensor("in_" + n, v.shape, mybir.dt.from_np(v.dtype), kind="ExternalInput").ap()
            for n, v in arrays.items()}
    out = nc.dram_tensor("out_0", (TOK, D), F32, kind="ExternalOutput").ap()
    build(nc, args, out)
    r = _run(nc, [{"in_" + n: v for n, v in arrays.items()}], core_ids=[0])
    return r.results[0]["out_0"].reshape(B, LQ, D)
```

```python
from contextlib import ExitStack

import numpy as np
import concourse.bass as bass
from concourse import mybir

F32 = mybir.dt.float32
BF16 = mybir.dt.bfloat16
U8 = mybir.dt.uint8
ALU = mybir.AluOpType
ACT = mybir.ActivationFunctionType
AX = mybir.AxisListType

B, LQ, D, LK = 32, 56, 256, 1500
TOK = B * LQ
KT = D // 128
KP = 128
NKT = -(-LK // KP)
LKP = NKT * KP
NCH, CH = 3, 500
HU = 8
COLS = HU * LQ
SLOTS = NKT
INNER = 4 * D
BIG = float(2.0 ** 126)
K_PART = (0, 0, 0, 1, 1, 2)
Q_PART = (0, 1, 2, 0, 1, 0)
NMX = 3
STACK_DMAS = 9
SUB = 2 * LQ
CHUNK = 4 * SUB
NCHUNK = TOK // CHUNK


class Layer:
    def __init__(self, n, heads, kv_heads, eps):
        self.n, self.heads, self.kv, self.eps = n, heads, kv_heads, eps
        self.hd = D // heads
        self.ub = heads // HU
        self.upi = 2 * self.ub
        self.nu = B * self.ub
        self.hk = HU * kv_heads // heads
        self.m_row = 97 if n == 0 else 104
        self.kvd = kv_heads * self.hd
        self.second = 64 if n == 0 else LQ
        self.krows = min(128, self.kvd)
        self.scale = float(self.hd) ** -0.5
        if n == 0:
            self.events = {0: "V", 1: "V", 2: "V", 3: "m", 4: "V", 5: "V", 6: "K", 7: "V", 8: "K", 10: "K"}
        else:
            self.events = {3: "m", 5: "T", 8: "K"}
        self.npr = 3 if n == 0 else 4
        self.vt = NKT // self.ub
        self.v_copies = NKT if n == 0 else NCH


L0 = Layer(0, 16, 16, 1e-5)
L1 = Layer(1, 32, 8, 1e-6)


def wait(eng, sem, n, apart=False):
    if not isinstance(n, int):
        eng.wait_ge(sem, n)
        if apart:
            eng.nop(nofuse=True)
    elif n > 0:
        eng.wait_ge(sem, n)


def attention(nc, ly, q_stack, ctx_t, kmask, amask, wk, bk, wv, k_const, q_const, i2_d, ident_d, key_dram, o_t):
    P = f"a{ly.n}_"
    UB, UPI, NU, HD, HK, NPR = ly.ub, ly.upi, ly.nu, ly.hd, ly.hk, ly.npr
    NI = B // 2
    M = ly.m_row
    CR = 6 * HD
    VW = HD + 1
    OG = 2 if ly.n == 0 else 4
    VROW = ly.kv * VW
    first = ly.n == 0

    with ExitStack() as ctx:
        def sb(name, shape, dt):
            return ctx.enter_context(nc.sbuf_tensor(P + name, shape, dt))

        def pb(name, shape, dt=F32):
            return ctx.enter_context(nc.psum_tensor(P + name, shape, dt))

        def sem(name):
            return ctx.enter_context(nc.semaphore(P + name))

        stack_k = [sb(f"stack_k{i}", [128, HK, LKP], BF16) for i in range(4)]
        stack_q = [sb(f"stack_q{i}", [128, HU, LQ], BF16) for i in range(4)]
        ctxt = [sb(f"ctxt{i}", [128, KT, LK], F32) for i in range(2)]
        k32 = [sb(f"k32_{i}", [128, 4 * KP if first else LK], F32) for i in range(2)]
        k_rest = sb("k_rest", [128, 4 * KP if first else LK], F32)
        k_parts = [sb(f"k_parts{i}", [128, 3, LK], BF16) for i in range(2)]
        v_sb = [sb(f"v_sb{i}", [128, NKT, ly.kv, VW], F32) for i in range(2)]
        probs = [sb(f"probs{i}", [128, COLS], F32) for i in range(NPR)]
        ot_sb = [sb(f"ot_sb{i}", [128, OG, LQ], F32) for i in range(2)]
        w_sb = sb("w_sb", [128, KT, 2, ly.kvd], F32)
        bk_sb = sb("bk_sb", [128, 2], F32)
        ident = sb("ident", [128, 128], F32)
        identb = sb("identb", [128, 128], BF16)
        pair_max = [sb(f"pair_max{i}", [128, 4, NCH], F32) for i in range(2)]
        row_max = sb("row_max", [128, 4], F32)
        max_rest = sb("max_rest", [128, 4], F32)
        neg_parts = [sb(f"neg_parts{i}", [128, 4, 3], BF16) for i in range(2)]
        neg_rows = [sb(f"neg_rows{i}", [3, HU, LQ], BF16) for i in range(2)]
        if not first:
            v_t = [sb(f"v_t{i}", [128, LKP], F32) for i in range(2)]
        if first:
            kmask_sb = [sb(f"kmask{i}", [128, LK], U8) for i in range(2)]
            bias_row = [sb(f"bias_row{i}", [1, LK], BF16) for i in range(2)]
        else:
            mask_f = sb("mask_f", [128, LK], F32)
            mask_rest = sb("mask_rest", [128, LK], F32)
            mask_p = [sb(f"mask_p{i}", [128, LK], BF16) for i in range(2)]
            mask_p2 = [sb(f"mask_p2_{i}", [128, LK], BF16) for i in range(2)]
            mask_01 = [sb(f"mask_01_{i}", [128, LK], F32) for i in range(2)]
            stack_m = [sb(f"stack_m{i}", [128, LKP], BF16) for i in range(2)]
            i2 = sb("i2", [128, COLS], BF16)

        mx = [pb(f"mx{i}", [128, 512]) for i in range(NMX)]
        ex = [pb(f"ex{i}", [128, 512]) for i in range(2)]
        pv = [pb(f"pv{i}", [128, 512]) for i in range(2)]
        pj = pb("pj", [128, 512])

        s_const = sem("const_loaded")
        s_init = sem("init_done")
        s_identb = sem("identb_done")
        s_ctx = [sem(f"ctx_loaded{i}") for i in range(2)]
        s_kstore = [sem(f"key_parts_stored{i}") for i in range(2)]
        s_stack = [sem(f"stack_loaded{i}") for i in range(4)]
        s_neg = [sem(f"neg_rows_loaded{i}") for i in range(2)]
        s_ot = [sem(f"o_t_stored{i}") for i in range(2)]
        s_scored = sem("exp_tile_scored")
        s_exp = sem("exp_done")
        s_pv = sem("probs_used")
        s_otc = sem("o_t_copied")
        s_mxs = sem("max_tile_scored")
        s_mxd = sem("max_tile_reduced")
        s_rm = sem("row_max_steps")
        s_np = sem("neg_parts_done")
        s_pjf = sem("proj_bank_filled")
        s_vd = sem("value_tile_done")
        s_kd = sem("key_chunk_done")
        s_kp = sem("key_part_steps")
        s_vt = sem("value_chunk_copied")
        s_ng = sem("neg_rows_done")
        if first:
            s_bias = sem("bias_row_done")
        else:
            s_mf = sem("mask_loaded")
            s_ms = sem("mask_steps")
            s_m01 = sem("mask_01_done")
            s_m2 = sem("mask_p2_done")
            s_stm = sem("stack_m_loaded")

        def is_in(i, v, total=NU, per=UPI):
            return not isinstance(i, int) or 0 <= per * i + v < total

        def q(i, v, k):
            return (UPI // k) * i + v // k

        def keys_in(tile):
            return min(KP, LK - tile * KP)

        def chunk_len(n):
            return min(4 * KP, LK - 4 * KP * n)

        def chunk(n):
            return slice(4 * KP * n, 4 * KP * n + chunk_len(n))

        def pj_events(i, v, slot):
            found = []
            for e in ly.events.get(slot, ""):
                batch = v // UB
                if e == "m" and is_in(i, v + 1):
                    found.append(("m", 0))
                if e == "V" and is_in(i, batch + 1, B, 2):
                    n = [s for s in sorted(ly.events) if "V" in ly.events[s]].index(slot)
                    found.append(("V", (v % UB) * ly.vt + n))
                if e == "T" and v % UB < NCH and is_in(i, batch + 1, B, 2):
                    found.append(("T", v % UB))
                if e == "K" and is_in(i, batch + 2, B, 2):
                    if first:
                        found.append(("K", [s for s in sorted(ly.events) if "K" in ly.events[s]].index(slot)))
                    elif v % UB < NCH:
                        found.append(("K", v % UB))
            return found

        def all_events(i):
            return [(v, *e) for v in range(UPI) for s in range(SLOTS) for e in pj_events(i, v, s)]

        PJ_BEFORE, PJ_PER = len(all_events(-1)), len(all_events(0))

        def pj_base(i):
            return 0 if isinstance(i, int) and i < 0 else PJ_PER * i + PJ_BEFORE

        def iterations(eng, body):
            body(-1)
            body(0)
            with eng.Fori(1, NI - 2) as i:
                body(i)
            body(NI - 2)
            body(NI - 1)

        def stack_count(i, v):
            return 16 * STACK_DMAS * (q(i, v, 4) + 1)

        loads = [(w_sb[:, :, 0, :], wk.rearrange("(k p) n -> p k n", p=128)),
                 (w_sb[:, :, 1, :], wv.rearrange("(k p) n -> p k n", p=128)),
                 (bk_sb[0:ly.krows, 0:ly.kvd // ly.krows], bk[:]),
                 (ident[:], ident_d[:])]
        for s in range(4):
            loads.append((stack_k[s][128 - k_const.shape[0]:, :, 0:LK],
                          k_const.unsqueeze(1).to_broadcast([k_const.shape[0], HK, LK])))
            loads.append((stack_q[s][CR:, :, :], q_const.rearrange("p (h q) -> p h q", h=HU)))
        if not first:
            loads.append((i2[:], i2_d[:]))
        MEMSETS = 11 if first else 18

        KSTEPS = 4 * NCH

        def ready(eng):
            eng.wait_ge(s_const, 16 * len(loads))
            eng.wait_ge(s_init, MEMSETS)

        block = ctx.enter_context(nc.Block())

        @block.sync
        def _(sp):
            for dst, src in loads:
                sp.dma_start(dst, src).then_inc(s_const, 16)
            ready(sp)

            def load_ctx(n, x):
                sp.dma_start(ctxt[x][:], ctx_t[n].rearrange("(k p) s -> p k s", p=128)).then_inc(s_ctx[x], 16)
                if first:
                    sp.dma_start(kmask_sb[x][:], kmask[n].rearrange("(o s) -> o s", o=1).to_broadcast([128, LK])
                                 ).then_inc(s_ctx[x], 16)

            load_ctx(0, 0)

            def body(i):
                for v in range(UPI):
                    b = v // UB
                    if is_in(i, v + 3):
                        w = v + 3
                        s = w % 4
                        wb = w // UB
                        wait(sp, s_scored, SLOTS * (UPI * i + w - 3), apart=True)
                        if first:
                            wait(sp, s_kstore[w % 2], 16 * (q(i, w, 2) + 1), apart=True)
                            wait(sp, s_bias, 2 * i + wb + 1, apart=True)
                            sp.dma_start(stack_k[s][96:97, :, 0:LK],
                                         bias_row[wb % 2][:].unsqueeze(1).to_broadcast([1, HK, LK])
                                         ).then_inc(s_stack[s], 16)
                            src_k = key_dram[w % 4]
                        else:
                            wait(sp, s_kstore[wb % 2], 16 * (i + wb // 2 + 1), apart=True)
                            wait(sp, s_m2, 2 * i + wb + 1, apart=True)
                            sp.dma_start(stack_k[s][CR:CR + LQ, :, 0:LK],
                                         mask_p2[wb % 2][0:LQ, :].unsqueeze(1).to_broadcast([LQ, HK, LK])
                                         ).then_inc(s_stack[s], 16)
                            src_k = key_dram[wb % 2, (w % UB) * HK * HD:(w % UB + 1) * HK * HD]
                        src_k = src_k.rearrange("(d h) p n -> d p h n", d=HD)
                        col = (2 * i + wb) * LQ
                        for r in range(6):
                            sp.dma_start(stack_k[s][r * HD:(r + 1) * HD, :, 0:LK],
                                         src_k[:, K_PART[r]]).then_inc(s_stack[s], 16)
                        sp.dma_start(stack_q[s][0:CR, :, :],
                                     q_stack[w % UB, :, :, bass.ds(col, LQ)]).then_inc(s_stack[s], 16)
                        sp.dma_start(stack_q[s][M:M + 3, :, :],
                                     q_const[q_const.shape[0] - 3:, :].rearrange("p (h q) -> p h q", h=HU)).then_inc(s_stack[s], 16)
                    if is_in(i, v + 1):
                        w = v + 1
                        wait(sp, s_ng, UPI * i + w + 1, apart=True)
                        sp.dma_start(stack_q[w % 4][M:M + 3, :, :], neg_rows[w % 2][:]).then_inc(s_neg[w % 2], 16)
                    if not first and v % UB == 0 and is_in(i, b + 2, B, 2):
                        n = 2 * i + b + 2
                        wait(sp, s_m01, n, apart=True)
                        for h in range(2):
                            sp.dma_start(mask_f[h * LQ:(h + 1) * LQ, :], amask[n]).then_inc(s_mf, 16)
                    if not first and v % UB == 0 and is_in(i, b + 1, B, 2):
                        n = 2 * i + b + 1
                        wait(sp, s_m2, n + 1, apart=True)
                        wait(sp, s_scored, SLOTS * UB * (n - 1), apart=True)
                        for h in range(2):
                            sp.dma_start(stack_m[(b + 1) % 2][h * LQ:(h + 1) * LQ, 0:LK],
                                         mask_p[h][h * LQ:(h + 1) * LQ, :]).then_inc(s_stm, 16)
                    if v % UB == UB - 1 and is_in(i, b + 3, B, 2):
                        n = 2 * i + b + 3
                        if first:
                            wait(sp, s_vd, NKT * (n - 1), apart=True)
                        else:
                            wait(sp, s_kd, NCH * (n - 1), apart=True)
                            wait(sp, s_vt, NCH * (n - 1), apart=True)
                        load_ctx(n, (b + 1) % 2)
                    if first and is_in(i, v + 4):
                        w = v + 4
                        wait(sp, s_kp, KSTEPS * (UPI * i + w + 1), apart=True)
                        wait(sp, s_stack[w % 4], stack_count(i, w - 4), apart=True)
                        sp.dma_start(key_dram[w % 4], k_parts[w % 2][:]).then_inc(s_kstore[w % 2], 16)

            iterations(sp, body)
            for p in range(2):
                sp.wait_ge(s_ot[p], 16 * (NU // 2))

        @block.gpsimd
        def _(pool):
            for x in range(2):
                nc.gpsimd.memset(v_sb[x][:], 1.0).then_inc(s_init, 1)
            for x in range(4):
                nc.gpsimd.memset(stack_k[x][:, :, LK:LKP], 0.0).then_inc(s_init, 1)
            if not first:
                for t in (mask_f, mask_01[0], mask_01[1]):
                    nc.gpsimd.memset(t[:], 0.0).then_inc(s_init, 1)
                for x in range(2):
                    nc.gpsimd.memset(stack_m[x][:], 0.0).then_inc(s_init, 1)
                    nc.gpsimd.memset(v_t[x][:, LK:LKP], 0.0).then_inc(s_init, 1)
            ready(pool)

            def split_keys(i, w, x, n, slot, free):
                rows = ly.krows
                wait(pool, s_kd, NCH * (n + 1), apart=True)
                wait(pool, s_kstore[x], free, apart=True)
                src, rest, parts = k32[x][0:rows, :], k_rest[0:rows, :], k_parts[x][0:rows]
                nc.gpsimd.tensor_copy(parts[:, 0, :], src).then_inc(s_kp, 1)
                wait(pool, s_kp, 4 * n + 1, apart=True)
                nc.gpsimd.tensor_tensor(rest, src, parts[:, 0, :], ALU.subtract).then_inc(s_kp, 1)
                wait(pool, s_kp, 4 * n + 2, apart=True)
                nc.gpsimd.tensor_copy(parts[:, 1, :], rest).then_inc(s_kp, 1)
                wait(pool, s_kp, 4 * n + 3, apart=True)
                nc.gpsimd.tensor_tensor(parts[:, 2, :], rest, parts[:, 1, :], ALU.subtract).then_inc(s_kp, 1)
                wait(pool, s_kp, 4 * n + 4, apart=True)
                wait(pool, *slot, apart=True)
                return parts

            def body(i):
                for v in range(UPI):
                    b = v // UB
                    if not is_in(i, b + 2, B, 2):
                        continue
                    n = 2 * i + b + 2
                    if first:
                        if v % UB == 0:
                            wait(pool, s_ctx[b % 2], 32 * (i + b // 2 + 2), apart=True)
                            wait(pool, s_stack[(v + 1) % 4], stack_count(i, v + 1), apart=True)
                            nc.gpsimd.tensor_scalar(bias_row[b % 2][:], kmask_sb[b % 2][0:1, :], -1.0, BIG,
                                                    ALU.add, ALU.mult).then_inc(s_bias, 1)
                    elif v % UB == 0:
                        wait(pool, s_mf, 32 * (n + 1), apart=True)
                        wait(pool, s_stm, 32 * n, apart=True)
                        wait(pool, s_ms, 4 * n, apart=True)
                        nc.gpsimd.tensor_scalar(mask_f[:], mask_f[:], -BIG, None, ALU.max).then_inc(s_ms, 1)
                        wait(pool, s_ms, 4 * n + 1, apart=True)
                        nc.gpsimd.tensor_copy(mask_p[0][:], mask_f[:]).then_inc(s_ms, 1)
                        wait(pool, s_ms, 4 * n + 2, apart=True)
                        nc.gpsimd.tensor_tensor(mask_rest[:], mask_f[:], mask_p[0][:], ALU.subtract).then_inc(s_ms, 1)
                        wait(pool, s_ms, 4 * n + 3, apart=True)
                        nc.gpsimd.tensor_copy(mask_p[1][:], mask_rest[:]).then_inc(s_ms, 1)
                    elif v % UB == 1:
                        wait(pool, s_ms, 4 * n + 4, apart=True)
                        wait(pool, s_stack[(v + 2) % 4], stack_count(i, v + 2), apart=True)
                        nc.gpsimd.tensor_tensor(mask_p2[b % 2][:], mask_rest[:], mask_p[1][:],
                                                ALU.subtract).then_inc(s_m2, 1)
                    elif v % UB == 2:
                        parts = split_keys(i, v, b % 2, n, (s_stack[(v + 1) % 4], stack_count(i, v + 1)),
                                           16 * (i + b // 2 + 1))
                        pool.dma_start(key_dram[b % 2], parts).then_inc(s_kstore[b % 2], 16)
                    else:
                        wait(pool, s_m2, n + 1, apart=True)
                        wait(pool, s_mxd, SLOTS * UB * (n - 1), apart=True)
                        nc.gpsimd.tensor_tensor(mask_01[b % 2][:], mask_f[:], mask_p2[b % 2][:],
                                                ALU.subtract).then_inc(s_m01, 1)

            iterations(pool, body)

        @block.scalar
        def _(act):
            def drain_o(i, v):
                p = v % 2
                b = v // UB
                wait(act, s_pv, SLOTS * (UPI * i + v + 1))
                wait(act, s_ot[p], 16 * q(i, v, 2))
                nc.scalar.copy(ot_sb[p][:], pv[p][:, 0:OG * LQ].rearrange("p (g q) -> p g q", g=OG)).then_inc(s_otc, 1)
                wait(act, s_otc, UPI * i + v + 1)
                g = OG * (v % UB)
                act.dma_start(o_t[:, g:g + OG, bass.ds((2 * i + b) * LQ, LQ)], ot_sb[p][:]).then_inc(s_ot[p], 16)

            def bank_event(i, v, kind, n, k):
                b = v // UB
                wait(act, s_pjf, pj_base(i) + k + 1)
                if kind == "V":
                    nc.scalar.copy(v_sb[(b + 1) % 2][0:keys_in(n), n, :, 0:HD],
                                   pj[0:keys_in(n), 0:ly.kvd].rearrange("p (h d) -> p h d", d=HD)).then_inc(s_vd, 1)
                elif kind == "T":
                    nc.scalar.copy(v_sb[(b + 1) % 2][0:KP, 4 * n:4 * n + 4, :, 0:HD],
                                   pj[0:KP, 0:4 * ly.kvd].rearrange("p (t h d) -> p t h d", h=ly.kv, d=HD)).then_inc(s_vd, 1)
                else:
                    nc.scalar.copy(v_t[b % 2][64:128, chunk(n)], pj[64:128, 0:chunk_len(n)]).then_inc(s_vt, 1)

            def body(i):
                k = 0
                for v in range(UPI):
                    for slot in range(SLOTS):
                        if is_in(i, v):
                            t = SLOTS * (UPI * i + v) + slot
                            act.wait_ge(s_scored, t + 1)
                            wait(act, s_pv, t + 1 - NPR)
                            n = SLOTS * v + slot
                            nc.scalar.activation(probs[n % NPR][0:KP, :], ex[n % 2][0:KP, 0:COLS],
                                                 ACT.Exp).then_inc(s_exp, 1)
                        if slot == 2 and is_in(i, v) and is_in(i, v - 1):
                            drain_o(i, v - 1)
                        for kind, n in pj_events(i, v, slot):
                            if kind in "VT" or kind == "K" and not first:
                                bank_event(i, v, kind, n, k)
                            k += 1

            iterations(act, body)
            drain_o(NI - 1, UPI - 1)

        @block.vector
        def _(dve):
            for x in range(2):
                nc.vector.memset(pv[x][:], 0.0).then_inc(s_init, 1)
            for x in range(NMX):
                nc.vector.memset(mx[x][:], 0.0).then_inc(s_init, 1)
            ready(dve)
            nc.vector.tensor_copy(identb[:], ident[:]).then_inc(s_identb, 1)

            def bank_event(i, v, kind, n, k):
                b = v // UB
                wait(dve, s_pjf, pj_base(i) + k + 1)
                if kind == "K":
                    if first:
                        w, part = v + 4, k_parts[v % 2][:, :, chunk(n)]
                        key, rest = k32[0][:, 0:chunk_len(n)], k_rest[:, 0:chunk_len(n)]
                        done = KSTEPS * (UPI * i + w) + 4 * n
                        if n == 0:
                            wait(dve, s_kstore[w % 2], 16 * q(i, w, 2))
                        nc.vector.scalar_tensor_tensor(
                            out=key, in0=pj[:, 0:chunk_len(n)], scalar=bk_sb[:, w % UB:w % UB + 1],
                            in1=kmask_sb[b % 2][:, chunk(n)], op0=ALU.add, op1=ALU.mult).then_inc(s_kd, 1)
                        wait(dve, s_kd, NCH * (UPI * i + w) + n + 1)
                        nc.vector.tensor_copy(part[:, 0], key).then_inc(s_kp, 1)
                        wait(dve, s_kp, done + 1)
                        nc.vector.tensor_tensor(rest, key, part[:, 0], ALU.subtract).then_inc(s_kp, 1)
                        wait(dve, s_kp, done + 2)
                        nc.vector.tensor_copy(part[:, 1], rest).then_inc(s_kp, 1)
                        wait(dve, s_kp, done + 3)
                        nc.vector.tensor_tensor(part[:, 2], rest, part[:, 1], ALU.subtract).then_inc(s_kp, 1)
                    else:
                        if n == 0:
                            wait(dve, s_kp, 4 * (2 * i + b + 1))
                        r = ly.krows
                        nc.vector.tensor_scalar(k32[b % 2][0:r, chunk(n)], pj[0:r, 0:chunk_len(n)], bk_sb[0:r, 0:1],
                                                None, ALU.add).then_inc(s_kd, 1)
                else:
                    wait(dve, s_neg[(v + 1) % 2], 16 * q(i, v + 1, 2))
                    nc.vector.tensor_copy(
                        neg_rows[(v + 1) % 2][:].rearrange("p (a h) q -> p a h q", h=2),
                        pj[0:3, :].rearrange("p (a c) -> p a c", a=4)[:, :, 0:2 * ly.second].rearrange(
                            "p a (h q) -> p a h q", h=2)[:, :, :, 0:LQ]).then_inc(s_ng, 1)

            def body(i):
                k = 0
                for v in range(UPI):
                    for slot in range(SLOTS):
                        if is_in(i, v + 2):
                            w = v + 2
                            t = SLOTS * (UPI * i + w) + slot
                            pair, c = slot // NCH, slot % NCH
                            bank = mx[(SLOTS * w + slot) % NMX]
                            dst = pair_max[w % 2][:, pair, c:c + 1]
                            wait(dve, s_mxs, t + 1, apart=not first)
                            if first:
                                nc.vector.tensor_reduce(dst, bank[:, 0:CH], AX.X, ALU.max).then_inc(s_mxd, 1)
                            else:
                                wb = w // UB
                                if slot == 0 and w % UB == 0:
                                    wait(dve, s_m01, 2 * i + wb + 1, apart=True)
                                nc.vector.tensor_tensor_reduce(
                                    out=bank[:, 0:CH], in0=bank[:, 0:CH], in1=mask_01[wb % 2][:, c * CH:(c + 1) * CH],
                                    scale=1.0, scalar=-3.4028235e38, op0=ALU.add, op1=ALU.max,
                                    accum_out=dst).then_inc(s_mxd, 1)
                        for kind, n in pj_events(i, v, slot):
                            if kind in "mK":
                                bank_event(i, v, kind, n, k)
                            k += 1
                    if is_in(i, v + 2):
                        w = v + 2
                        g = 4 * (UPI * i + w)
                        parts = neg_parts[w % 2]
                        wait(dve, s_mxd, SLOTS * (UPI * i + w + 1))
                        nc.vector.tensor_reduce(row_max[:], pair_max[w % 2][:], AX.X, ALU.max).then_inc(s_rm, 1)
                        wait(dve, s_rm, g + 1)
                        wait(dve, s_ng, UPI * i + w - 1)
                        nc.vector.tensor_scalar(parts[:, :, 0], row_max[:], -1.0, None, ALU.mult).then_inc(s_rm, 1)
                        wait(dve, s_rm, g + 2)
                        nc.vector.scalar_tensor_tensor(out=max_rest[:], in0=row_max[:], scalar=-1.0, in1=parts[:, :, 0],
                                                       op0=ALU.mult, op1=ALU.subtract).then_inc(s_rm, 1)
                        wait(dve, s_rm, g + 3)
                        nc.vector.tensor_copy(parts[:, :, 1], max_rest[:]).then_inc(s_rm, 1)
                        wait(dve, s_rm, g + 4)
                        nc.vector.tensor_tensor(parts[:, :, 2], max_rest[:], parts[:, :, 1],
                                                ALU.subtract).then_inc(s_np, 1)

            iterations(dve, body)

        @block.tensor
        def _(pe):
            ready(pe)
            pe.wait_ge(s_identb, 1)

            def exp_scores(i, v, slot):
                s, b = v % 4, v // UB
                k = SLOTS * v + slot
                bank = ex[k % 2]
                keys = slice(slot * KP, (slot + 1) * KP)
                if slot == 0:
                    wait(pe, s_neg[v % 2], 16 * (q(i, v, 2) + 1))
                    if not first and v % UB == 0:
                        wait(pe, s_stm, 32 * (2 * i + b + 1))
                wait(pe, s_exp, SLOTS * (UPI * i + v) + slot - 1)
                if first:
                    for h in range(HU):
                        mm = nc.tensor.matmul(bank[0:KP, h * LQ:(h + 1) * LQ], stack_k[s][:, h, keys],
                                              stack_q[s][:, h, :], start=True, stop=True, skip_group_check=True)
                else:
                    nc.tensor.matmul(bank[0:KP, 0:COLS], stack_m[b % 2][:, keys], i2[:], start=True, stop=False,
                                     skip_group_check=True)
                    for g in range(HK):
                        n = HU // HK
                        mm = nc.tensor.matmul(bank[0:KP, g * n * LQ:(g + 1) * n * LQ], stack_k[s][:, g, keys],
                                              stack_q[s][:, g * n:(g + 1) * n, :], start=False, stop=True,
                                              skip_group_check=True)
                mm.then_inc(s_scored, 1)

            def max_scores(i, w, slot):
                s = w % 4
                pair, c = slot // NCH, slot % NCH
                if slot == 0:
                    wait(pe, s_stack[s], stack_count(i, w))
                wait(pe, s_mxd, SLOTS * (UPI * i + w) + slot + 1 - NMX)
                bank = mx[(SLOTS * w + slot) % NMX]
                keys = slice(c * CH, (c + 1) * CH)
                if first:
                    for h in range(2):
                        head = 2 * pair + h
                        mm = nc.tensor.matmul(bank[64 * h:64 * h + LQ, 0:CH], stack_q[s][:, head, :],
                                              stack_k[s][:, head, keys], start=True, stop=True,
                                              skip_group_check=True)
                else:
                    mm = nc.tensor.matmul(bank[0:2 * LQ, 0:CH], stack_q[s][:, 2 * pair:2 * pair + 2, :],
                                          stack_k[s][:, pair // 2, keys], start=True, stop=True)
                mm.then_inc(s_mxs, 1)

            def use_probs(i, v, slot):
                b = v // UB
                k = SLOTS * v + slot
                p = probs[k % NPR]
                bank = pv[v % 2]
                pe.wait_ge(s_exp, SLOTS * (UPI * i + v) + slot + 1)
                if slot == 0:
                    wait(pe, s_otc, UPI * i + v - 1)
                    if v % UB == 0:
                        wait(pe, s_vd, ly.v_copies * (2 * i + b + 1))
                rows = keys_in(slot)
                if first:
                    for g in range(2):
                        for j in range(4):
                            head = 4 * g + j
                            mm = nc.tensor.matmul(bank[32 * j:32 * j + VW, g * LQ:(g + 1) * LQ],
                                                  v_sb[b % 2][0:rows, slot, (v % UB) * HU + head, :],
                                                  p[0:rows, head * LQ:(head + 1) * LQ],
                                                  start=(slot == 0 and g == 0), stop=(slot == SLOTS - 1),
                                                  skip_group_check=True)
                else:
                    for g in range(2):
                        j = 2 * (slot % 2) + g
                        mm = nc.tensor.matmul(bank[32 * j:32 * j + VW, 0:4 * LQ],
                                              v_sb[b % 2][0:rows, slot, 2 * (v % UB) + g, :],
                                              p[0:rows, g * 4 * LQ:(g + 1) * 4 * LQ],
                                              start=(slot < 2), stop=(slot >= SLOTS - 2), skip_group_check=True)
                mm.then_inc(s_pv, 1)

            def proj_free(i, k):
                if k > 0:
                    v, kind, n = all_events(i)[k - 1]
                elif isinstance(i, int) and i < 0:
                    return
                else:
                    v, kind, n = all_events(i - 1 if isinstance(i, int) else i)[-1]
                    v -= UPI
                b = v // UB
                if kind in "VT":
                    wait(pe, s_vd, ly.v_copies * (2 * i + b + 1) + n + 1)
                elif kind == "K":
                    if not first:
                        wait(pe, s_vt, NCH * (2 * i + b + 2) + n + 1)
                    wait(pe, s_kd, NCH * (UPI * i + v + 4 if first else 2 * i + b + 2) + n + 1)
                else:
                    wait(pe, s_ng, UPI * i + v + 2)

            def bank_event(i, v, kind, n, k):
                b = v // UB
                proj_free(i, k)
                if kind == "V":
                    for kt in range(KT):
                        mm = nc.tensor.matmul(pj[0:keys_in(n), 0:ly.kvd],
                                              ctxt[(b + 1) % 2][:, kt, n * KP:n * KP + keys_in(n)],
                                              w_sb[:, kt, 1, :], start=(kt == 0), stop=(kt == KT - 1))
                    mm.then_inc(s_pjf, 1)
                elif kind == "K":
                    if n == 0 and (not first or v % UB == 0):
                        pe.wait_ge(s_ctx[b % 2], (32 if first else 16) * (i + b // 2 + 2))
                    m = (v % UB) * 128 if first else 0
                    for kt in range(KT):
                        mm = nc.tensor.matmul(pj[:, 0:chunk_len(n)],
                                              w_sb[:, kt].rearrange("p a n -> p (a n)")[:, m:m + 128],
                                              ctxt[b % 2][:, kt, chunk(n)],
                                              start=(kt == 0), stop=(kt == KT - 1))
                    mm.then_inc(s_pjf, 1)
                elif kind == "T":
                    wait(pe, s_vt, NCH * (2 * i + b + 1) + n + 1, apart=True)
                    for t in range(4):
                        at = (4 * n + t) * KP
                        mm = nc.tensor.transpose(pj[0:KP, t * ly.kvd:(t + 1) * ly.kvd],
                                                 v_t[(b + 1) % 2][64:128, at:at + KP], ident[64:128, 64:128])
                    mm.then_inc(s_pjf, 1)
                else:
                    wait(pe, s_np, UPI * i + v + 2)
                    for pair in range(4):
                        mm = nc.tensor.matmul(pj[0:3, pair * 128:(pair + 1) * 128], neg_parts[(v + 1) % 2][:, pair, :],
                                              identb[:], start=True, stop=True, skip_group_check=True)
                    mm.then_inc(s_pjf, 1)

            def body(i):
                k = 0
                for v in range(UPI):
                    for slot in range(SLOTS):
                        if is_in(i, v):
                            exp_scores(i, v, slot)
                        if is_in(i, v + 2):
                            max_scores(i, v + 2, slot)
                        for back in ((1,) if first else (2, 1) if slot % 2 == 0 else ()):
                            if slot > 0 and is_in(i, v):
                                use_probs(i, v, slot - back)
                            if slot == 0 and is_in(i, v - 1):
                                use_probs(i, v - 1, SLOTS - back)
                        for kind, n in pj_events(i, v, slot):
                            bank_event(i, v, kind, n, k)
                            k += 1
            iterations(pe, body)
            for back in ((1,) if first else (2, 1)):
                use_probs(NI - 1, UPI - 1, SLOTS - back)


class Chain:

    def __init__(self, eng, sem, per):
        self.eng, self.sem, self.per, self.n, self.i = eng, sem, per, 0, 0

    def begin(self, i):
        self.i, self.n = i, 0

    def link(self, ins, apart=False):
        ins.then_inc(self.sem, 1)
        self.n += 1
        wait(self.eng, self.sem, self.i * self.per + self.n, apart)

    def end(self):
        assert self.n == self.per, self.n


def row(v, n):
    return v.rearrange("(o n) -> o n", o=1).to_broadcast([128, n])


def row_stats(nc, link, x, eps, stats, aggr, inv_var):
    for s in range(4):
        link(nc.vector.bn_stats(stats[0:SUB, s, :], x[0:SUB, s, :]), apart=True)
        link(nc.vector.bn_aggr(aggr[0:SUB, s, :], stats[0:SUB, s, :]))
    link(nc.vector.tensor_scalar(inv_var[0:SUB, :], aggr[0:SUB, :, 1], eps, None, ALU.add))
    link(nc.vector.reciprocal(inv_var[0:SUB, :], inv_var[0:SUB, :]))


def normalize(nc, link, out, x, aggr, rstd):
    for s in range(4):
        link(nc.vector.tensor_scalar(out[0:SUB, s, :], x[0:SUB, s, :], aggr[0:SUB, s, 0:1], rstd[0:SUB, s:s + 1],
                                     ALU.subtract, ALU.mult))


def transpose_rows(nc, banks, x, ident):
    for kt in range(KT):
        for s in range(4):
            mm = nc.tensor.transpose(banks[kt][:, s * SUB:(s + 1) * SUB], x[0:SUB, s, kt * 128:(kt + 1) * 128],
                                     ident[0:SUB, 0:SUB])
    return mm


def project_queries(nc, banks, w, x_t):
    for m in range(2):
        for kt in range(KT):
            mm = nc.tensor.matmul(banks[m][:, 0:CHUNK], w[:, kt, m * 128:(m + 1) * 128], x_t[:, kt, :],
                                  start=(kt == 0), stop=(kt == KT - 1))
    return mm


def split_queries(nc, link, parts, q32, rest, banks, bias, scale):
    for m in range(2):
        link(nc.vector.tensor_scalar(q32[:, m, :], banks[m][:, 0:CHUNK], bias[:, m:m + 1], scale, ALU.add, ALU.mult))
    link(nc.vector.tensor_copy(parts[:, 0], q32[:]))
    link(nc.vector.tensor_tensor(rest[:], q32[:], parts[:, 0], ALU.subtract))
    link(nc.vector.tensor_copy(parts[:, 1], rest[:]))
    link(nc.vector.tensor_tensor(parts[:, 2], rest[:], parts[:, 1], ALU.subtract))


def store_queries(sp, ly, q_stack, parts, i, s_out):
    rows = HU * ly.hd
    tiles = q_stack.rearrange("(m e) c h t -> e m c h t", e=128 // rows)
    for r in range(6):
        for e in range(128 // rows):
            dst = tiles[e, :, r * ly.hd:(r + 1) * ly.hd, :, bass.ds(i * CHUNK, CHUNK)]
            sp.dma_start(dst.rearrange("m d h t -> (d h) m t"),
                         parts[e * rows:(e + 1) * rows, Q_PART[r], :, :]).then_inc(s_out, 16)


def first_queries(nc, x, ln_w, ln_b, wq, bq, ident_d, q_stack):
    with ExitStack() as ctx:
        def sb(name, shape, dt=F32):
            return ctx.enter_context(nc.sbuf_tensor("q_" + name, shape, dt))

        def sem(name):
            return ctx.enter_context(nc.semaphore("q_" + name))

        x_sb, xn = sb("x", [128, 4, D]), sb("xn", [128, 4, D])
        x_t = sb("x_t", [128, KT, CHUNK])
        stats, aggr = sb("stats", [128, 4, 6]), sb("aggr", [128, 4, 2])
        inv_var, rstd = sb("inv_var", [128, 4]), sb("rstd", [128, 4])
        s_var, s_rstd = sem("variances_done"), sem("rstd_done")
        w, lw, lb, b, ident = (sb("w", [128, KT, D]), sb("lw", [128, 2]), sb("lb", [128, 2]), sb("b", [128, 2]),
                               sb("ident", [128, 128]))
        q32, rest = sb("q32", [128, 2, CHUNK]), sb("rest", [128, 2, CHUNK])
        parts = sb("parts", [128, 3, 2, CHUNK], BF16)
        t_banks = [ctx.enter_context(nc.psum_tensor(f"q_t{i}", [128, 512], F32)) for i in range(2)]
        q_banks = [ctx.enter_context(nc.psum_tensor(f"q_q{i}", [128, 512], F32)) for i in range(2)]
        s_w, s_x, s_out = sem("weights_loaded"), sem("x_loaded"), sem("queries_stored")
        s_xn, s_tp, s_xt, s_qp, s_q, s_dve = (sem("x_normed"), sem("x_transposed"), sem("x_t_done"),
                                              sem("queries_projected"), sem("queries_split"), sem("dve_steps"))
        loads = [(w[:], wq.rearrange("(k p) n -> p k n", p=128)), (lw[:], ln_w[:]), (lb[:], ln_b[:]),
                 (b[:], bq[:]), (ident[:], ident_d[:])]
        block = ctx.enter_context(nc.Block())

        @block.sync
        def _(sp):
            for dst, src in loads:
                sp.dma_start(dst, src).then_inc(s_w, 16)
            with sp.Fori(0, NCHUNK) as i:
                sp.dma_start(x_sb[0:SUB], x[bass.ds(i * CHUNK, CHUNK), :].rearrange("(s p) d -> p s d", p=SUB)).then_inc(s_x, 16)
                wait(sp, s_q, i + 1, apart=True)
                store_queries(sp, L0, q_stack, parts, i, s_out)
            sp.wait_ge(s_out, 96 * NCHUNK)

        @block.scalar
        def _(act):
            with act.Fori(0, NCHUNK) as i:
                act.wait_ge(s_var, i + 1)
                nc.scalar.activation(rstd[0:SUB, :], inv_var[0:SUB, :], ACT.Sqrt).then_inc(s_rstd, 1)

        @block.vector
        def _(dve):
            chain = Chain(dve, s_dve, 22)
            dve.wait_ge(s_w, 16 * len(loads))
            with dve.Fori(0, NCHUNK) as i:
                chain.begin(i)
                dve.wait_ge(s_x, 16 * i + 16)
                row_stats(nc, chain.link, x_sb, L0.eps, stats, aggr, inv_var)
                dve.sem_inc(s_var, 1)
                dve.wait_ge(s_rstd, i + 1)
                normalize(nc, chain.link, xn, x_sb, aggr, rstd)
                dve.sem_inc(s_xn, 1)
                dve.wait_ge(s_tp, i + 1)
                for kt in range(KT):
                    chain.link(nc.vector.tensor_scalar(x_t[:, kt, :], t_banks[kt][:, 0:CHUNK], lw[:, kt:kt + 1],
                                                       lb[:, kt:kt + 1], ALU.mult, ALU.add))
                dve.sem_inc(s_xt, 1)
                dve.wait_ge(s_qp, i + 1)
                split_queries(nc, chain.link, parts, q32, rest, q_banks, b, L0.scale)
                dve.sem_inc(s_q, 1)
                dve.wait_ge(s_out, 96 * i + 96)
                chain.end()

        @block.tensor
        def _(pe):
            pe.wait_ge(s_w, 16 * len(loads))
            with pe.Fori(0, NCHUNK) as i:
                pe.wait_ge(s_xn, i + 1)
                transpose_rows(nc, t_banks, xn, ident).then_inc(s_tp, 1)
                pe.wait_ge(s_xt, i + 1)
                project_queries(nc, q_banks, w, x_t).then_inc(s_qp, 1)


def middle(nc, x, o_t, bv, wc, bc, ln_w, ln_b, wf, bf, wp, bp, wq1, bq1, ident_d, hidden_d, q_stack):
    H, HD = L0.heads, L0.hd
    G = H // 4
    MF = INNER // 128
    with ExitStack() as ctx:
        def sb(name, shape, dt=F32):
            return ctx.enter_context(nc.sbuf_tensor("m_" + name, shape, dt))

        def sem(name):
            return ctx.enter_context(nc.semaphore("m_" + name))

        x_sb = sb("x", [128, 4, D])
        ot_sb = sb("ot", [128, G, CHUNK])
        inv = sb("inv", [128, 4, H])
        bv_sb = sb("bv", [128, KT])
        o_sb = sb("o", [128, 4, D])
        t_sb = sb("t", [128, KT, CHUNK])
        hid, yn, out = sb("hid", [128, 4, D]), sb("yn", [128, 4, D]), sb("out", [128, 4, D])
        act_t = sb("act_t", [128, MF, CHUNK])
        stats, aggr = sb("stats", [128, 4, 6]), sb("aggr", [128, 4, 2])
        inv_var, rstd = sb("inv_var", [128, 4]), sb("rstd", [128, 4])
        s_var, s_rstd = sem("variances_done"), sem("rstd_done")
        wc_sb, wf_sb, wp_sb, wq_sb = (sb("wc", [128, KT, D]), sb("wf", [128, KT, INNER]), sb("wp", [128, MF, D]),
                                      sb("wq", [128, KT, D]))
        bc_sb, bp_sb = sb("bc", [128, D]), sb("bp", [128, D])
        lw, lb, bf_sb, bq_sb, ident = (sb("lw", [128, 2]), sb("lb", [128, 2]), sb("bf", [128, MF]), sb("bq", [128, 2]),
                                       sb("ident", [128, 128]))
        q32, rest = sb("q32", [128, 2, CHUNK]), sb("rest", [128, 2, CHUNK])
        parts = sb("parts", [128, 3, 2, CHUNK], BF16)
        bank = [ctx.enter_context(nc.psum_tensor(f"m_b{i}", [128, 512], F32)) for i in range(8)]
        s_w, s_in, s_out = sem("weights_loaded"), sem("inputs_loaded"), sem("outputs_stored")
        s_pe = sem("pe_stages")
        s_on, s_ot, s_yn, s_yt, s_x1, s_x1t, s_q, s_dve = (
            sem("o_normed"), sem("o_t_done"), sem("hidden_normed"), sem("hidden_t_done"), sem("output_done"),
            sem("output_t_done"), sem("queries_split"), sem("dve_steps"))
        s_fc, s_gelu, s_qp = sem("fc_tile_projected"), sem("gelu_done"), sem("queries_projected")
        loads = [(wc_sb[:], wc.rearrange("(k p) n -> p k n", p=128)), (wf_sb[:], wf.rearrange("(k p) n -> p k n", p=128)),
                 (wp_sb[:], wp.rearrange("(k p) n -> p k n", p=128)), (wq_sb[:], wq1.rearrange("(k p) n -> p k n", p=128)),
                 (bc_sb[:], row(bc, D)), (bp_sb[:], row(bp, D)), (lw[:], ln_w[:]), (lb[:], ln_b[:]),
                 (bf_sb[:], bf[:]), (bv_sb[:], bv[:]), (bq_sb[:], bq1[:]), (ident[:], ident_d[:])]
        block = ctx.enter_context(nc.Block())

        @block.sync
        def _(sp):
            for dst, src in loads:
                sp.dma_start(dst, src).then_inc(s_w, 16)
            with sp.Fori(0, NCHUNK) as i:
                sp.dma_start(ot_sb[:], o_t[:, :, bass.ds(i * CHUNK, CHUNK)]).then_inc(s_in, 16)
                sp.dma_start(x_sb[0:SUB], x[bass.ds(i * CHUNK, CHUNK), :].rearrange("(s p) d -> p s d", p=SUB)).then_inc(s_in, 16)
                wait(sp, s_x1, i + 1, apart=True)
                sp.dma_start(hidden_d[bass.ds(i * CHUNK, CHUNK), :].rearrange("(s p) d -> p s d", p=SUB),
                             out[0:SUB]).then_inc(s_out, 16)
                wait(sp, s_q, i + 1, apart=True)
                store_queries(sp, L1, q_stack, parts, i, s_out)
            sp.wait_ge(s_out, 208 * NCHUNK)

        @block.scalar
        def _(act):
            act.wait_ge(s_w, 16 * len(loads))
            with act.Fori(0, NCHUNK) as i:
                act.wait_ge(s_var, i + 1)
                nc.scalar.activation(rstd[0:SUB, :], inv_var[0:SUB, :], ACT.Sqrt).then_inc(s_rstd, 1)
                for m in range(MF):
                    act.wait_ge(s_fc, i * MF + m + 1)
                    nc.scalar.activation(act_t[:, m, :], bank[m % 4][:, 0:CHUNK], ACT.Gelu_apprx_tanh,
                                         bias=bf_sb[:, m:m + 1]).then_inc(s_gelu, 1)

        @block.vector
        def _(dve):
            chain = Chain(dve, s_dve, 50)
            dve.wait_ge(s_w, 16 * len(loads))
            with dve.Fori(0, NCHUNK) as i:
                chain.begin(i)
                dve.wait_ge(s_in, 32 * i + 32)
                dve.wait_ge(s_pe, 6 * i + 1)
                for s in range(4):
                    o = bank[s][0:SUB, :].rearrange("p (h r) -> p h r", r=32)
                    chain.link(nc.vector.reciprocal(inv[0:SUB, s, :], o[:, :, HD]))
                    chain.link(nc.vector.tensor_tensor(
                        o_sb[0:SUB, s, :].rearrange("p (h d) -> p h d", d=HD), o[:, :, 0:HD],
                        inv[0:SUB, s, :].unsqueeze(2).to_broadcast([SUB, H, HD]), ALU.mult))
                dve.sem_inc(s_on, 1)
                for s in range(4):
                    chain.link(nc.vector.tensor_tensor(x_sb[0:SUB, s, :], x_sb[0:SUB, s, :], bc_sb[0:SUB, :], ALU.add))
                dve.wait_ge(s_pe, 6 * i + 2)
                for kt in range(KT):
                    chain.link(nc.vector.tensor_scalar(t_sb[:, kt, :], bank[4 + kt][:, 0:CHUNK], bv_sb[:, kt:kt + 1],
                                                       None, ALU.add))
                dve.sem_inc(s_ot, 1)
                dve.wait_ge(s_pe, 6 * i + 3)
                for s in range(4):
                    src = bank[6 + s // 2][0:SUB, (s % 2) * D:(s % 2 + 1) * D]
                    chain.link(nc.vector.tensor_tensor(hid[0:SUB, s, :], src, x_sb[0:SUB, s, :], ALU.add))
                row_stats(nc, chain.link, hid, L0.eps, stats, aggr, inv_var)
                dve.sem_inc(s_var, 1)
                dve.wait_ge(s_rstd, i + 1)
                normalize(nc, chain.link, yn, hid, aggr, rstd)
                dve.sem_inc(s_yn, 1)
                dve.wait_ge(s_pe, 6 * i + 4)
                for kt in range(KT):
                    chain.link(nc.vector.tensor_scalar(t_sb[:, kt, :], bank[4 + kt][:, 0:CHUNK], lw[:, kt:kt + 1],
                                                       lb[:, kt:kt + 1], ALU.mult, ALU.add))
                dve.sem_inc(s_yt, 1)
                for s in range(4):
                    chain.link(nc.vector.tensor_tensor(hid[0:SUB, s, :], hid[0:SUB, s, :], bp_sb[0:SUB, :], ALU.add))
                dve.wait_ge(s_pe, 6 * i + 5)
                for s in range(4):
                    src = bank[6 + s // 2][0:SUB, (s % 2) * D:(s % 2 + 1) * D]
                    chain.link(nc.vector.tensor_tensor(out[0:SUB, s, :], src, hid[0:SUB, s, :], ALU.add))
                dve.sem_inc(s_x1, 1)
                dve.wait_ge(s_pe, 6 * i + 6)
                for kt in range(KT):
                    chain.link(nc.vector.tensor_copy(t_sb[:, kt, :], bank[4 + kt][:, 0:CHUNK]))
                dve.sem_inc(s_x1t, 1)
                dve.wait_ge(s_qp, i + 1)
                split_queries(nc, chain.link, parts, q32, rest, bank[0:2], bq_sb, L1.scale)
                dve.sem_inc(s_q, 1)
                dve.wait_ge(s_out, 208 * i + 208)
                chain.end()

        @block.tensor
        def _(pe):
            pe.wait_ge(s_w, 16 * len(loads))
            with pe.Fori(0, NCHUNK) as i:
                pe.wait_ge(s_in, 32 * i + 32)
                for s in range(4):
                    for g in range(G):
                        mm = nc.tensor.transpose(bank[s][0:SUB, g * 128:(g + 1) * 128],
                                                 ot_sb[:, g, s * SUB:(s + 1) * SUB], ident[:])
                mm.then_inc(s_pe, 1)
                pe.wait_ge(s_on, i + 1)
                transpose_rows(nc, bank[4:6], o_sb, ident).then_inc(s_pe, 1)
                pe.wait_ge(s_ot, i + 1)
                for s in range(4):
                    for kt in range(KT):
                        mm = nc.tensor.matmul(bank[6 + s // 2][0:SUB, (s % 2) * D:(s % 2 + 1) * D],
                                              t_sb[:, kt, s * SUB:(s + 1) * SUB], wc_sb[:, kt, :],
                                              start=(kt == 0), stop=(kt == KT - 1))
                mm.then_inc(s_pe, 1)
                pe.wait_ge(s_yn, i + 1)
                transpose_rows(nc, bank[4:6], yn, ident).then_inc(s_pe, 1)
                pe.wait_ge(s_yt, i + 1)
                for m in range(MF):
                    if m >= 4:
                        pe.wait_ge(s_gelu, i * MF + m - 3)
                    for kt in range(KT):
                        mm = nc.tensor.matmul(bank[m % 4][:, 0:CHUNK], wf_sb[:, kt, m * 128:(m + 1) * 128],
                                              t_sb[:, kt, :], start=(kt == 0), stop=(kt == KT - 1))
                    mm.then_inc(s_fc, 1)
                pe.wait_ge(s_gelu, i * MF + MF)
                for s in range(4):
                    for m in range(MF):
                        mm = nc.tensor.matmul(bank[6 + s // 2][0:SUB, (s % 2) * D:(s % 2 + 1) * D],
                                              act_t[:, m, s * SUB:(s + 1) * SUB], wp_sb[:, m, :],
                                              start=(m == 0), stop=(m == MF - 1))
                mm.then_inc(s_pe, 1)
                pe.wait_ge(s_x1, i + 1)
                transpose_rows(nc, bank[4:6], out, ident).then_inc(s_pe, 1)
                pe.wait_ge(s_x1t, i + 1)
                project_queries(nc, bank[0:2], wq_sb, t_sb).then_inc(s_qp, 1)


def last(nc, hidden_d, o_t, bv, wo, bo, gamma, beta, ident_d, fold_d, out_d):
    H, HD = L1.heads, L1.hd
    G = H // 2
    VW = HD + 1
    with ExitStack() as ctx:
        def sb(name, shape, dt=F32):
            return ctx.enter_context(nc.sbuf_tensor("l_" + name, shape, dt))

        def sem(name):
            return ctx.enter_context(nc.semaphore("l_" + name))

        x_sb = sb("x", [128, 4, D])
        ot_sb = sb("ot", [128, G, CHUNK])
        inv = sb("inv", [128, 4, H])
        bv_sb = sb("bv", [128, KT])
        o_sb = sb("o", [128, 4, D])
        t_sb = sb("t", [128, KT, CHUNK])
        hid, yn = sb("hid", [128, 4, D]), sb("yn", [128, 4, D])
        stats, aggr = sb("stats", [128, 4, 6]), sb("aggr", [128, 4, 2])
        inv_var, rstd = sb("inv_var", [128, 4]), sb("rstd", [128, 4])
        s_var, s_rstd = sem("variances_done"), sem("rstd_done")
        wo_sb, bo_sb, ga_sb, be_sb, ident = (sb("wo", [128, KT, D]), sb("bo", [128, D]), sb("ga", [128, D]),
                                             sb("be", [128, D]), sb("ident", [128, 128]))
        bank = [ctx.enter_context(nc.psum_tensor(f"l_b{i}", [128, 512], F32)) for i in range(8)]
        s_w, s_in, s_out = sem("weights_loaded"), sem("inputs_loaded"), sem("outputs_stored")
        s_tp, s_pe, s_on, s_ot, s_y, s_dve = (
            sem("sums_transposed"), sem("pe_stages"), sem("o_normed"), sem("o_t_done"),
            sem("output_done"), sem("dve_steps"))
        fold = sb("fold", [128, 2 * VW])
        loads = [(bv_sb[:], bv[:]), (wo_sb[:], wo.rearrange("(k p) n -> p k n", p=128)), (bo_sb[:], row(bo, D)),
                 (ga_sb[:], row(gamma, D)), (fold[:], fold_d[:]),
                 (be_sb[:], row(beta, D)), (ident[:], ident_d[:])]
        block = ctx.enter_context(nc.Block())

        @block.sync
        def _(sp):
            for dst, src in loads:
                sp.dma_start(dst, src).then_inc(s_w, 16)
            with sp.Fori(0, NCHUNK) as i:
                sp.dma_start(ot_sb[:], o_t[:, :, bass.ds(i * CHUNK, CHUNK)]).then_inc(s_in, 16)
                sp.dma_start(x_sb[0:SUB], hidden_d[bass.ds(i * CHUNK, CHUNK), :].rearrange("(s p) d -> p s d", p=SUB)).then_inc(s_in, 16)
                wait(sp, s_y, i + 1, apart=True)
                sp.dma_start(out_d[bass.ds(i * CHUNK, CHUNK), :].rearrange("(s p) d -> p s d", p=SUB),
                             yn[0:SUB]).then_inc(s_out, 16)
            sp.wait_ge(s_out, 16 * NCHUNK)

        @block.scalar
        def _(act):
            with act.Fori(0, NCHUNK) as i:
                act.wait_ge(s_var, i + 1)
                nc.scalar.activation(rstd[0:SUB, :], inv_var[0:SUB, :], ACT.Sqrt).then_inc(s_rstd, 1)

        @block.vector
        def _(dve):
            chain = Chain(dve, s_dve, 40)
            dve.wait_ge(s_w, 16 * len(loads))
            with dve.Fori(0, NCHUNK) as i:
                chain.begin(i)
                dve.wait_ge(s_in, 32 * i + 32)
                for s in range(4):
                    dve.wait_ge(s_tp, 4 * i + s + 1)
                    o = bank[s][0:SUB, 0:H * VW].rearrange("p (h c) -> p h c", c=VW)
                    chain.link(nc.vector.reciprocal(inv[0:SUB, s, :], o[:, :, HD]))
                    chain.link(nc.vector.tensor_tensor(
                        o_sb[0:SUB, s, :].rearrange("p (h d) -> p h d", d=HD), o[:, :, 0:HD],
                        inv[0:SUB, s, :].unsqueeze(2).to_broadcast([SUB, H, HD]), ALU.mult))
                    dve.sem_inc(s_on, 1)
                dve.wait_ge(s_pe, 2 * i + 1)
                for kt in range(KT):
                    chain.link(nc.vector.tensor_scalar(t_sb[:, kt, :], bank[4 + kt][:, 0:CHUNK], bv_sb[:, kt:kt + 1],
                                                       None, ALU.add))
                dve.sem_inc(s_ot, 1)
                for s in range(4):
                    chain.link(nc.vector.tensor_tensor(x_sb[0:SUB, s, :], x_sb[0:SUB, s, :], bo_sb[0:SUB, :], ALU.add))
                dve.wait_ge(s_pe, 2 * i + 2)
                for s in range(4):
                    src = bank[6 + s // 2][0:SUB, (s % 2) * D:(s % 2 + 1) * D]
                    chain.link(nc.vector.tensor_tensor(hid[0:SUB, s, :], src, x_sb[0:SUB, s, :], ALU.add))
                row_stats(nc, chain.link, hid, L1.eps, stats, aggr, inv_var)
                dve.sem_inc(s_var, 1)
                dve.wait_ge(s_rstd, i + 1)
                normalize(nc, chain.link, yn, hid, aggr, rstd)
                for s in range(4):
                    chain.link(nc.vector.tensor_tensor(yn[0:SUB, s, :], yn[0:SUB, s, :], ga_sb[0:SUB, :], ALU.mult))
                for s in range(4):
                    chain.link(nc.vector.tensor_tensor(yn[0:SUB, s, :], yn[0:SUB, s, :], be_sb[0:SUB, :], ALU.add))
                dve.sem_inc(s_y, 1)
                dve.wait_ge(s_out, 16 * i + 16)
                chain.end()

        @block.tensor
        def _(pe):
            pe.wait_ge(s_w, 16 * len(loads))
            with pe.Fori(0, NCHUNK) as i:
                pe.wait_ge(s_in, 32 * i + 32)
                for s in range(4):
                    for g in range(G):
                        mm = nc.tensor.matmul(bank[s][0:SUB, g * 2 * VW:(g + 1) * 2 * VW],
                                              ot_sb[:, g, s * SUB:(s + 1) * SUB], fold[:], start=True, stop=True,
                                              skip_group_check=True)
                    mm.then_inc(s_tp, 1)
                pe.wait_ge(s_on, 4 * i + 4)
                transpose_rows(nc, bank[4:6], o_sb, ident).then_inc(s_pe, 1)
                pe.wait_ge(s_ot, i + 1)
                for s in range(4):
                    for kt in range(KT):
                        mm = nc.tensor.matmul(bank[6 + s // 2][0:SUB, (s % 2) * D:(s % 2 + 1) * D],
                                              t_sb[:, kt, s * SUB:(s + 1) * SUB], wo_sb[:, kt, :],
                                              start=(kt == 0), stop=(kt == KT - 1))
                mm.then_inc(s_pe, 1)


def build(nc, a, out):
    def scratch(name, shape, dt=F32):
        return nc.dram_tensor(name, shape, dt, kind="Internal").ap()

    q0, q1 = (scratch(f"q_stack{ly.n}", [ly.ub, 6 * ly.hd, HU, TOK], BF16) for ly in (L0, L1))
    keys0 = scratch("key_parts0", [4, 128, 3, LK], BF16)
    keys1 = scratch("key_parts1", [2, L1.kvd, 3, LK], BF16)
    o_t0, o_t1 = scratch("o_t0", [128, L0.heads // 4, TOK]), scratch("o_t1", [128, L1.heads // 2, TOK])
    hidden = scratch("hidden", [TOK, D])
    w0, w1 = "L0_xattn_", "L1_xattn_"
    first_queries(nc, a["x"], a[w0 + "ln1_w"], a[w0 + "ln1_b"], a[w0 + "q_w"], a[w0 + "q_b"], a["ident"], q0)
    attention(nc, L0, q0, a["ctx_t"], a["kmask"], None, a[w0 + "k_w"], a[w0 + "k_b"], a[w0 + "v_w"],
              a["k_const0"], a["q_const0"], a["i2"], a["ident"], keys0, o_t0)
    middle(nc, a["x"], o_t0, a[w0 + "v_b"], a[w0 + "cproj_w"], a[w0 + "cproj_b"], a[w0 + "ln2_w"], a[w0 + "ln2_b"], a[w0 + "fc_w"],
           a[w0 + "fc_b"], a[w0 + "proj_w"], a[w0 + "proj_b"], a[w1 + "Wq"], a[w1 + "bq"], a["ident"], hidden, q1)
    attention(nc, L1, q1, a["ctx_t"], None, a["amask"], a[w1 + "Wk"], a[w1 + "bk"], a[w1 + "Wv"],
              a["k_const1"], a["q_const1"], a["i2"], a["ident"], keys1, o_t1)
    last(nc, hidden, o_t1, a["bv_heads1"], a[w1 + "Wo"], a[w1 + "bo"], a[w1 + "gamma"], a[w1 + "beta"], a["ident"], a["fold"], out)


COLUMNS = ["L0_xattn_" + n for n in ("ln1_w", "ln1_b", "q_b", "k_b", "v_b", "ln2_w", "ln2_b", "fc_b")] + [
    "L1_xattn_bq", "L1_xattn_bk"]


def by_unit(v, units, heads, hd):
    v = v.reshape(v.shape[:-1] + (units, heads, hd))
    return np.ascontiguousarray(np.swapaxes(v, -1, -2).reshape(v.shape[:-3] + (-1,)))


def layouts(inputs, bf16):
    a = {n: np.ascontiguousarray(v) for n, v in inputs.items() if n.startswith("L")}
    for ly, q_names, k_names in ((L0, ("L0_xattn_q_w", "L0_xattn_q_b"), ("L0_xattn_k_w", "L0_xattn_k_b")),
                                 (L1, ("L1_xattn_Wq", "L1_xattn_bq"), ("L1_xattn_Wk", "L1_xattn_bk"))):
        for n in q_names:
            a[n] = by_unit(a[n], ly.ub, HU, ly.hd)
        for n in k_names:
            a[n] = by_unit(a[n], ly.ub, ly.hk, ly.hd)
    for n in COLUMNS:
        v = a[n].reshape(-1)
        a[n] = np.ascontiguousarray(v.reshape(-1, min(128, v.size)).T)
    bv = np.ascontiguousarray(inputs["L1_xattn_bv"]).reshape(L1.kv, 1, L1.hd)
    bv = np.broadcast_to(bv, (L1.kv, L1.heads // L1.kv, L1.hd))
    heads = (L1.ub, 2, L1.heads // L1.kv)
    a["bv_heads1"] = np.ascontiguousarray(bv.reshape(heads + (L1.hd,)).swapaxes(1, 2).reshape(KT, 128).T)
    wo = a["L1_xattn_Wo"]
    a["L1_xattn_Wo"] = np.ascontiguousarray(wo.reshape(heads + (L1.hd, D)).swapaxes(1, 2).reshape(D, D))
    a["x"] = np.ascontiguousarray(inputs["x"]).reshape(TOK, D)
    a["ctx_t"] = np.ascontiguousarray(np.asarray(inputs["ctx_2048"]).transpose(0, 2, 1))
    a["kmask"] = np.ascontiguousarray(inputs["mask_BxS2_bf1"]).view(np.uint8)
    a["amask"] = np.ascontiguousarray(inputs["mask_Bx1xSxS2_ff0"]).reshape(B, LQ, LK)
    a["ident"] = np.eye(128, dtype=np.float32)
    width = L1.hd + 1
    fold = np.zeros((4, 32, 2, width), np.float32)
    for j in range(4):
        fold[j, 0:width, j % 2] = np.eye(width)
    a["fold"] = fold.reshape(128, 2 * width)
    eye = np.tile(np.eye(LQ), (1, HU))
    k0 = np.zeros((32, LK))
    k0[1:4] = 1
    k1 = np.zeros((24, LK))
    k1[0:3] = 1
    q0 = np.zeros((32, COLS))
    q0[0] = 1
    q1 = np.zeros((80, COLS))
    q1[0:LQ] = eye
    i2 = np.zeros((128, COLS))
    i2[0:LQ] = eye
    i2[LQ:2 * LQ] = eye
    for name, v in (("k_const0", k0), ("k_const1", k1), ("q_const0", q0), ("q_const1", q1), ("i2", i2)):
        a[name] = v.astype(bf16)
    return a


def kernel(**inputs):
    import concourse.bacc as _bacc
    from concourse.bass_utils import run_bass_kernel_spmd as _run

    nc = _bacc.Bacc("TRN2", target_bir_lowering=False, num_devices=1)
    arrays = layouts(inputs, mybir.dt.np(BF16))
    args = {n: nc.dram_tensor("in_" + n, v.shape, mybir.dt.from_np(v.dtype), kind="ExternalInput").ap()
            for n, v in arrays.items()}
    out = nc.dram_tensor("out_0", (TOK, D), F32, kind="ExternalOutput").ap()
    build(nc, args, out)
    r = _run(nc, [{"in_" + n: v for n, v in arrays.items()}], core_ids=[0])
    return r.results[0]["out_0"].reshape(B, LQ, D)
```

```python
from contextlib import ExitStack

import numpy as np
import concourse.bass as bass
from concourse import mybir

F32 = mybir.dt.float32
BF16 = mybir.dt.bfloat16
U8 = mybir.dt.uint8
ALU = mybir.AluOpType
ACT = mybir.ActivationFunctionType
AX = mybir.AxisListType

B, LQ, D, LK = 32, 56, 256, 1500
TOK = B * LQ
KT = D // 128
KP = 128
NKT = -(-LK // KP)
LKP = NKT * KP
NCH, CH = 3, 500
HU = 8
COLS = HU * LQ
SLOTS = NKT
INNER = 4 * D
BIG = float(2.0 ** 126)
K_PART = (0, 0, 0, 1, 1, 2)
Q_PART = (0, 1, 2, 0, 1, 0)
NMX = 3
STACK_DMAS = 9
SUB = 2 * LQ
CHUNK = 4 * SUB
NCHUNK = TOK // CHUNK


class Layer:
    def __init__(self, n, heads, kv_heads, eps):
        self.n, self.heads, self.kv, self.eps = n, heads, kv_heads, eps
        self.hd = D // heads
        self.ub = heads // HU
        self.upi = 2 * self.ub
        self.nu = B * self.ub
        self.hk = HU * kv_heads // heads
        self.m_row = 97 if n == 0 else 104
        self.kvd = kv_heads * self.hd
        self.second = 64 if n == 0 else LQ
        self.krows = min(128, self.kvd)
        self.scale = float(self.hd) ** -0.5
        if n == 0:
            self.events = {0: "V", 1: "V", 2: "V", 3: "m", 4: "V", 5: "V", 6: "K", 7: "V", 8: "K", 10: "K"}
        else:
            self.events = {3: "m", 5: "T", 8: "K"}
        self.npr = 3 if n == 0 else 4
        self.npv, self.npj, self.drain = (1, 2, 0) if n == 0 else (2, 1, 2)
        self.vt = NKT // self.ub
        self.v_copies = NKT if n == 0 else NCH


L0 = Layer(0, 16, 16, 1e-5)
L1 = Layer(1, 32, 8, 1e-6)


def wait(eng, sem, n, apart=False):
    if not isinstance(n, int):
        eng.wait_ge(sem, n)
        if apart:
            eng.nop(nofuse=True)
    elif n > 0:
        eng.wait_ge(sem, n)


def attention(nc, ly, q_stack, ctx_t, kmask, amask, wk, bk, wv, k_const, q_const, i2_d, ident_d, key_dram, o_t):
    P = f"a{ly.n}_"
    UB, UPI, NU, HD, HK, NPR = ly.ub, ly.upi, ly.nu, ly.hd, ly.hk, ly.npr
    NI = B // 2
    M = ly.m_row
    NPV, NPJ = ly.npv, ly.npj
    CR = 6 * HD
    VW = HD + 1
    OG = 2 if ly.n == 0 else 4
    VROW = ly.kv * VW
    first = ly.n == 0

    with ExitStack() as ctx:
        def sb(name, shape, dt):
            return ctx.enter_context(nc.sbuf_tensor(P + name, shape, dt))

        def pb(name, shape, dt=F32):
            return ctx.enter_context(nc.psum_tensor(P + name, shape, dt))

        def sem(name):
            return ctx.enter_context(nc.semaphore(P + name))

        stack_k = [sb(f"stack_k{i}", [128, HK, LKP], BF16) for i in range(4)]
        stack_q = [sb(f"stack_q{i}", [128, HU, LQ], BF16) for i in range(4)]
        ctxt = [sb(f"ctxt{i}", [128, KT, LK], F32) for i in range(2)]
        k32 = [sb(f"k32_{i}", [128, 4 * KP if first else LK], F32) for i in range(1 if first else 2)]
        k_rest = sb("k_rest", [128, 4 * KP if first else LK], F32)
        k_parts = [sb(f"k_parts{i}", [128, 3, LK], BF16) for i in range(2)]
        v_sb = [sb(f"v_sb{i}", [128, NKT, ly.kv, VW], F32) for i in range(2)]
        probs = [sb(f"probs{i}", [128, COLS], F32) for i in range(NPR)]
        ot_sb = [sb(f"ot_sb{i}", [128, OG, LQ], F32) for i in range(2)]
        w_sb = sb("w_sb", [128, KT, 2, ly.kvd], F32)
        bk_sb = sb("bk_sb", [128, 2], F32)
        ident = sb("ident", [128, 128], F32)
        identb = sb("identb", [128, 128], BF16)
        pair_max = [sb(f"pair_max{i}", [128, 4, NCH], F32) for i in range(2)]
        row_max = sb("row_max", [128, 4], F32)
        max_rest = sb("max_rest", [128, 4], F32)
        neg_parts = [sb(f"neg_parts{i}", [128, 4, 3], BF16) for i in range(2)]
        neg_rows = [sb(f"neg_rows{i}", [3, HU, LQ], BF16) for i in range(2)]
        if not first:
            v_t = [sb(f"v_t{i}", [128, LKP], F32) for i in range(2)]
        if first:
            kmask_sb = [sb(f"kmask{i}", [128, LK], U8) for i in range(2)]
            bias_row = [sb(f"bias_row{i}", [1, LK], BF16) for i in range(2)]
        else:
            mask_f = sb("mask_f", [128, LK], F32)
            mask_rest = sb("mask_rest", [128, LK], F32)
            mask_p = [sb(f"mask_p{i}", [128, LK], BF16) for i in range(2)]
            mask_p2 = [sb(f"mask_p2_{i}", [128, LK], BF16) for i in range(2)]
            mask_01 = [sb(f"mask_01_{i}", [128, LK], F32) for i in range(2)]
            stack_m = [sb(f"stack_m{i}", [128, LKP], BF16) for i in range(2)]
            i2 = sb("i2", [128, COLS], BF16)

        mx = [pb(f"mx{i}", [128, 512]) for i in range(NMX)]
        ex = [pb(f"ex{i}", [128, 512]) for i in range(2)]
        pv = [pb(f"pv{i}", [128, 512]) for i in range(NPV)]
        pjs = [pb(f"pj{i}", [128, 512]) for i in range(NPJ)]

        s_weights = sem("weights_loaded")
        s_const = sem("const_loaded")
        s_init = sem("init_done")
        s_identb = sem("identb_done")
        s_ctx = [sem(f"ctx_loaded{i}") for i in range(2)]
        s_kstore = [sem(f"key_parts_stored{i}") for i in range(2)]
        s_stack = [sem(f"stack_loaded{i}") for i in range(4)]
        s_neg = [sem(f"neg_rows_loaded{i}") for i in range(2)]
        s_ot = [sem(f"o_t_stored{i}") for i in range(2)]
        s_scored = sem("exp_tile_scored")
        s_exp = sem("exp_done")
        s_pv = sem("probs_used")
        s_otc = sem("o_t_copied")
        s_mxs = sem("max_tile_scored")
        s_mxd = sem("max_tile_reduced")
        s_rm = sem("row_max_steps")
        s_np = sem("neg_parts_done")
        s_pjf = sem("proj_bank_filled")
        s_vd = sem("value_tile_done")
        s_kd = sem("key_chunk_done")
        s_kp = sem("key_part_steps")
        s_vt = sem("value_chunk_copied")
        s_ng = sem("neg_rows_done")
        if first:
            s_bias = sem("bias_row_done")
        else:
            s_mf = sem("mask_loaded")
            s_ms = sem("mask_steps")
            s_m01 = sem("mask_01_done")
            s_m2 = sem("mask_p2_done")
            s_stm = sem("stack_m_loaded")

        def is_in(i, v, total=NU, per=UPI):
            return not isinstance(i, int) or 0 <= per * i + v < total

        def q(i, v, k):
            return (UPI // k) * i + v // k

        def keys_in(tile):
            return min(KP, LK - tile * KP)

        def chunk_len(n):
            return min(4 * KP, LK - 4 * KP * n)

        def chunk(n):
            return slice(4 * KP * n, 4 * KP * n + chunk_len(n))

        def pj_events(i, v, slot):
            found = []
            for e in ly.events.get(slot, ""):
                batch = v // UB
                if e == "m" and is_in(i, v + 1):
                    found.append(("m", 0))
                if e == "V" and is_in(i, batch + 1, B, 2):
                    n = [s for s in sorted(ly.events) if "V" in ly.events[s]].index(slot)
                    found.append(("V", (v % UB) * ly.vt + n))
                if e == "T" and v % UB < NCH and is_in(i, batch + 1, B, 2):
                    found.append(("T", v % UB))
                if e == "K" and is_in(i, batch + 2, B, 2):
                    if first:
                        found.append(("K", [s for s in sorted(ly.events) if "K" in ly.events[s]].index(slot)))
                    elif v % UB < NCH:
                        found.append(("K", v % UB))
            return found

        def all_events(i):
            return [(v, *e) for v in range(UPI) for s in range(SLOTS) for e in pj_events(i, v, s)]

        PJ_BEFORE, PJ_PER = len(all_events(-1)), len(all_events(0))

        def pj_base(i):
            return 0 if isinstance(i, int) and i < 0 else PJ_PER * i + PJ_BEFORE

        def pj_bank(i, k):
            assert PJ_PER % NPJ == 0
            return pjs[(k if isinstance(i, int) and i < 0 else PJ_BEFORE + k) % NPJ]

        def iterations(eng, body):
            body(-1)
            body(0)
            with eng.Fori(1, NI - 2) as i:
                body(i)
            body(NI - 2)
            body(NI - 1)

        def stack_count(i, v):
            return 16 * STACK_DMAS * (q(i, v, 4) + 1)

        weights = [(w_sb[:, :, 0, :], wk.rearrange("(k p) n -> p k n", p=128)),
                   (w_sb[:, :, 1, :], wv.rearrange("(k p) n -> p k n", p=128)),
                   (bk_sb[0:ly.krows, 0:ly.kvd // ly.krows], bk[:]),
                   (ident[:], ident_d[:])]
        loads = []
        for s in range(4):
            loads.append((stack_k[s][128 - k_const.shape[0]:, :, 0:LK],
                          k_const.unsqueeze(1).to_broadcast([k_const.shape[0], HK, LK])))
            loads.append((stack_q[s][CR:, :, :], q_const.rearrange("p (h q) -> p h q", h=HU)))
        if not first:
            loads.append((i2[:], i2_d[:]))
        MEMSETS = 10 if first else 18

        KSTEPS = 4 * NCH

        def ready(eng):
            eng.wait_ge(s_const, 16 * len(loads))
            eng.wait_ge(s_init, MEMSETS)

        block = ctx.enter_context(nc.Block())

        @block.sync
        def _(sp):
            def load_ctx(n, x):
                sp.dma_start(ctxt[x][:], ctx_t[n].rearrange("(k p) s -> p k s", p=128)).then_inc(s_ctx[x], 16)
                if first:
                    sp.dma_start(kmask_sb[x][:], kmask[n].rearrange("(o s) -> o s", o=1).to_broadcast([128, LK])
                                 ).then_inc(s_ctx[x], 16)

            load_ctx(0, 0)
            for dst, src in weights:
                sp.dma_start(dst, src).then_inc(s_weights, 16)
            for dst, src in loads:
                sp.dma_start(dst, src).then_inc(s_const, 16)
            ready(sp)

            def body(i):
                for v in range(UPI):
                    b = v // UB
                    if is_in(i, v + 3):
                        w = v + 3
                        s = w % 4
                        wb = w // UB
                        wait(sp, s_scored, SLOTS * (UPI * i + w - 3), apart=True)
                        if first:
                            wait(sp, s_kstore[w % 2], 16 * (q(i, w, 2) + 1), apart=True)
                            wait(sp, s_bias, 2 * i + wb + 1, apart=True)
                            sp.dma_start(stack_k[s][96:97, :, 0:LK],
                                         bias_row[wb % 2][:].unsqueeze(1).to_broadcast([1, HK, LK])
                                         ).then_inc(s_stack[s], 16)
                            src_k = key_dram[w % 4]
                        else:
                            wait(sp, s_kstore[wb % 2], 16 * (i + wb // 2 + 1), apart=True)
                            wait(sp, s_m2, 2 * i + wb + 1, apart=True)
                            sp.dma_start(stack_k[s][CR:CR + LQ, :, 0:LK],
                                         mask_p2[wb % 2][0:LQ, :].unsqueeze(1).to_broadcast([LQ, HK, LK])
                                         ).then_inc(s_stack[s], 16)
                            src_k = key_dram[wb % 2, (w % UB) * HK * HD:(w % UB + 1) * HK * HD]
                        src_k = src_k.rearrange("(d h) p n -> d p h n", d=HD)
                        col = (2 * i + wb) * LQ
                        for r in range(6):
                            sp.dma_start(stack_k[s][r * HD:(r + 1) * HD, :, 0:LK],
                                         src_k[:, K_PART[r]]).then_inc(s_stack[s], 16)
                        sp.dma_start(stack_q[s][0:CR, :, :],
                                     q_stack[w % UB, :, :, bass.ds(col, LQ)]).then_inc(s_stack[s], 16)
                        sp.dma_start(stack_q[s][M:M + 3, :, :],
                                     q_const[q_const.shape[0] - 3:, :].rearrange("p (h q) -> p h q", h=HU)).then_inc(s_stack[s], 16)
                    if is_in(i, v + 1):
                        w = v + 1
                        wait(sp, s_ng, UPI * i + w + 1, apart=True)
                        sp.dma_start(stack_q[w % 4][M:M + 3, :, :], neg_rows[w % 2][:]).then_inc(s_neg[w % 2], 16)
                    if not first and v % UB == 0 and is_in(i, b + 2, B, 2):
                        n = 2 * i + b + 2
                        wait(sp, s_m01, n, apart=True)
                        for h in range(2):
                            sp.dma_start(mask_f[h * LQ:(h + 1) * LQ, :], amask[n]).then_inc(s_mf, 16)
                    if not first and v % UB == 0 and is_in(i, b + 1, B, 2):
                        n = 2 * i + b + 1
                        wait(sp, s_m2, n + 1, apart=True)
                        wait(sp, s_scored, SLOTS * UB * (n - 1), apart=True)
                        for h in range(2):
                            sp.dma_start(stack_m[(b + 1) % 2][h * LQ:(h + 1) * LQ, 0:LK],
                                         mask_p[h][h * LQ:(h + 1) * LQ, :]).then_inc(s_stm, 16)
                    if v % UB == UB - 1 and is_in(i, b + 3, B, 2):
                        n = 2 * i + b + 3
                        if first:
                            wait(sp, s_vd, NKT * (n - 1), apart=True)
                        else:
                            wait(sp, s_kd, NCH * (n - 1), apart=True)
                            wait(sp, s_vt, NCH * (n - 1), apart=True)
                        load_ctx(n, (b + 1) % 2)
                    if first and is_in(i, v + 4):
                        w = v + 4
                        wait(sp, s_kp, KSTEPS * (UPI * i + w + 1), apart=True)
                        wait(sp, s_stack[w % 4], stack_count(i, w - 4), apart=True)
                        sp.dma_start(key_dram[w % 4], k_parts[w % 2][:]).then_inc(s_kstore[w % 2], 16)

            iterations(sp, body)
            for p in range(2):
                sp.wait_ge(s_ot[p], 16 * (NU // 2))

        @block.gpsimd
        def _(pool):
            for x in range(2):
                nc.gpsimd.memset(v_sb[x][:], 1.0).then_inc(s_init, 1)
            for x in range(4):
                nc.gpsimd.memset(stack_k[x][:, :, LK:LKP], 0.0).then_inc(s_init, 1)
            if not first:
                for t in (mask_f, mask_01[0], mask_01[1]):
                    nc.gpsimd.memset(t[:], 0.0).then_inc(s_init, 1)
                for x in range(2):
                    nc.gpsimd.memset(stack_m[x][:], 0.0).then_inc(s_init, 1)
                    nc.gpsimd.memset(v_t[x][:, LK:LKP], 0.0).then_inc(s_init, 1)
            ready(pool)

            def split_keys(i, w, x, n, slot, free):
                rows = ly.krows
                wait(pool, s_kd, NCH * (n + 1), apart=True)
                wait(pool, s_kstore[x], free, apart=True)
                src, rest, parts = k32[x][0:rows, :], k_rest[0:rows, :], k_parts[x][0:rows]
                nc.gpsimd.tensor_copy(parts[:, 0, :], src).then_inc(s_kp, 1)
                wait(pool, s_kp, 4 * n + 1, apart=True)
                nc.gpsimd.tensor_tensor(rest, src, parts[:, 0, :], ALU.subtract).then_inc(s_kp, 1)
                wait(pool, s_kp, 4 * n + 2, apart=True)
                nc.gpsimd.tensor_copy(parts[:, 1, :], rest).then_inc(s_kp, 1)
                wait(pool, s_kp, 4 * n + 3, apart=True)
                nc.gpsimd.tensor_tensor(parts[:, 2, :], rest, parts[:, 1, :], ALU.subtract).then_inc(s_kp, 1)
                wait(pool, s_kp, 4 * n + 4, apart=True)
                wait(pool, *slot, apart=True)
                return parts

            def body(i):
                for v in range(UPI):
                    b = v // UB
                    if not is_in(i, b + 2, B, 2):
                        continue
                    n = 2 * i + b + 2
                    if first:
                        if v % UB == 0:
                            wait(pool, s_ctx[b % 2], 32 * (i + b // 2 + 2), apart=True)
                            wait(pool, s_stack[(v + 1) % 4], stack_count(i, v + 1), apart=True)
                            nc.gpsimd.tensor_scalar(bias_row[b % 2][:], kmask_sb[b % 2][0:1, :], -1.0, BIG,
                                                    ALU.add, ALU.mult).then_inc(s_bias, 1)
                    elif v % UB == 0:
                        wait(pool, s_mf, 32 * (n + 1), apart=True)
                        wait(pool, s_stm, 32 * n, apart=True)
                        wait(pool, s_ms, 4 * n, apart=True)
                        nc.gpsimd.tensor_scalar(mask_f[:], mask_f[:], -BIG, None, ALU.max).then_inc(s_ms, 1)
                        wait(pool, s_ms, 4 * n + 1, apart=True)
                        nc.gpsimd.tensor_copy(mask_p[0][:], mask_f[:]).then_inc(s_ms, 1)
                        wait(pool, s_ms, 4 * n + 2, apart=True)
                        nc.gpsimd.tensor_tensor(mask_rest[:], mask_f[:], mask_p[0][:], ALU.subtract).then_inc(s_ms, 1)
                        wait(pool, s_ms, 4 * n + 3, apart=True)
                        nc.gpsimd.tensor_copy(mask_p[1][:], mask_rest[:]).then_inc(s_ms, 1)
                    elif v % UB == 1:
                        wait(pool, s_ms, 4 * n + 4, apart=True)
                        wait(pool, s_stack[(v + 2) % 4], stack_count(i, v + 2), apart=True)
                        nc.gpsimd.tensor_tensor(mask_p2[b % 2][:], mask_rest[:], mask_p[1][:],
                                                ALU.subtract).then_inc(s_m2, 1)
                    elif v % UB == 2:
                        parts = split_keys(i, v, b % 2, n, (s_stack[(v + 1) % 4], stack_count(i, v + 1)),
                                           16 * (i + b // 2 + 1))
                        pool.dma_start(key_dram[b % 2], parts).then_inc(s_kstore[b % 2], 16)
                    else:
                        wait(pool, s_m2, n + 1, apart=True)
                        wait(pool, s_mxd, SLOTS * UB * (n - 1), apart=True)
                        nc.gpsimd.tensor_tensor(mask_01[b % 2][:], mask_f[:], mask_p2[b % 2][:],
                                                ALU.subtract).then_inc(s_m01, 1)

            iterations(pool, body)

        @block.scalar
        def _(act):
            def drain_o(i, v):
                p = v % 2
                b = v // UB
                act.wait_ge(s_pv, SLOTS * (UPI * i + v + 1))
                wait(act, s_ot[p], 16 * q(i, v, 2))
                nc.scalar.copy(ot_sb[p][:], pv[v % NPV][:, 0:OG * LQ].rearrange("p (g q) -> p g q", g=OG)).then_inc(s_otc, 1)
                act.wait_ge(s_otc, UPI * i + v + 1)
                g = OG * (v % UB)
                act.dma_start(o_t[:, g:g + OG, bass.ds((2 * i + b) * LQ, LQ)], ot_sb[p][:]).then_inc(s_ot[p], 16)

            def bank_event(i, v, kind, n, k):
                b, pj = v // UB, pj_bank(i, k)
                act.wait_ge(s_pjf, pj_base(i) + k + 1)
                if kind == "V":
                    nc.scalar.copy(v_sb[(b + 1) % 2][0:keys_in(n), n, :, 0:HD],
                                   pj[0:keys_in(n), 0:ly.kvd].rearrange("p (h d) -> p h d", d=HD)).then_inc(s_vd, 1)
                elif kind == "T":
                    nc.scalar.copy(v_sb[(b + 1) % 2][0:KP, 4 * n:4 * n + 4, :, 0:HD],
                                   pj[0:KP, 0:4 * ly.kvd].rearrange("p (t h d) -> p t h d", h=ly.kv, d=HD)).then_inc(s_vd, 1)
                else:
                    nc.scalar.copy(v_t[b % 2][64:128, chunk(n)], pj[64:128, 0:chunk_len(n)]).then_inc(s_vt, 1)

            def body(i):
                k = 0
                for v in range(UPI):
                    for slot in range(SLOTS):
                        if is_in(i, v):
                            t = SLOTS * (UPI * i + v) + slot
                            act.wait_ge(s_scored, t + 1)
                            wait(act, s_pv, t + 1 - NPR)
                            n = SLOTS * v + slot
                            nc.scalar.activation(probs[n % NPR][0:KP, :], ex[n % 2][0:KP, 0:COLS],
                                                 ACT.Exp).then_inc(s_exp, 1)
                        if slot == ly.drain and is_in(i, v) and is_in(i, v - 1):
                            drain_o(i, v - 1)
                        for kind, n in pj_events(i, v, slot):
                            if kind in "VT" or kind == "K" and not first:
                                bank_event(i, v, kind, n, k)
                            k += 1

            iterations(act, body)
            drain_o(NI - 1, UPI - 1)

        @block.vector
        def _(dve):
            for x in range(NPV):
                nc.vector.memset(pv[x][:], 0.0).then_inc(s_init, 1)
            for x in range(NMX):
                nc.vector.memset(mx[x][:], 0.0).then_inc(s_init, 1)
            dve.wait_ge(s_weights, 16 * len(weights))
            dve.wait_ge(s_init, MEMSETS)
            nc.vector.tensor_copy(identb[:], ident[:]).then_inc(s_identb, 1)

            def bank_event(i, v, kind, n, k):
                b, pj = v // UB, pj_bank(i, k)
                dve.wait_ge(s_pjf, pj_base(i) + k + 1)
                if kind == "K":
                    if first:
                        w, part = v + 4, k_parts[v % 2][:, :, chunk(n)]
                        key, rest = k32[0][:, 0:chunk_len(n)], k_rest[:, 0:chunk_len(n)]
                        done = KSTEPS * (UPI * i + w) + 4 * n
                        if n == 0:
                            wait(dve, s_kstore[w % 2], 16 * q(i, w, 2))
                        nc.vector.scalar_tensor_tensor(
                            out=key, in0=pj[:, 0:chunk_len(n)], scalar=bk_sb[:, w % UB:w % UB + 1],
                            in1=kmask_sb[b % 2][:, chunk(n)], op0=ALU.add, op1=ALU.mult).then_inc(s_kd, 1)
                        dve.wait_ge(s_kd, NCH * (UPI * i + w) + n + 1)
                        nc.vector.tensor_copy(part[:, 0], key).then_inc(s_kp, 1)
                        dve.wait_ge(s_kp, done + 1)
                        nc.vector.tensor_tensor(rest, key, part[:, 0], ALU.subtract).then_inc(s_kp, 1)
                        dve.wait_ge(s_kp, done + 2)
                        nc.vector.tensor_copy(part[:, 1], rest).then_inc(s_kp, 1)
                        dve.wait_ge(s_kp, done + 3)
                        nc.vector.tensor_tensor(part[:, 2], rest, part[:, 1], ALU.subtract).then_inc(s_kp, 1)
                    else:
                        if n == 0:
                            wait(dve, s_kp, 4 * (2 * i + b + 1))
                        r = ly.krows
                        nc.vector.tensor_scalar(k32[b % 2][0:r, chunk(n)], pj[0:r, 0:chunk_len(n)], bk_sb[0:r, 0:1],
                                                None, ALU.add).then_inc(s_kd, 1)
                else:
                    wait(dve, s_neg[(v + 1) % 2], 16 * q(i, v + 1, 2))
                    nc.vector.tensor_copy(
                        neg_rows[(v + 1) % 2][:].rearrange("p (a h) q -> p a h q", h=2),
                        pj[0:3, :].rearrange("p (a c) -> p a c", a=4)[:, :, 0:2 * ly.second].rearrange(
                            "p a (h q) -> p a h q", h=2)[:, :, :, 0:LQ]).then_inc(s_ng, 1)

            def body(i):
                k = 0
                for v in range(UPI):
                    for slot in range(SLOTS):
                        if is_in(i, v + 2):
                            w = v + 2
                            t = SLOTS * (UPI * i + w) + slot
                            pair, c = slot // NCH, slot % NCH
                            bank = mx[(SLOTS * w + slot) % NMX]
                            dst = pair_max[w % 2][:, pair, c:c + 1]
                            wait(dve, s_mxs, t + 1, apart=not first)
                            if first:
                                nc.vector.tensor_reduce(dst, bank[:, 0:CH], AX.X, ALU.max).then_inc(s_mxd, 1)
                            else:
                                wb = w // UB
                                if slot == 0 and w % UB == 0:
                                    wait(dve, s_m01, 2 * i + wb + 1, apart=True)
                                nc.vector.tensor_tensor_reduce(
                                    out=bank[:, 0:CH], in0=bank[:, 0:CH], in1=mask_01[wb % 2][:, c * CH:(c + 1) * CH],
                                    scale=1.0, scalar=-3.4028235e38, op0=ALU.add, op1=ALU.max,
                                    accum_out=dst).then_inc(s_mxd, 1)
                        for kind, n in pj_events(i, v, slot):
                            if kind in "mK":
                                bank_event(i, v, kind, n, k)
                            k += 1
                    if is_in(i, v + 2):
                        w = v + 2
                        g = 4 * (UPI * i + w)
                        parts = neg_parts[w % 2]
                        dve.wait_ge(s_mxd, SLOTS * (UPI * i + w + 1))
                        nc.vector.tensor_reduce(row_max[:], pair_max[w % 2][:], AX.X, ALU.max).then_inc(s_rm, 1)
                        dve.wait_ge(s_rm, g + 1)
                        wait(dve, s_ng, UPI * i + w - 1)
                        nc.vector.tensor_scalar(parts[:, :, 0], row_max[:], -1.0, None, ALU.mult).then_inc(s_rm, 1)
                        dve.wait_ge(s_rm, g + 2)
                        nc.vector.scalar_tensor_tensor(out=max_rest[:], in0=row_max[:], scalar=-1.0, in1=parts[:, :, 0],
                                                       op0=ALU.mult, op1=ALU.subtract).then_inc(s_rm, 1)
                        dve.wait_ge(s_rm, g + 3)
                        nc.vector.tensor_copy(parts[:, :, 1], max_rest[:]).then_inc(s_rm, 1)
                        dve.wait_ge(s_rm, g + 4)
                        nc.vector.tensor_tensor(parts[:, :, 2], max_rest[:], parts[:, :, 1],
                                                ALU.subtract).then_inc(s_np, 1)

            iterations(dve, body)

        @block.tensor
        def _(pe):
            pe.wait_ge(s_weights, 16 * len(weights))
            pe.wait_ge(s_init, MEMSETS)
            pe.wait_ge(s_identb, 1)

            def exp_scores(i, v, slot):
                s, b = v % 4, v // UB
                k = SLOTS * v + slot
                bank = ex[k % 2]
                keys = slice(slot * KP, (slot + 1) * KP)
                if slot == 0:
                    pe.wait_ge(s_neg[v % 2], 16 * (q(i, v, 2) + 1))
                    if not first and v % UB == 0:
                        pe.wait_ge(s_stm, 32 * (2 * i + b + 1))
                wait(pe, s_exp, SLOTS * (UPI * i + v) + slot - 1)
                if first:
                    for h in range(HU):
                        mm = nc.tensor.matmul(bank[0:KP, h * LQ:(h + 1) * LQ], stack_k[s][:, h, keys],
                                              stack_q[s][:, h, :], start=True, stop=True, skip_group_check=True)
                else:
                    nc.tensor.matmul(bank[0:KP, 0:COLS], stack_m[b % 2][:, keys], i2[:], start=True, stop=False,
                                     skip_group_check=True)
                    for g in range(HK):
                        n = HU // HK
                        mm = nc.tensor.matmul(bank[0:KP, g * n * LQ:(g + 1) * n * LQ], stack_k[s][:, g, keys],
                                              stack_q[s][:, g * n:(g + 1) * n, :], start=False, stop=True,
                                              skip_group_check=True)
                mm.then_inc(s_scored, 1)

            def max_scores(i, w, slot):
                s = w % 4
                pair, c = slot // NCH, slot % NCH
                if slot == 0:
                    pe.wait_ge(s_stack[s], stack_count(i, w))
                wait(pe, s_mxd, SLOTS * (UPI * i + w) + slot + 1 - NMX)
                bank = mx[(SLOTS * w + slot) % NMX]
                keys = slice(c * CH, (c + 1) * CH)
                if first:
                    for h in range(2):
                        head = 2 * pair + h
                        mm = nc.tensor.matmul(bank[64 * h:64 * h + LQ, 0:CH], stack_q[s][:, head, :],
                                              stack_k[s][:, head, keys], start=True, stop=True,
                                              skip_group_check=True)
                else:
                    mm = nc.tensor.matmul(bank[0:2 * LQ, 0:CH], stack_q[s][:, 2 * pair:2 * pair + 2, :],
                                          stack_k[s][:, pair // 2, keys], start=True, stop=True)
                mm.then_inc(s_mxs, 1)

            def use_probs(i, v, slot):
                b = v // UB
                k = SLOTS * v + slot
                p = probs[k % NPR]
                bank = pv[v % NPV]
                pe.wait_ge(s_exp, SLOTS * (UPI * i + v) + slot + 1)
                if slot == 0:
                    wait(pe, s_otc, UPI * i + v + 1 - NPV)
                    if v % UB == 0:
                        pe.wait_ge(s_vd, ly.v_copies * (2 * i + b + 1))
                rows = keys_in(slot)
                if first:
                    for g in range(2):
                        for j in range(4):
                            head = 4 * g + j
                            mm = nc.tensor.matmul(bank[32 * j:32 * j + VW, g * LQ:(g + 1) * LQ],
                                                  v_sb[b % 2][0:rows, slot, (v % UB) * HU + head, :],
                                                  p[0:rows, head * LQ:(head + 1) * LQ],
                                                  start=(slot == 0 and g == 0), stop=(slot == SLOTS - 1),
                                                  skip_group_check=True)
                else:
                    for g in range(2):
                        j = 2 * (slot % 2) + g
                        mm = nc.tensor.matmul(bank[32 * j:32 * j + VW, 0:4 * LQ],
                                              v_sb[b % 2][0:rows, slot, 2 * (v % UB) + g, :],
                                              p[0:rows, g * 4 * LQ:(g + 1) * 4 * LQ],
                                              start=(slot < 2), stop=(slot >= SLOTS - 2), skip_group_check=True)
                mm.then_inc(s_pv, 1)

            def proj_free(i, k):
                if k >= NPJ:
                    v, kind, n = all_events(i)[k - NPJ]
                elif isinstance(i, int) and i < 0:
                    return
                else:
                    v, kind, n = all_events(i - 1 if isinstance(i, int) else i)[k - NPJ]
                    v -= UPI
                b = v // UB
                if kind in "VT":
                    pe.wait_ge(s_vd, ly.v_copies * (2 * i + b + 1) + n + 1)
                elif kind == "K":
                    if not first:
                        pe.wait_ge(s_vt, NCH * (2 * i + b + 2) + n + 1)
                    pe.wait_ge(s_kd, NCH * (UPI * i + v + 4 if first else 2 * i + b + 2) + n + 1)
                else:
                    pe.wait_ge(s_ng, UPI * i + v + 2)

            def bank_event(i, v, kind, n, k):
                b, pj = v // UB, pj_bank(i, k)
                proj_free(i, k)
                if kind == "V":
                    for kt in range(KT):
                        mm = nc.tensor.matmul(pj[0:keys_in(n), 0:ly.kvd],
                                              ctxt[(b + 1) % 2][:, kt, n * KP:n * KP + keys_in(n)],
                                              w_sb[:, kt, 1, :], start=(kt == 0), stop=(kt == KT - 1))
                    mm.then_inc(s_pjf, 1)
                elif kind == "K":
                    if n == 0 and (not first or v % UB == 0):
                        pe.wait_ge(s_ctx[b % 2], (32 if first else 16) * (i + b // 2 + 2))
                    m = (v % UB) * 128 if first else 0
                    for kt in range(KT):
                        mm = nc.tensor.matmul(pj[:, 0:chunk_len(n)],
                                              w_sb[:, kt].rearrange("p a n -> p (a n)")[:, m:m + 128],
                                              ctxt[b % 2][:, kt, chunk(n)],
                                              start=(kt == 0), stop=(kt == KT - 1))
                    mm.then_inc(s_pjf, 1)
                elif kind == "T":
                    wait(pe, s_vt, NCH * (2 * i + b + 1) + n + 1, apart=True)
                    for t in range(4):
                        at = (4 * n + t) * KP
                        mm = nc.tensor.transpose(pj[0:KP, t * ly.kvd:(t + 1) * ly.kvd],
                                                 v_t[(b + 1) % 2][64:128, at:at + KP], ident[64:128, 64:128])
                    mm.then_inc(s_pjf, 1)
                else:
                    pe.wait_ge(s_np, UPI * i + v + 2)
                    for pair in range(4):
                        mm = nc.tensor.matmul(pj[0:3, pair * 128:(pair + 1) * 128], neg_parts[(v + 1) % 2][:, pair, :],
                                              identb[:], start=True, stop=True, skip_group_check=True)
                    mm.then_inc(s_pjf, 1)

            def body(i):
                k = 0
                for v in range(UPI):
                    for slot in range(SLOTS):
                        if is_in(i, v):
                            exp_scores(i, v, slot)
                        if is_in(i, v + 2):
                            max_scores(i, v + 2, slot)
                        for back in ((1,) if first else (2, 1) if slot % 2 == 0 else ()):
                            if slot > 0 and is_in(i, v):
                                use_probs(i, v, slot - back)
                            if slot == 0 and is_in(i, v - 1):
                                use_probs(i, v - 1, SLOTS - back)
                        for kind, n in pj_events(i, v, slot):
                            bank_event(i, v, kind, n, k)
                            k += 1
            iterations(pe, body)
            for back in ((1,) if first else (2, 1)):
                use_probs(NI - 1, UPI - 1, SLOTS - back)


class Chain:

    def __init__(self, eng, sem, per):
        self.eng, self.sem, self.per, self.n, self.i = eng, sem, per, 0, 0

    def begin(self, i):
        self.i, self.n = i, 0

    def add(self, ins):
        ins.then_inc(self.sem, 1)
        self.n += 1

    def sync(self, apart=False):
        wait(self.eng, self.sem, self.i * self.per + self.n, apart)

    def end(self):
        assert self.n == self.per, self.n


def iterations_of_two(eng, body):
    body(0)
    with eng.Fori(1, NCHUNK // 2) as i:
        body(i)


def row(v, n):
    return v.rearrange("(o n) -> o n", o=1).to_broadcast([128, n])


def on_rows(v):
    return v[0:SUB, :].unsqueeze(1).to_broadcast([SUB, 4, D])


def token_rows(t, c):
    return t[bass.ds(c * CHUNK, CHUNK), :].rearrange("(s p) d -> p s d", p=SUB)


def row_stats(nc, chain, x, eps, stats, aggr, inv_var):
    for s in range(4):
        chain.add(nc.vector.bn_stats(stats[0:SUB, s, :], x[0:SUB, s, :]))
    chain.sync(apart=True)
    for s in range(4):
        chain.add(nc.vector.bn_aggr(aggr[0:SUB, s, :], stats[0:SUB, s, :]))
    chain.sync()
    chain.add(nc.vector.tensor_scalar(inv_var[0:SUB, :], aggr[0:SUB, :, 1], eps, None, ALU.add))
    chain.sync()
    chain.add(nc.vector.reciprocal(inv_var[0:SUB, :], inv_var[0:SUB, :]))
    chain.sync()


def normalize(nc, chain, out, x, aggr, rstd):
    for s in range(4):
        chain.add(nc.vector.tensor_scalar(out[0:SUB, s, :], x[0:SUB, s, :], aggr[0:SUB, s, 0:1], rstd[0:SUB, s:s + 1],
                                          ALU.subtract, ALU.mult))
    chain.sync()


def divide_sums(nc, chain, banks, inv, o, heads, hd):
    sums = [banks[s][0:SUB, 0:heads * (hd + 1)].rearrange("p (h c) -> p h c", c=hd + 1) for s in range(4)]
    for s in range(4):
        chain.add(nc.vector.reciprocal(inv[0:SUB, s, :], sums[s][:, :, hd]))
    chain.sync()
    for s in range(4):
        chain.add(nc.vector.tensor_tensor(
            o[0:SUB, s, :].rearrange("p (h d) -> p h d", d=hd), sums[s][:, :, 0:hd],
            inv[0:SUB, s, :].unsqueeze(2).to_broadcast([SUB, heads, hd]), ALU.mult))
    chain.sync()


def columns_out(nc, chain, dst, banks, scale, bias):
    for kt in range(KT):
        src = banks[kt][:, 0:CHUNK]
        if scale is None:
            chain.add(nc.vector.tensor_scalar(dst[:, kt, :], src, bias[:, kt:kt + 1], None, ALU.add))
        else:
            chain.add(nc.vector.tensor_scalar(dst[:, kt, :], src, scale[:, kt:kt + 1], bias[:, kt:kt + 1],
                                              ALU.mult, ALU.add))
    chain.sync()


def add_rows(nc, chain, dst, banks, x):
    for r in range(2):
        chain.add(nc.vector.tensor_tensor(dst[0:SUB, 2 * r:2 * r + 2, :],
                                          banks[r][0:SUB, :].rearrange("p (s d) -> p s d", d=D),
                                          x[0:SUB, 2 * r:2 * r + 2, :], ALU.add))
    chain.sync()


def gather_sums(nc, banks, sums, gather):
    n = gather.shape[1]
    for s in range(4):
        for g in range(sums.shape[1]):
            mm = nc.tensor.matmul(banks[s][0:SUB, g * n:(g + 1) * n], sums[:, g, s * SUB:(s + 1) * SUB], gather[:],
                                  start=True, stop=True, skip_group_check=True)
    return mm


def transpose_rows(nc, banks, x, ident):
    for kt in range(KT):
        for s in range(4):
            mm = nc.tensor.transpose(banks[kt][:, s * SUB:(s + 1) * SUB], x[0:SUB, s, kt * 128:(kt + 1) * 128],
                                     ident[0:SUB, 0:SUB])
    return mm


def project_rows(nc, banks, x_t, w, tiles):
    for s in range(4):
        for k in range(tiles):
            mm = nc.tensor.matmul(banks[s // 2][0:SUB, (s % 2) * D:(s % 2 + 1) * D], x_t[:, k, s * SUB:(s + 1) * SUB],
                                  w[:, k, :], start=(k == 0), stop=(k == tiles - 1))
    return mm


def project_queries(nc, banks, w, x_t):
    for m in range(2):
        for kt in range(KT):
            mm = nc.tensor.matmul(banks[m][:, 0:CHUNK], w[:, kt, m * 128:(m + 1) * 128], x_t[:, kt, :],
                                  start=(kt == 0), stop=(kt == KT - 1))
    return mm


def split_queries(nc, chain, parts, q32, rest, banks, bias, scale):
    for m in range(2):
        chain.add(nc.vector.tensor_scalar(q32[:, m, :], banks[m][:, 0:CHUNK], bias[:, m:m + 1], scale,
                                          ALU.add, ALU.mult))
    chain.sync()
    chain.add(nc.vector.tensor_copy(parts[:, 0], q32[:]))
    chain.sync()
    chain.add(nc.vector.tensor_tensor(rest[:], q32[:], parts[:, 0], ALU.subtract))
    chain.sync()
    chain.add(nc.vector.tensor_copy(parts[:, 1], rest[:]))
    chain.sync()
    chain.add(nc.vector.tensor_tensor(parts[:, 2], rest[:], parts[:, 1], ALU.subtract))
    chain.sync()


def query_stores(ly):
    return 6 * (128 // (HU * ly.hd))


def store_queries(sp, ly, q_stack, parts, c, s_out):
    rows = HU * ly.hd
    tiles = q_stack.rearrange("(m e) c h t -> e m c h t", e=128 // rows)
    for r in range(6):
        for e in range(128 // rows):
            dst = tiles[e, :, r * ly.hd:(r + 1) * ly.hd, :, bass.ds(c * CHUNK, CHUNK)]
            sp.dma_start(dst.rearrange("m d h t -> (d h) m t"),
                         parts[e * rows:(e + 1) * rows, Q_PART[r], :, :]).then_inc(s_out, 16)



def first_queries(nc, x_d, ln_w, ln_b, wq, bq, ident_d, q_stack):
    with ExitStack() as ctx:
        def sb(name, shape, dt=F32):
            return ctx.enter_context(nc.sbuf_tensor("q_" + name, shape, dt))

        def two(name, shape, dt=F32):
            return [sb(f"{name}{x}", shape, dt) for x in range(2)]

        def sem(name):
            return ctx.enter_context(nc.semaphore("q_" + name))

        x_sb, xn = two("x", [128, 4, D]), two("xn", [128, 4, D])
        x_t = two("x_t", [128, KT, CHUNK])
        stats, aggr = two("stats", [128, 4, 6]), two("aggr", [128, 4, 2])
        inv_var, rstd = two("inv_var", [128, 4]), two("rstd", [128, 4])
        q32, rest = two("q32", [128, 2, CHUNK]), two("rest", [128, 2, CHUNK])
        parts = two("parts", [128, 3, 2, CHUNK], BF16)
        w, lw, lb, b, ident = (sb("w", [128, KT, D]), sb("lw", [128, 2]), sb("lb", [128, 2]), sb("b", [128, 2]),
                               sb("ident", [128, 128]))
        banks = [[ctx.enter_context(nc.psum_tensor(f"q_b{x}_{k}", [128, 512], F32)) for k in range(4)] for x in range(2)]
        s_w = sem("weights_loaded")
        s_x, s_out = [sem(f"x_loaded{x}") for x in range(2)], [sem(f"queries_stored{x}") for x in range(2)]
        s_var, s_rstd, s_xn, s_tp, s_xt, s_qp, s_q, s_dve = (
            sem("variances_done"), sem("rstd_done"), sem("x_normed"), sem("x_transposed"), sem("x_t_done"),
            sem("queries_projected"), sem("queries_split"), sem("dve_steps"))
        loads = [(w[:], wq.rearrange("(k p) n -> p k n", p=128)), (lw[:], ln_w[:]), (lb[:], ln_b[:]),
                 (b[:], bq[:]), (ident[:], ident_d[:])]
        STORED = 16 * query_stores(L0)
        block = ctx.enter_context(nc.Block())

        @block.sync
        def _(sp):
            for x in range(2):
                sp.dma_start(x_sb[x][0:SUB], token_rows(x_d, x)).then_inc(s_x[x], 16)
            for dst, src in loads:
                sp.dma_start(dst, src).then_inc(s_w, 16)

            def store(i):
                for x in range(2):
                    sp.wait_ge(s_q, 2 * i + x + 1)
                    sp.nop(nofuse=True)
                    store_queries(sp, L0, q_stack, parts[x], 2 * i + x, s_out[x])

            with sp.Fori(0, NCHUNK // 2 - 1) as i:
                for x in range(2):
                    sp.wait_ge(s_xn, 2 * i + x + 1)
                    sp.nop(nofuse=True)
                    sp.dma_start(x_sb[x][0:SUB], token_rows(x_d, 2 * i + x + 2)).then_inc(s_x[x], 16)
                store(i)
            store(NCHUNK // 2 - 1)
            for x in range(2):
                sp.wait_ge(s_out[x], STORED * NCHUNK // 2)

        @block.scalar
        def _(act):
            with act.Fori(0, NCHUNK // 2) as i:
                for x in range(2):
                    act.wait_ge(s_var, 2 * i + x + 1)
                    nc.scalar.activation(rstd[x][0:SUB, :], inv_var[x][0:SUB, :], ACT.Sqrt).then_inc(s_rstd, 1)

        @block.vector
        def _(dve):
            chain = Chain(dve, s_dve, 2 * 22)
            dve.wait_ge(s_w, 16 * len(loads))

            def body(i):
                chain.begin(i)
                for x in range(2):
                    dve.wait_ge(s_x[x], 16 * i + 16)
                    row_stats(nc, chain, x_sb[x], L0.eps, stats[x], aggr[x], inv_var[x])
                    dve.sem_inc(s_var, 1)
                for x in range(2):
                    dve.wait_ge(s_rstd, 2 * i + x + 1)
                    normalize(nc, chain, xn[x], x_sb[x], aggr[x], rstd[x])
                    dve.sem_inc(s_xn, 1)
                for x in range(2):
                    dve.wait_ge(s_tp, 2 * i + x + 1)
                    columns_out(nc, chain, x_t[x], banks[x][0:2], lw, lb)
                    dve.sem_inc(s_xt, 1)
                for x in range(2):
                    wait(dve, s_out[x], STORED * i, apart=True)
                    dve.wait_ge(s_qp, 2 * i + x + 1)
                    split_queries(nc, chain, parts[x], q32[x], rest[x], banks[x][2:4], b, L0.scale)
                    dve.sem_inc(s_q, 1)
                chain.end()

            iterations_of_two(dve, body)

        @block.tensor
        def _(pe):
            pe.wait_ge(s_w, 16 * len(loads))

            def body(i):
                for x in range(2):
                    pe.wait_ge(s_xn, 2 * i + x + 1)
                    transpose_rows(nc, banks[x][0:2], xn[x], ident).then_inc(s_tp, 1)
                for x in range(2):
                    wait(pe, s_q, 2 * i + x - 1, apart=True)
                    pe.wait_ge(s_xt, 2 * i + x + 1)
                    project_queries(nc, banks[x][2:4], w, x_t[x]).then_inc(s_qp, 1)

            iterations_of_two(pe, body)


def middle(nc, x_d, o_t, bv, wc, bc, ln_w, ln_b, wf, bf, wp, bp, wq1, bq1, ident_d, gather_d, hidden_d, q_stack):
    H, HD = L0.heads, L0.hd
    G = H // 4
    MF = INNER // 128
    with ExitStack() as ctx:
        def sb(name, shape, dt=F32):
            return ctx.enter_context(nc.sbuf_tensor("m_" + name, shape, dt))

        def two(name, shape, dt=F32):
            return [sb(f"{name}{x}", shape, dt) for x in range(2)]

        def sem(name):
            return ctx.enter_context(nc.semaphore("m_" + name))

        x_sb, ot_sb = two("x", [128, 4, D]), two("ot", [128, G, CHUNK])
        inv, o_sb = two("inv", [128, 4, H]), two("o", [128, 4, D])
        t_sb = two("t", [128, KT, CHUNK])
        hid, yn, out = two("hid", [128, 4, D]), two("yn", [128, 4, D]), two("out", [128, 4, D])
        act_t = two("act_t", [128, MF, CHUNK])
        stats, aggr = two("stats", [128, 4, 6]), two("aggr", [128, 4, 2])
        inv_var, rstd = two("inv_var", [128, 4]), two("rstd", [128, 4])
        q32, rest = two("q32", [128, 2, CHUNK]), sb("rest", [128, 2, CHUNK])
        parts = two("parts", [128, 3, 2, CHUNK], BF16)
        wc_sb, wf_sb, wp_sb, wq_sb = (sb("wc", [128, KT, D]), sb("wf", [128, KT, INNER]), sb("wp", [128, MF, D]),
                                      sb("wq", [128, KT, D]))
        bc_sb, bp_sb = sb("bc", [128, D]), sb("bp", [128, D])
        bv_sb, lw, lb, bf_sb, bq_sb = (sb("bv", [128, KT]), sb("lw", [128, 2]), sb("lb", [128, 2]),
                                       sb("bf", [128, MF]), sb("bq", [128, 2]))
        ident, gather = sb("ident", [128, 128]), sb("gather", [128, 4 * (HD + 1)])
        banks = [[ctx.enter_context(nc.psum_tensor(f"m_b{x}_{k}", [128, 512], F32)) for k in range(4)] for x in range(2)]
        s_w = sem("weights_loaded")
        s_in, s_out = [sem(f"inputs_loaded{x}") for x in range(2)], [sem(f"outputs_stored{x}") for x in range(2)]
        s_dve = sem("dve_steps")
        s_tp, s_np, s_cp, s_yp, s_mp, s_xp, s_qp = (
            sem("sums_transposed"), sem("o_transposed"), sem("output_projected"), sem("hidden_transposed"),
            sem("mlp_projected"), sem("output_transposed"), sem("queries_projected"))
        s_fc, s_gelu, s_var, s_rstd = (sem("fc_tile_projected"), sem("gelu_done"), sem("variances_done"),
                                       sem("rstd_done"))
        s_on, s_ot, s_hid, s_yn, s_yt, s_x1, s_x1t, s_q = (
            sem("o_normed"), sem("o_t_done"), sem("hidden_done"), sem("hidden_normed"), sem("hidden_t_done"),
            sem("output_done"), sem("output_t_done"), sem("queries_split"))
        loads = [(ident[:], ident_d[:]), (gather[:], gather_d[:]), (bc_sb[:], row(bc, D)), (bv_sb[:], bv[:]),
                 (wc_sb[:], wc.rearrange("(k p) n -> p k n", p=128)), (lw[:], ln_w[:]), (lb[:], ln_b[:]),
                 (bp_sb[:], row(bp, D)), (wf_sb[:], wf.rearrange("(k p) n -> p k n", p=128)), (bf_sb[:], bf[:]),
                 (wp_sb[:], wp.rearrange("(k p) n -> p k n", p=128)), (bq_sb[:], bq1[:]),
                 (wq_sb[:], wq1.rearrange("(k p) n -> p k n", p=128))]
        STORED = 16 * (1 + query_stores(L1))
        block = ctx.enter_context(nc.Block())

        @block.sync
        def _(sp):
            def load_sums(x, c):
                sp.dma_start(ot_sb[x][:], o_t[:, :, bass.ds(c * CHUNK, CHUNK)]).then_inc(s_in[x], 16)

            def load_x(x, c):
                sp.dma_start(x_sb[x][0:SUB], token_rows(x_d, c)).then_inc(s_in[x], 16)

            def store(i):
                for x in range(2):
                    sp.wait_ge(s_x1, 2 * i + x + 1)
                    sp.nop(nofuse=True)
                    sp.dma_start(token_rows(hidden_d, 2 * i + x), out[x][0:SUB]).then_inc(s_out[x], 16)
                for x in range(2):
                    sp.wait_ge(s_q, 2 * i + x + 1)
                    sp.nop(nofuse=True)
                    store_queries(sp, L1, q_stack, parts[x], 2 * i + x, s_out[x])

            for x in range(2):
                load_sums(x, x)
                load_x(x, x)
            for dst, src in loads:
                sp.dma_start(dst, src).then_inc(s_w, 16)
            with sp.Fori(0, NCHUNK // 2 - 1) as i:
                for x in range(2):
                    sp.wait_ge(s_tp, 2 * i + x + 1)
                    sp.nop(nofuse=True)
                    load_sums(x, 2 * i + x + 2)
                for x in range(2):
                    sp.wait_ge(s_hid, 2 * i + x + 1)
                    sp.nop(nofuse=True)
                    load_x(x, 2 * i + x + 2)
                store(i)
            store(NCHUNK // 2 - 1)
            for x in range(2):
                sp.wait_ge(s_out[x], STORED * NCHUNK // 2)

        @block.scalar
        def _(act):
            act.wait_ge(s_w, 16 * len(loads))
            with act.Fori(0, NCHUNK // 2) as i:
                for x in range(2):
                    act.wait_ge(s_var, 2 * i + x + 1)
                    nc.scalar.activation(rstd[x][0:SUB, :], inv_var[x][0:SUB, :], ACT.Sqrt).then_inc(s_rstd, 1)
                for x in range(2):
                    for m in range(MF):
                        act.wait_ge(s_fc, (2 * i + x) * MF + m + 1)
                        nc.scalar.activation(act_t[x][:, m, :], banks[x][m % 4][:, 0:CHUNK], ACT.Gelu_apprx_tanh,
                                             bias=bf_sb[:, m:m + 1]).then_inc(s_gelu, 1)

        @block.vector
        def _(dve):
            chain = Chain(dve, s_dve, 2 * 40)
            dve.wait_ge(s_w, 16 * len(loads))

            def body(i):
                chain.begin(i)
                for x in range(2):
                    dve.wait_ge(s_tp, 2 * i + x + 1)
                    divide_sums(nc, chain, banks[x], inv[x], o_sb[x], H, HD)
                    dve.sem_inc(s_on, 1)
                    dve.wait_ge(s_in[x], 32 * i + 32)
                    chain.add(nc.vector.tensor_tensor(x_sb[x][0:SUB], x_sb[x][0:SUB], on_rows(bc_sb), ALU.add))
                for x in range(2):
                    dve.wait_ge(s_np, 2 * i + x + 1)
                    columns_out(nc, chain, t_sb[x], banks[x][0:2], None, bv_sb)
                    dve.sem_inc(s_ot, 1)
                for x in range(2):
                    dve.wait_ge(s_cp, 2 * i + x + 1)
                    add_rows(nc, chain, hid[x], banks[x][2:4], x_sb[x])
                    dve.sem_inc(s_hid, 1)
                    row_stats(nc, chain, hid[x], L0.eps, stats[x], aggr[x], inv_var[x])
                    dve.sem_inc(s_var, 1)
                for x in range(2):
                    dve.wait_ge(s_rstd, 2 * i + x + 1)
                    normalize(nc, chain, yn[x], hid[x], aggr[x], rstd[x])
                    dve.sem_inc(s_yn, 1)
                    chain.add(nc.vector.tensor_tensor(hid[x][0:SUB], hid[x][0:SUB], on_rows(bp_sb), ALU.add))
                for x in range(2):
                    dve.wait_ge(s_yp, 2 * i + x + 1)
                    columns_out(nc, chain, t_sb[x], banks[x][0:2], lw, lb)
                    dve.sem_inc(s_yt, 1)
                for x in range(2):
                    wait(dve, s_out[x], STORED * i, apart=True)
                    dve.wait_ge(s_mp, 2 * i + x + 1)
                    add_rows(nc, chain, out[x], banks[x][2:4], hid[x])
                    dve.sem_inc(s_x1, 1)
                for x in range(2):
                    dve.wait_ge(s_xp, 2 * i + x + 1)
                    for kt in range(KT):
                        chain.add(nc.vector.tensor_copy(t_sb[x][:, kt, :], banks[x][kt][:, 0:CHUNK]))
                    chain.sync()
                    dve.sem_inc(s_x1t, 1)
                for x in range(2):
                    dve.wait_ge(s_qp, 2 * i + x + 1)
                    split_queries(nc, chain, parts[x], q32[x], rest, banks[x][2:4], bq_sb, L1.scale)
                    dve.sem_inc(s_q, 1)
                chain.end()

            iterations_of_two(dve, body)

        @block.tensor
        def _(pe):
            pe.wait_ge(s_w, 16 * len(loads))

            def body(i):
                for x in range(2):
                    wait(pe, s_q, 2 * i + x - 1, apart=True)
                    pe.wait_ge(s_in[x], 32 * i + 32)
                    gather_sums(nc, banks[x], ot_sb[x], gather).then_inc(s_tp, 1)
                for x in range(2):
                    pe.wait_ge(s_on, 2 * i + x + 1)
                    transpose_rows(nc, banks[x][0:2], o_sb[x], ident).then_inc(s_np, 1)
                for x in range(2):
                    pe.wait_ge(s_ot, 2 * i + x + 1)
                    project_rows(nc, banks[x][2:4], t_sb[x], wc_sb, KT).then_inc(s_cp, 1)
                for x in range(2):
                    pe.wait_ge(s_yn, 2 * i + x + 1)
                    transpose_rows(nc, banks[x][0:2], yn[x], ident).then_inc(s_yp, 1)
                for x in range(2):
                    pe.wait_ge(s_yt, 2 * i + x + 1)
                    for m in range(MF):
                        if m >= 4:
                            pe.wait_ge(s_gelu, (2 * i + x) * MF + m - 3)
                        for kt in range(KT):
                            mm = nc.tensor.matmul(banks[x][m % 4][:, 0:CHUNK], wf_sb[:, kt, m * 128:(m + 1) * 128],
                                                  t_sb[x][:, kt, :], start=(kt == 0), stop=(kt == KT - 1))
                        mm.then_inc(s_fc, 1)
                for x in range(2):
                    pe.wait_ge(s_gelu, (2 * i + x) * MF + MF)
                    project_rows(nc, banks[x][2:4], act_t[x], wp_sb, MF).then_inc(s_mp, 1)
                for x in range(2):
                    pe.wait_ge(s_x1, 2 * i + x + 1)
                    transpose_rows(nc, banks[x][0:2], out[x], ident).then_inc(s_xp, 1)
                for x in range(2):
                    pe.wait_ge(s_x1t, 2 * i + x + 1)
                    project_queries(nc, banks[x][2:4], wq_sb, t_sb[x]).then_inc(s_qp, 1)

            iterations_of_two(pe, body)


def last(nc, hidden_d, o_t, bv, wo, bo, gamma, beta, ident_d, gather_d, out_d):
    H, HD = L1.heads, L1.hd
    G = H // 2
    with ExitStack() as ctx:
        def sb(name, shape, dt=F32):
            return ctx.enter_context(nc.sbuf_tensor("l_" + name, shape, dt))

        def two(name, shape, dt=F32):
            return [sb(f"{name}{x}", shape, dt) for x in range(2)]

        def sem(name):
            return ctx.enter_context(nc.semaphore("l_" + name))

        x_sb, ot_sb = two("x", [128, 4, D]), two("ot", [128, G, CHUNK])
        inv, o_sb = two("inv", [128, 4, H]), two("o", [128, 4, D])
        t_sb = two("t", [128, KT, CHUNK])
        hid, yn = two("hid", [128, 4, D]), two("yn", [128, 4, D])
        stats, aggr = two("stats", [128, 4, 6]), two("aggr", [128, 4, 2])
        inv_var, rstd = two("inv_var", [128, 4]), two("rstd", [128, 4])
        wo_sb, bv_sb = sb("wo", [128, KT, D]), sb("bv", [128, KT])
        bo_sb, ga_sb, be_sb = sb("bo", [128, D]), sb("ga", [128, D]), sb("be", [128, D])
        ident, gather = sb("ident", [128, 128]), sb("gather", [128, 2 * (HD + 1)])
        banks = [[ctx.enter_context(nc.psum_tensor(f"l_b{x}_{k}", [128, 512], F32)) for k in range(4)] for x in range(2)]
        s_w = sem("weights_loaded")
        s_in, s_out = [sem(f"inputs_loaded{x}") for x in range(2)], [sem(f"outputs_stored{x}") for x in range(2)]
        s_tp, s_np, s_op, s_on, s_ot, s_hid, s_y, s_var, s_rstd, s_dve = (
            sem("sums_transposed"), sem("o_transposed"), sem("output_projected"), sem("o_normed"), sem("o_t_done"),
            sem("hidden_done"), sem("output_done"), sem("variances_done"), sem("rstd_done"), sem("dve_steps"))
        loads = [(ident[:], ident_d[:]), (gather[:], gather_d[:]), (bo_sb[:], row(bo, D)), (bv_sb[:], bv[:]),
                 (wo_sb[:], wo.rearrange("(k p) n -> p k n", p=128)), (ga_sb[:], row(gamma, D)), (be_sb[:], row(beta, D))]
        block = ctx.enter_context(nc.Block())

        @block.sync
        def _(sp):
            def load_sums(x, c):
                sp.dma_start(ot_sb[x][:], o_t[:, :, bass.ds(c * CHUNK, CHUNK)]).then_inc(s_in[x], 16)

            def load_x(x, c):
                sp.dma_start(x_sb[x][0:SUB], token_rows(hidden_d, c)).then_inc(s_in[x], 16)

            def store(i):
                for x in range(2):
                    sp.wait_ge(s_y, 2 * i + x + 1)
                    sp.nop(nofuse=True)
                    sp.dma_start(token_rows(out_d, 2 * i + x), yn[x][0:SUB]).then_inc(s_out[x], 16)

            for dst, src in loads:
                sp.dma_start(dst, src).then_inc(s_w, 16)
            for x in range(2):
                load_sums(x, x)
                load_x(x, x)
            with sp.Fori(0, NCHUNK // 2 - 1) as i:
                for x in range(2):
                    sp.wait_ge(s_tp, 2 * i + x + 1)
                    sp.nop(nofuse=True)
                    load_sums(x, 2 * i + x + 2)
                for x in range(2):
                    sp.wait_ge(s_hid, 2 * i + x + 1)
                    sp.nop(nofuse=True)
                    load_x(x, 2 * i + x + 2)
                store(i)
            store(NCHUNK // 2 - 1)
            for x in range(2):
                sp.wait_ge(s_out[x], 16 * NCHUNK // 2)

        @block.scalar
        def _(act):
            with act.Fori(0, NCHUNK // 2) as i:
                for x in range(2):
                    act.wait_ge(s_var, 2 * i + x + 1)
                    nc.scalar.activation(rstd[x][0:SUB, :], inv_var[x][0:SUB, :], ACT.Sqrt).then_inc(s_rstd, 1)

        @block.vector
        def _(dve):
            chain = Chain(dve, s_dve, 2 * 29)
            dve.wait_ge(s_w, 16 * len(loads))

            def body(i):
                chain.begin(i)
                for x in range(2):
                    dve.wait_ge(s_tp, 2 * i + x + 1)
                    divide_sums(nc, chain, banks[x], inv[x], o_sb[x], H, HD)
                    dve.sem_inc(s_on, 1)
                    dve.wait_ge(s_in[x], 32 * i + 32)
                    chain.add(nc.vector.tensor_tensor(x_sb[x][0:SUB], x_sb[x][0:SUB], on_rows(bo_sb), ALU.add))
                for x in range(2):
                    dve.wait_ge(s_np, 2 * i + x + 1)
                    columns_out(nc, chain, t_sb[x], banks[x][0:2], None, bv_sb)
                    dve.sem_inc(s_ot, 1)
                for x in range(2):
                    dve.wait_ge(s_op, 2 * i + x + 1)
                    add_rows(nc, chain, hid[x], banks[x][2:4], x_sb[x])
                    dve.sem_inc(s_hid, 1)
                    row_stats(nc, chain, hid[x], L1.eps, stats[x], aggr[x], inv_var[x])
                    dve.sem_inc(s_var, 1)
                for x in range(2):
                    wait(dve, s_out[x], 16 * i, apart=True)
                    dve.wait_ge(s_rstd, 2 * i + x + 1)
                    normalize(nc, chain, yn[x], hid[x], aggr[x], rstd[x])
                    chain.add(nc.vector.tensor_tensor(yn[x][0:SUB], yn[x][0:SUB], on_rows(ga_sb), ALU.mult))
                    chain.sync()
                    chain.add(nc.vector.tensor_tensor(yn[x][0:SUB], yn[x][0:SUB], on_rows(be_sb), ALU.add))
                    chain.sync()
                    dve.sem_inc(s_y, 1)
                chain.end()

            iterations_of_two(dve, body)

        @block.tensor
        def _(pe):
            pe.wait_ge(s_w, 16 * len(loads))

            def body(i):
                for x in range(2):
                    wait(pe, s_hid, 2 * i + x - 1, apart=True)
                    pe.wait_ge(s_in[x], 32 * i + 32)
                    gather_sums(nc, banks[x], ot_sb[x], gather).then_inc(s_tp, 1)
                for x in range(2):
                    pe.wait_ge(s_on, 2 * i + x + 1)
                    transpose_rows(nc, banks[x][0:2], o_sb[x], ident).then_inc(s_np, 1)
                for x in range(2):
                    pe.wait_ge(s_ot, 2 * i + x + 1)
                    project_rows(nc, banks[x][2:4], t_sb[x], wo_sb, KT).then_inc(s_op, 1)

            iterations_of_two(pe, body)


def build(nc, a, out):
    def scratch(name, shape, dt=F32):
        return nc.dram_tensor(name, shape, dt, kind="Internal").ap()

    q0, q1 = (scratch(f"q_stack{ly.n}", [ly.ub, 6 * ly.hd, HU, TOK], BF16) for ly in (L0, L1))
    keys0 = scratch("key_parts0", [4, 128, 3, LK], BF16)
    keys1 = scratch("key_parts1", [2, L1.kvd, 3, LK], BF16)
    o_t0, o_t1 = scratch("o_t0", [128, L0.heads // 4, TOK]), scratch("o_t1", [128, L1.heads // 2, TOK])
    hidden = scratch("hidden", [TOK, D])
    w0, w1 = "L0_xattn_", "L1_xattn_"
    first_queries(nc, a["x"], a[w0 + "ln1_w"], a[w0 + "ln1_b"], a[w0 + "q_w"], a[w0 + "q_b"], a["ident"], q0)
    attention(nc, L0, q0, a["ctx_t"], a["kmask"], None, a[w0 + "k_w"], a[w0 + "k_b"], a[w0 + "v_w"],
              a["k_const0"], a["q_const0"], a["i2"], a["ident"], keys0, o_t0)
    middle(nc, a["x"], o_t0, a[w0 + "v_b"], a[w0 + "cproj_w"], a[w0 + "cproj_b"], a[w0 + "ln2_w"], a[w0 + "ln2_b"], a[w0 + "fc_w"],
           a[w0 + "fc_b"], a[w0 + "proj_w"], a[w0 + "proj_b"], a[w1 + "Wq"], a[w1 + "bq"], a["ident"],
           a["gather0"], hidden, q1)
    attention(nc, L1, q1, a["ctx_t"], None, a["amask"], a[w1 + "Wk"], a[w1 + "bk"], a[w1 + "Wv"],
              a["k_const1"], a["q_const1"], a["i2"], a["ident"], keys1, o_t1)
    last(nc, hidden, o_t1, a["bv_heads1"], a[w1 + "Wo"], a[w1 + "bo"], a[w1 + "gamma"], a[w1 + "beta"], a["ident"], a["gather1"], out)


COLUMNS = ["L0_xattn_" + n for n in ("ln1_w", "ln1_b", "q_b", "k_b", "v_b", "ln2_w", "ln2_b", "fc_b")] + [
    "L1_xattn_bq", "L1_xattn_bk"]


def by_unit(v, units, heads, hd):
    v = v.reshape(v.shape[:-1] + (units, heads, hd))
    return np.ascontiguousarray(np.swapaxes(v, -1, -2).reshape(v.shape[:-3] + (-1,)))


def layouts(inputs, bf16):
    a = {n: np.ascontiguousarray(v) for n, v in inputs.items() if n.startswith("L")}
    for ly, q_names, k_names in ((L0, ("L0_xattn_q_w", "L0_xattn_q_b"), ("L0_xattn_k_w", "L0_xattn_k_b")),
                                 (L1, ("L1_xattn_Wq", "L1_xattn_bq"), ("L1_xattn_Wk", "L1_xattn_bk"))):
        for n in q_names:
            a[n] = by_unit(a[n], ly.ub, HU, ly.hd)
        for n in k_names:
            a[n] = by_unit(a[n], ly.ub, ly.hk, ly.hd)
    for n in COLUMNS:
        v = a[n].reshape(-1)
        a[n] = np.ascontiguousarray(v.reshape(-1, min(128, v.size)).T)
    bv = np.ascontiguousarray(inputs["L1_xattn_bv"]).reshape(L1.kv, 1, L1.hd)
    bv = np.broadcast_to(bv, (L1.kv, L1.heads // L1.kv, L1.hd))
    heads = (L1.ub, 2, L1.heads // L1.kv)
    a["bv_heads1"] = np.ascontiguousarray(bv.reshape(heads + (L1.hd,)).swapaxes(1, 2).reshape(KT, 128).T)
    wo = a["L1_xattn_Wo"]
    a["L1_xattn_Wo"] = np.ascontiguousarray(wo.reshape(heads + (L1.hd, D)).swapaxes(1, 2).reshape(D, D))
    a["x"] = np.ascontiguousarray(inputs["x"]).reshape(TOK, D)
    a["ctx_t"] = np.ascontiguousarray(np.asarray(inputs["ctx_2048"]).transpose(0, 2, 1))
    a["kmask"] = np.ascontiguousarray(inputs["mask_BxS2_bf1"]).view(np.uint8)
    a["amask"] = np.ascontiguousarray(inputs["mask_Bx1xSxS2_ff0"]).reshape(B, LQ, LK)
    a["ident"] = np.eye(128, dtype=np.float32)
    for ly, n in ((L0, 4), (L1, 2)):
        gather = np.zeros((4, 32, n, ly.hd + 1), np.float32)
        for j in range(4):
            gather[j, 0:ly.hd + 1, j % n] = np.eye(ly.hd + 1)
        a[f"gather{ly.n}"] = gather.reshape(128, -1)
    eye = np.tile(np.eye(LQ), (1, HU))
    k0 = np.zeros((32, LK))
    k0[1:4] = 1
    k1 = np.zeros((24, LK))
    k1[0:3] = 1
    q0 = np.zeros((32, COLS))
    q0[0] = 1
    q1 = np.zeros((80, COLS))
    q1[0:LQ] = eye
    i2 = np.zeros((128, COLS))
    i2[0:LQ] = eye
    i2[LQ:2 * LQ] = eye
    for name, v in (("k_const0", k0), ("k_const1", k1), ("q_const0", q0), ("q_const1", q1), ("i2", i2)):
        a[name] = v.astype(bf16)
    return a


def kernel(**inputs):
    import concourse.bacc as _bacc
    from concourse.bass_utils import run_bass_kernel_spmd as _run

    nc = _bacc.Bacc("TRN2", target_bir_lowering=False, num_devices=1)
    arrays = layouts(inputs, mybir.dt.np(BF16))
    args = {n: nc.dram_tensor("in_" + n, v.shape, mybir.dt.from_np(v.dtype), kind="ExternalInput").ap()
            for n, v in arrays.items()}
    out = nc.dram_tensor("out_0", (TOK, D), F32, kind="ExternalOutput").ap()
    build(nc, args, out)
    r = _run(nc, [{"in_" + n: v for n, v in arrays.items()}], core_ids=[0])
    return r.results[0]["out_0"].reshape(B, LQ, D)
```
